# Optimizing a Trainium2 kernel written in Bass

```python
import numpy as np
import jax
import jax.numpy as jnp

def _softmax(x, axis=-1):
    return jax.nn.softmax(x, axis=axis)

def _gelu(x):
    return jax.nn.gelu(x, approximate=True)

def _silu(x):
    return jax.nn.silu(x)

def _sigmoid(x):
    return jax.nn.sigmoid(x)

def _layernorm(x, axis=-1, eps=1e-05):
    m = jnp.mean(x, axis=axis, keepdims=True)
    v = jnp.var(x, axis=axis, keepdims=True)
    return (x - m) / jnp.sqrt(v + eps)

def _scatter_add(tgt, idx, src, axis=0):
    return tgt.at[idx].add(src)

def _segment_sum(src, seg, n):
    return jax.ops.segment_sum(src, seg, n)
kernel_name = 'mk_seq_postln_d4_jaxref_r8_dac9fa'

def setup_inputs(seed: int=0):
    np.random.seed(seed)
    _w = jnp.asarray

    def _L0_attn_setup():
        import jax, jax.numpy as jnp
        import numpy as np
        EPS = 1e-06
        key = jax.random.key(seed)
        kx, kw = jax.random.split(key)
        B, L, D = (4, 1024, 128)
        x = jax.random.normal(kx, (B, L, D), dtype=jnp.float32)
        W = jax.random.normal(kw, (D, 3 * D), dtype=jnp.float32) * 0.02
        return {'x': x, 'W': W}
    _L0_attn_in = _L0_attn_setup()

    def _L0_ffn_setup():
        import jax, jax.numpy as jnp
        import numpy as np
        D_MODEL = 128
        D_FF = 512
        NUM_EXPERTS = 8
        key = jax.random.key(seed)
        ks = jax.random.split(key, 8)
        scale_in = 1.0 / np.sqrt(D_MODEL)
        scale_ff = 1.0 / np.sqrt(D_FF)
        x = jax.random.normal(ks[0], (4, 256, D_MODEL), dtype=jnp.float32)
        gate_w = jax.random.uniform(ks[1], (NUM_EXPERTS, D_MODEL), jnp.float32, -scale_in, scale_in)
        gate_b = jax.random.uniform(ks[2], (NUM_EXPERTS,), jnp.float32, -scale_in, scale_in)
        expert_bias = jnp.zeros((NUM_EXPERTS,), dtype=jnp.float32)
        w1 = jax.random.uniform(ks[3], (NUM_EXPERTS, D_MODEL, D_FF), jnp.float32, -scale_in, scale_in)
        b1 = jax.random.uniform(ks[4], (NUM_EXPERTS, D_FF), jnp.float32, -scale_in, scale_in)
        w2 = jax.random.uniform(ks[5], (NUM_EXPERTS, D_FF, D_MODEL), jnp.float32, -scale_ff, scale_ff)
        b2 = jax.random.uniform(ks[6], (NUM_EXPERTS, D_MODEL), jnp.float32, -scale_ff, scale_ff)
        return {'x': x, 'gate_w': gate_w, 'gate_b': gate_b, 'expert_bias': expert_bias, 'w1': w1, 'b1': b1, 'w2': w2, 'b2': b2}
    _L0_ffn_in = _L0_ffn_setup()

    def _L1_attn_setup():
        import jax, jax.numpy as jnp
        import numpy as np
        NUM_HEAD = 16
        D_Q = 64
        D_KV = 64
        ROPE_BASE = 10000.0

        def _cos_sin(seq_len, dim):
            pos = jnp.arange(seq_len, dtype=jnp.float32)[:, None]
            ids = jnp.arange(dim // 2, dtype=jnp.float32)
            theta = ROPE_BASE ** (-2.0 * ids) / (dim // 2)
            r = pos * theta[None, :]
            return (jnp.cos(r), jnp.sin(r))

        def _rope(x, cos, sin):
            b, s, d = x.shape
            xv = x.reshape(b, s, d // 2, 2)
            x0, x1 = (xv[..., 0], xv[..., 1])
            out = jnp.stack([x0 * cos - x1 * sin, x1 * cos + x0 * sin], axis=-1)
            return out.reshape(b, s, d)
        key = jax.random.key(seed)
        ks = jax.random.split(key, 10)
        d_model, d_q, d_kv = (128, D_Q, D_KV)
        b, s = (2, 256)
        w = lambda k, i, o: jax.random.normal(k, (i, o), dtype=jnp.float32) * 0.02
        return {'x': jax.random.normal(ks[0], (b, s, d_model), dtype=jnp.float32), 'Wd_q_w': w(ks[1], d_model, d_q), 'Wd_q_b': jnp.zeros((d_q,), jnp.float32), 'Wu_q_w': w(ks[2], d_q, d_model), 'Wu_q_b': jnp.zeros((d_model,), jnp.float32), 'Wq_r_w': w(ks[3], d_q, d_model), 'Wq_r_b': jnp.zeros((d_model,), jnp.float32), 'Wk_r_w': w(ks[4], d_model, d_model), 'Wk_r_b': jnp.zeros((d_model,), jnp.float32), 'Wd_kv_w': w(ks[5], d_model, d_kv), 'Wd_kv_b': jnp.zeros((d_kv,), jnp.float32), 'Wu_k_w': w(ks[6], d_kv, d_model), 'Wu_k_b': jnp.zeros((d_model,), jnp.float32), 'Wu_v_w': w(ks[7], d_kv, d_model), 'Wu_v_b': jnp.zeros((d_model,), jnp.float32), 'Wo_w': w(ks[8], d_model, d_model), 'Wo_b': jnp.zeros((d_model,), jnp.float32)}
    _L1_attn_in = _L1_attn_setup()

    def _L1_ffn_setup():
        import jax, jax.numpy as jnp
        import numpy as np
        DIM = 128
        DEPTH = 2
        HEADS = 8
        DIM_HEAD = 64
        WINDOW = 64
        INNER = HEADS * DIM_HEAD
        HID = int(DIM * 4 * 2 / 3)
        B, N = (2, 1024)
        QK_SCALE = 8.0

        def shift_token(t):
            t1, t2 = jnp.split(t, 2, axis=-1)
            t2 = jnp.pad(t2, ((0, 0), (1, 0), (0, 0)))[:, :-1]
            return jnp.concatenate([t1, t2], axis=-1)

        def l2norm(t):
            return t / jnp.clip(jnp.linalg.norm(t, axis=-1, keepdims=True), 1e-12)

        def rotate_half(x):
            x1, x2 = jnp.split(x, 2, axis=-1)
            return jnp.concatenate([-x2, x1], axis=-1)

        def rotary_xpos(q, k):
            n = q.shape[-2]
            half_idx = jnp.arange(0, DIM_HEAD, 2, dtype=jnp.float32)
            inv_freq = 1.0 / 10000.0 ** (half_idx / DIM_HEAD)
            t = jnp.arange(n, dtype=jnp.float32)
            freqs = t[:, None] * inv_freq[None, :]
            freqs = jnp.concatenate([freqs, freqs], axis=-1)
            base = (half_idx + 0.4 * DIM_HEAD) / (1.4 * DIM_HEAD)
            power = (t - n // 2) / float(WINDOW // 2)
            scale = base[None, :] ** power[:, None]
            scale = jnp.concatenate([scale, scale], axis=-1)
            cos, sin = (jnp.cos(freqs), jnp.sin(freqs))
            q = q * cos * scale + rotate_half(q) * sin * scale
            k = k * cos / scale + rotate_half(k) * sin / scale
            return (q, k)

        def local_attention(q, k, v):
            b, h, n, d = q.shape
            w = n // WINDOW
            bq = q.reshape(b, h, w, WINDOW, d) * QK_SCALE
            bk = k.reshape(b, h, w, WINDOW, d)
            bv = v.reshape(b, h, w, WINDOW, d)

            def look_around(t):
                p = jnp.pad(t, ((0, 0), (0, 0), (1, 0), (0, 0), (0, 0)))
                return jnp.concatenate([p[:, :, :w], p[:, :, 1:]], axis=3)
            bk, bv = (look_around(bk), look_around(bv))
            bt = jnp.arange(n).reshape(w, WINDOW)
            btp = jnp.pad(bt, ((1, 0), (0, 0)), constant_values=-1)
            btk = jnp.concatenate([btp[:w], btp[1:]], axis=1)
            sim = jnp.einsum('bhwid,bhwjd->bhwij', bq, bk)
            i = bt[:, :, None]
            j = btk[:, None, :]
            mask = (i < j) | (i > j + WINDOW) | (j == -1)
            sim = jnp.where(mask, -jnp.finfo(sim.dtype).max, sim)
            attn = jax.nn.softmax(sim, axis=-1)
            out = jnp.einsum('bhwij,bhwjd->bhwid', attn, bv)
            return out.reshape(b, h, n, d)

        def _layer(x, wqkv, qs, ksc, wo, lg, lb, w1, b1, w2, b2):
            b, n, _ = x.shape
            h = shift_token(x)
            qkv = h @ wqkv
            q, k, v = jnp.split(qkv, 3, axis=-1)
            to_heads = lambda t: t.reshape(b, n, HEADS, DIM_HEAD).transpose(0, 2, 1, 3)
            q, k, v = (to_heads(q), to_heads(k), to_heads(v))
            q = l2norm(q) * qs
            k = l2norm(k) * ksc
            q, k = rotary_xpos(q, k)
            o = local_attention(q, k, v)
            o = o.transpose(0, 2, 1, 3).reshape(b, n, INNER)
            x = x + o @ wo
            h = shift_token(x)
            mu = h.mean(-1, keepdims=True)
            var = h.var(-1, keepdims=True)
            h = (h - mu) / jnp.sqrt(var + 1e-05) * lg + lb
            h = h @ w1 + b1
            a, g = jnp.split(h, 2, axis=-1)
            h = a * jax.nn.gelu(g, approximate=False)
            x = x + h @ w2 + b2
            return x
        key = jax.random.key(seed)
        ks = jax.random.split(key, 6)
        return {'x': jax.random.normal(ks[0], (B, N, DIM), jnp.float32), 'wqkv': jax.random.normal(ks[1], (DEPTH, DIM, 3 * INNER), jnp.float32) * 0.02, 'q_scale': jnp.ones((DEPTH, DIM_HEAD), jnp.float32), 'k_scale': jnp.ones((DEPTH, DIM_HEAD), jnp.float32), 'wo': jax.random.normal(ks[2], (DEPTH, INNER, DIM), jnp.float32) * 0.02, 'ln_g': jnp.ones((DEPTH, DIM), jnp.float32), 'ln_b': jnp.zeros((DEPTH, DIM), jnp.float32), 'w1': jax.random.normal(ks[3], (DEPTH, DIM, 2 * HID), jnp.float32) * 0.02, 'b1': jnp.zeros((DEPTH, 2 * HID), jnp.float32), 'w2': jax.random.normal(ks[4], (DEPTH, HID, DIM), jnp.float32) * 0.02, 'b2': jnp.zeros((DEPTH, DIM), jnp.float32)}
    _L1_ffn_in = _L1_ffn_setup()

    def _L2_attn_setup():
        import jax, jax.numpy as jnp
        import numpy as np
        DIM = 128
        DIM_HEAD = 16
        HEADS = 8
        EPS = 1e-05

        def rms_norm(x, gamma):
            n = jnp.sqrt(jnp.sum(x * x, axis=-1, keepdims=True))
            return gamma * (x / jnp.maximum(n, 1e-12)) * x.shape[-1] ** 0.5

        def second_taylor_expansion(x):
            d = x.shape[-1]
            x0 = jnp.ones(x.shape[:-1] + (1,), dtype=x.dtype)
            x2 = jnp.einsum('...i,...j->...ij', x, x) * 0.5 ** 0.5
            x2 = x2.reshape(x.shape[:-1] + (d * d,))
            return jnp.concatenate([x0, x, x2], axis=-1)
        key = jax.random.key(seed)
        ks = jax.random.split(key, 4)
        b, n = (4, 1024)
        dim_inner = DIM_HEAD * HEADS
        x = jax.random.normal(ks[0], (b, n, DIM), dtype=jnp.float32)
        gamma = jnp.ones((DIM,), dtype=jnp.float32)
        w_q = jax.random.normal(ks[1], (DIM, dim_inner), dtype=jnp.float32) * DIM ** (-0.5)
        w_kv = jax.random.normal(ks[2], (DIM, dim_inner * 2), dtype=jnp.float32) * DIM ** (-0.5)
        w_out = jax.random.normal(ks[3], (dim_inner, DIM), dtype=jnp.float32) * dim_inner ** (-0.5)
        return {'x': x, 'gamma': gamma, 'w_q': w_q, 'w_kv': w_kv, 'w_out': w_out}
    _L2_attn_in = _L2_attn_setup()

    def _L2_ffn_setup():
        import jax, jax.numpy as jnp
        import numpy as np
        D_IN, D_HID = (128, 512)

        def _ternary(key, shape):
            return jax.random.randint(key, shape, -1, 2).astype(jnp.float32)

        def _tlin(x, w, s):
            return jnp.einsum('bsi,oi->bso', x, w) * s
        key = jax.random.key(seed)
        ks = jax.random.split(key, 12)
        inv = lambda fan: 1.0 / np.sqrt(fan).astype(np.float32)
        return {'x': jax.random.normal(ks[0], (4, 256, D_IN), dtype=jnp.float32), 'w1_w': _ternary(ks[1], (D_HID, D_IN)), 'w1_s': jax.random.uniform(ks[2], (D_HID,), dtype=jnp.float32) * inv(D_IN), 'w2_w': _ternary(ks[3], (D_HID, D_IN)), 'w2_s': jax.random.uniform(ks[4], (D_HID,), dtype=jnp.float32) * inv(D_IN), 'h1_w': _ternary(ks[5], (D_HID, D_HID)), 'h1_s': jax.random.uniform(ks[6], (D_HID,), dtype=jnp.float32) * inv(D_HID), 'h2_w': _ternary(ks[7], (D_HID, D_HID)), 'h2_s': jax.random.uniform(ks[8], (D_HID,), dtype=jnp.float32) * inv(D_HID), 'w3_w': _ternary(ks[9], (D_IN, D_HID)), 'w3_s': jax.random.uniform(ks[10], (D_IN,), dtype=jnp.float32) * inv(D_HID)}
    _L2_ffn_in = _L2_ffn_setup()

    def _L3_attn_setup():
        import jax, jax.numpy as jnp
        import numpy as np
        PI = float(np.pi)
        EPS = 1e-06
        key = jax.random.key(seed)
        k1, k2, k3, k4, k5 = jax.random.split(key, 5)
        B, T, D, H, Dh = (4, 512, 128, 16, 64)

        def xavier(k, shape):
            fan_in, fan_out = (shape[-2], shape[-1])
            lim = float(np.sqrt(6.0 / (fan_in + fan_out)))
            return jax.random.uniform(k, shape, jnp.float32, -lim, lim)
        return {'query': jax.random.normal(k1, (B, T, D), jnp.float32), 'W_Q': xavier(k2, (H, D, 1)), 'W_K': xavier(k3, (H, D, 1)), 'W_V': xavier(k4, (H, D, Dh)), 'W_O': xavier(k5, (D, Dh, H))}
    _L3_attn_in = _L3_attn_setup()

    def _L3_ffn_setup():
        import jax, jax.numpy as jnp
        import numpy as np
        B, S, H, I, E_ROUTED, TOP_K = (8, 256, 128, 256, 8, 2)

        def _expert(x, Wg, Wu, Wd):
            return jax.nn.silu(x @ Wg.T) * (x @ Wu.T) @ Wd.T
        key = jax.random.key(seed)
        ks = jax.random.split(key, 9)
        s = 0.02
        return {'x': jax.random.normal(ks[0], (B, S, H), dtype=jnp.float32), 'Wg_s': jax.random.normal(ks[1], (I, H), dtype=jnp.float32) * s, 'Wu_s': jax.random.normal(ks[2], (I, H), dtype=jnp.float32) * s, 'Wd_s': jax.random.normal(ks[3], (H, I), dtype=jnp.float32) * s, 'Wg': jax.random.normal(ks[4], (E_ROUTED, I, H), dtype=jnp.float32) * s, 'Wu': jax.random.normal(ks[5], (E_ROUTED, I, H), dtype=jnp.float32) * s, 'Wd': jax.random.normal(ks[6], (E_ROUTED, H, I), dtype=jnp.float32) * s, 'Wr': jax.random.normal(ks[7], (E_ROUTED, H), dtype=jnp.float32) * s, 'rb': jnp.zeros((E_ROUTED,), dtype=jnp.float32)}
    _L3_ffn_in = _L3_ffn_setup()
    _d = {'L0_attn_x': _L0_attn_in['x'], 'L0_attn_W': _L0_attn_in['W'], 'L0_ffn_gate_w': _L0_ffn_in['gate_w'], 'L0_ffn_gate_b': _L0_ffn_in['gate_b'], 'L0_ffn_expert_bias': _L0_ffn_in['expert_bias'], 'L0_ffn_w1': _L0_ffn_in['w1'], 'L0_ffn_b1': _L0_ffn_in['b1'], 'L0_ffn_w2': _L0_ffn_in['w2'], 'L0_ffn_b2': _L0_ffn_in['b2'], 'L1_attn_Wd_q_w': _L1_attn_in['Wd_q_w'], 'L1_attn_Wd_q_b': _L1_attn_in['Wd_q_b'], 'L1_attn_Wu_q_w': _L1_attn_in['Wu_q_w'], 'L1_attn_Wu_q_b': _L1_attn_in['Wu_q_b'], 'L1_attn_Wq_r_w': _L1_attn_in['Wq_r_w'], 'L1_attn_Wq_r_b': _L1_attn_in['Wq_r_b'], 'L1_attn_Wk_r_w': _L1_attn_in['Wk_r_w'], 'L1_attn_Wk_r_b': _L1_attn_in['Wk_r_b'], 'L1_attn_Wd_kv_w': _L1_attn_in['Wd_kv_w'], 'L1_attn_Wd_kv_b': _L1_attn_in['Wd_kv_b'], 'L1_attn_Wu_k_w': _L1_attn_in['Wu_k_w'], 'L1_attn_Wu_k_b': _L1_attn_in['Wu_k_b'], 'L1_attn_Wu_v_w': _L1_attn_in['Wu_v_w'], 'L1_attn_Wu_v_b': _L1_attn_in['Wu_v_b'], 'L1_attn_Wo_w': _L1_attn_in['Wo_w'], 'L1_attn_Wo_b': _L1_attn_in['Wo_b'], 'L1_ffn_wqkv': _L1_ffn_in['wqkv'], 'L1_ffn_q_scale': _L1_ffn_in['q_scale'], 'L1_ffn_k_scale': _L1_ffn_in['k_scale'], 'L1_ffn_wo': _L1_ffn_in['wo'], 'L1_ffn_ln_g': _L1_ffn_in['ln_g'], 'L1_ffn_ln_b': _L1_ffn_in['ln_b'], 'L1_ffn_w1': _L1_ffn_in['w1'], 'L1_ffn_b1': _L1_ffn_in['b1'], 'L1_ffn_w2': _L1_ffn_in['w2'], 'L1_ffn_b2': _L1_ffn_in['b2'], 'L2_attn_gamma': _L2_attn_in['gamma'], 'L2_attn_w_q': _L2_attn_in['w_q'], 'L2_attn_w_kv': _L2_attn_in['w_kv'], 'L2_attn_w_out': _L2_attn_in['w_out'], 'L2_ffn_w1_w': _L2_ffn_in['w1_w'], 'L2_ffn_w1_s': _L2_ffn_in['w1_s'], 'L2_ffn_w2_w': _L2_ffn_in['w2_w'], 'L2_ffn_w2_s': _L2_ffn_in['w2_s'], 'L2_ffn_h1_w': _L2_ffn_in['h1_w'], 'L2_ffn_h1_s': _L2_ffn_in['h1_s'], 'L2_ffn_h2_w': _L2_ffn_in['h2_w'], 'L2_ffn_h2_s': _L2_ffn_in['h2_s'], 'L2_ffn_w3_w': _L2_ffn_in['w3_w'], 'L2_ffn_w3_s': _L2_ffn_in['w3_s'], 'L3_attn_W_Q': _L3_attn_in['W_Q'], 'L3_attn_W_K': _L3_attn_in['W_K'], 'L3_attn_W_V': _L3_attn_in['W_V'], 'L3_attn_W_O': _L3_attn_in['W_O'], 'L3_ffn_Wg_s': _L3_ffn_in['Wg_s'], 'L3_ffn_Wu_s': _L3_ffn_in['Wu_s'], 'L3_ffn_Wd_s': _L3_ffn_in['Wd_s'], 'L3_ffn_Wg': _L3_ffn_in['Wg'], 'L3_ffn_Wu': _L3_ffn_in['Wu'], 'L3_ffn_Wd': _L3_ffn_in['Wd'], 'L3_ffn_Wr': _L3_ffn_in['Wr'], 'L3_ffn_rb': _L3_ffn_in['rb']}
    _x0 = _d['L0_attn_x']
    _d['L0_attn_x'] = jax.random.normal(jax.random.fold_in(jax.random.key(seed), 1), (8, 256, 128), dtype=_x0.dtype)
    del _x0
    return _d

def reference(L0_attn_x, L0_attn_W, L0_ffn_gate_w, L0_ffn_gate_b, L0_ffn_expert_bias, L0_ffn_w1, L0_ffn_b1, L0_ffn_w2, L0_ffn_b2, L1_attn_Wd_q_w, L1_attn_Wd_q_b, L1_attn_Wu_q_w, L1_attn_Wu_q_b, L1_attn_Wq_r_w, L1_attn_Wq_r_b, L1_attn_Wk_r_w, L1_attn_Wk_r_b, L1_attn_Wd_kv_w, L1_attn_Wd_kv_b, L1_attn_Wu_k_w, L1_attn_Wu_k_b, L1_attn_Wu_v_w, L1_attn_Wu_v_b, L1_attn_Wo_w, L1_attn_Wo_b, L1_ffn_wqkv, L1_ffn_q_scale, L1_ffn_k_scale, L1_ffn_wo, L1_ffn_ln_g, L1_ffn_ln_b, L1_ffn_w1, L1_ffn_b1, L1_ffn_w2, L1_ffn_b2, L2_attn_gamma, L2_attn_w_q, L2_attn_w_kv, L2_attn_w_out, L2_ffn_w1_w, L2_ffn_w1_s, L2_ffn_w2_w, L2_ffn_w2_s, L2_ffn_h1_w, L2_ffn_h1_s, L2_ffn_h2_w, L2_ffn_h2_s, L2_ffn_w3_w, L2_ffn_w3_s, L3_attn_W_Q, L3_attn_W_K, L3_attn_W_V, L3_attn_W_O, L3_ffn_Wg_s, L3_ffn_Wu_s, L3_ffn_Wd_s, L3_ffn_Wg, L3_ffn_Wu, L3_ffn_Wd, L3_ffn_Wr, L3_ffn_rb):

    def _L0_attn_ref(x, W):
        import jax, jax.numpy as jnp
        import numpy as np
        EPS = 1e-06
        D = x.shape[-1]
        qkv = x @ W
        q, k, v = jnp.split(qkv, 3, axis=-1)
        q = jax.nn.elu(q) + 1.0
        k = jax.nn.elu(k) + 1.0
        KV = jnp.einsum('bld,blh->bhd', k, v)
        k_sum = k.sum(axis=1)
        Z = 1.0 / (jnp.einsum('bld,bd->bl', q, k_sum) + EPS)
        V = jnp.einsum('bld,bhd,bl->blh', q, KV, Z)
        return V

    def _L0_ffn_ref(x, gate_w, gate_b, expert_bias, w1, b1, w2, b2):
        import jax, jax.numpy as jnp
        import numpy as np
        D_MODEL = 128
        D_FF = 512
        NUM_EXPERTS = 8
        gate_logits = jnp.einsum('bsd,ed->bse', x, gate_w) + gate_b + expert_bias
        top_idx = jnp.argmax(gate_logits, axis=-1)
        out = jnp.zeros_like(x)
        for e in range(NUM_EXPERTS):
            mask = (top_idx == e)[..., None].astype(x.dtype)
            h = jax.nn.relu(jnp.einsum('bsd,df->bsf', x, w1[e]) + b1[e])
            y = jnp.einsum('bsf,fd->bsd', h, w2[e]) + b2[e]
            out = out + mask * y
        return out

    def _L1_attn_ref(x, Wd_q_w, Wd_q_b, Wu_q_w, Wu_q_b, Wq_r_w, Wq_r_b, Wk_r_w, Wk_r_b, Wd_kv_w, Wd_kv_b, Wu_k_w, Wu_k_b, Wu_v_w, Wu_v_b, Wo_w, Wo_b):
        import jax, jax.numpy as jnp
        import numpy as np
        NUM_HEAD = 16
        D_Q = 64
        D_KV = 64
        ROPE_BASE = 10000.0

        def _cos_sin(seq_len, dim):
            pos = jnp.arange(seq_len, dtype=jnp.float32)[:, None]
            ids = jnp.arange(dim // 2, dtype=jnp.float32)
            theta = ROPE_BASE ** (-2.0 * ids) / (dim // 2)
            r = pos * theta[None, :]
            return (jnp.cos(r), jnp.sin(r))

        def _rope(x, cos, sin):
            b, s, d = x.shape
            xv = x.reshape(b, s, d // 2, 2)
            x0, x1 = (xv[..., 0], xv[..., 1])
            out = jnp.stack([x0 * cos - x1 * sin, x1 * cos + x0 * sin], axis=-1)
            return out.reshape(b, s, d)
        b, s, d_model = x.shape
        h = NUM_HEAD
        hd = d_model // h
        scale = jnp.sqrt(jnp.float32(h + D_KV + D_Q))

        def heads(t):
            return t.reshape(b, s, h, hd).transpose(0, 2, 1, 3)
        cos, sin = _cos_sin(s, d_model)
        ct_q = x @ Wd_q_w + Wd_q_b
        qt_c = heads(ct_q @ Wu_q_w + Wu_q_b)
        qt_r = heads(_rope(ct_q @ Wq_r_w + Wq_r_b, cos, sin))
        query = qt_c + qt_r
        ct_kv = x @ Wd_kv_w + Wd_kv_b
        kt_c = heads(ct_kv @ Wu_k_w + Wu_k_b)
        kt_r = heads(_rope(x @ Wk_r_w + Wk_r_b, cos, sin))
        key = kt_c + kt_r
        value = heads(ct_kv @ Wu_v_w + Wu_v_b)
        attn = jnp.einsum('bhqd,bhkd->bhqk', query, key) / scale
        attn = jax.nn.softmax(attn, axis=-1)
        out = jnp.einsum('bhqk,bhkd->bhqd', attn, value)
        out = out.transpose(0, 2, 1, 3).reshape(b, s, d_model)
        return out @ Wo_w + Wo_b

    def _L1_ffn_ref(x, wqkv, q_scale, k_scale, wo, ln_g, ln_b, w1, b1, w2, b2):
        import jax, jax.numpy as jnp
        import numpy as np
        DIM = 128
        DEPTH = 2
        HEADS = 8
        DIM_HEAD = 64
        WINDOW = 64
        INNER = HEADS * DIM_HEAD
        HID = int(DIM * 4 * 2 / 3)
        B, N = (2, 1024)
        QK_SCALE = 8.0

        def shift_token(t):
            t1, t2 = jnp.split(t, 2, axis=-1)
            t2 = jnp.pad(t2, ((0, 0), (1, 0), (0, 0)))[:, :-1]
            return jnp.concatenate([t1, t2], axis=-1)

        def l2norm(t):
            return t / jnp.clip(jnp.linalg.norm(t, axis=-1, keepdims=True), 1e-12)

        def rotate_half(x):
            x1, x2 = jnp.split(x, 2, axis=-1)
            return jnp.concatenate([-x2, x1], axis=-1)

        def rotary_xpos(q, k):
            n = q.shape[-2]
            half_idx = jnp.arange(0, DIM_HEAD, 2, dtype=jnp.float32)
            inv_freq = 1.0 / 10000.0 ** (half_idx / DIM_HEAD)
            t = jnp.arange(n, dtype=jnp.float32)
            freqs = t[:, None] * inv_freq[None, :]
            freqs = jnp.concatenate([freqs, freqs], axis=-1)
            base = (half_idx + 0.4 * DIM_HEAD) / (1.4 * DIM_HEAD)
            power = (t - n // 2) / float(WINDOW // 2)
            scale = base[None, :] ** power[:, None]
            scale = jnp.concatenate([scale, scale], axis=-1)
            cos, sin = (jnp.cos(freqs), jnp.sin(freqs))
            q = q * cos * scale + rotate_half(q) * sin * scale
            k = k * cos / scale + rotate_half(k) * sin / scale
            return (q, k)

        def local_attention(q, k, v):
            b, h, n, d = q.shape
            w = n // WINDOW
            bq = q.reshape(b, h, w, WINDOW, d) * QK_SCALE
            bk = k.reshape(b, h, w, WINDOW, d)
            bv = v.reshape(b, h, w, WINDOW, d)

            def look_around(t):
                p = jnp.pad(t, ((0, 0), (0, 0), (1, 0), (0, 0), (0, 0)))
                return jnp.concatenate([p[:, :, :w], p[:, :, 1:]], axis=3)
            bk, bv = (look_around(bk), look_around(bv))
            bt = jnp.arange(n).reshape(w, WINDOW)
            btp = jnp.pad(bt, ((1, 0), (0, 0)), constant_values=-1)
            btk = jnp.concatenate([btp[:w], btp[1:]], axis=1)
            sim = jnp.einsum('bhwid,bhwjd->bhwij', bq, bk)
            i = bt[:, :, None]
            j = btk[:, None, :]
            mask = (i < j) | (i > j + WINDOW) | (j == -1)
            sim = jnp.where(mask, -jnp.finfo(sim.dtype).max, sim)
            attn = jax.nn.softmax(sim, axis=-1)
            out = jnp.einsum('bhwij,bhwjd->bhwid', attn, bv)
            return out.reshape(b, h, n, d)

        def _layer(x, wqkv, qs, ksc, wo, lg, lb, w1, b1, w2, b2):
            b, n, _ = x.shape
            h = shift_token(x)
            qkv = h @ wqkv
            q, k, v = jnp.split(qkv, 3, axis=-1)
            to_heads = lambda t: t.reshape(b, n, HEADS, DIM_HEAD).transpose(0, 2, 1, 3)
            q, k, v = (to_heads(q), to_heads(k), to_heads(v))
            q = l2norm(q) * qs
            k = l2norm(k) * ksc
            q, k = rotary_xpos(q, k)
            o = local_attention(q, k, v)
            o = o.transpose(0, 2, 1, 3).reshape(b, n, INNER)
            x = x + o @ wo
            h = shift_token(x)
            mu = h.mean(-1, keepdims=True)
            var = h.var(-1, keepdims=True)
            h = (h - mu) / jnp.sqrt(var + 1e-05) * lg + lb
            h = h @ w1 + b1
            a, g = jnp.split(h, 2, axis=-1)
            h = a * jax.nn.gelu(g, approximate=False)
            x = x + h @ w2 + b2
            return x
        for l in range(DEPTH):
            x = _layer(x, wqkv[l], q_scale[l], k_scale[l], wo[l], ln_g[l], ln_b[l], w1[l], b1[l], w2[l], b2[l])
        return x

    def _L2_attn_ref(x, gamma, w_q, w_kv, w_out):
        import jax, jax.numpy as jnp
        import numpy as np
        DIM = 128
        DIM_HEAD = 16
        HEADS = 8
        EPS = 1e-05

        def rms_norm(x, gamma):
            n = jnp.sqrt(jnp.sum(x * x, axis=-1, keepdims=True))
            return gamma * (x / jnp.maximum(n, 1e-12)) * x.shape[-1] ** 0.5

        def second_taylor_expansion(x):
            d = x.shape[-1]
            x0 = jnp.ones(x.shape[:-1] + (1,), dtype=x.dtype)
            x2 = jnp.einsum('...i,...j->...ij', x, x) * 0.5 ** 0.5
            x2 = x2.reshape(x.shape[:-1] + (d * d,))
            return jnp.concatenate([x0, x, x2], axis=-1)
        b, n, _ = x.shape
        h, dh = (HEADS, DIM_HEAD)
        normed = rms_norm(x, gamma)
        q = (normed @ w_q).reshape(b, n, h, dh).transpose(0, 2, 1, 3)
        kv = (normed @ w_kv).reshape(b, n, 2, h, dh).transpose(2, 0, 3, 1, 4)
        k, v = (kv[0], kv[1])
        q = q * dh ** (-0.5)
        q = second_taylor_expansion(q)
        k = second_taylor_expansion(k)
        kv_state = jnp.einsum('bhnd,bhne->bhde', k, v)
        k_sum = jnp.sum(k, axis=2)
        den = jnp.einsum('bhnd,bhd->bhn', q, k_sum)
        qk_inv = 1.0 / jnp.maximum(den, EPS)
        out = jnp.einsum('bhnd,bhde->bhne', q, kv_state) * qk_inv[..., None]
        out = out.transpose(0, 2, 1, 3).reshape(b, n, h * dh)
        return out @ w_out

    def _L2_ffn_ref(x, w1_w, w1_s, w2_w, w2_s, h1_w, h1_s, h2_w, h2_s, w3_w, w3_s):
        import jax, jax.numpy as jnp
        import numpy as np
        D_IN, D_HID = (128, 512)

        def _ternary(key, shape):
            return jax.random.randint(key, shape, -1, 2).astype(jnp.float32)

        def _tlin(x, w, s):
            return jnp.einsum('bsi,oi->bso', x, w) * s
        h = jax.nn.silu(_tlin(x, w1_w, w1_s)) * _tlin(x, w2_w, w2_s)
        h = jax.nn.gelu(_tlin(h, h1_w, h1_s), approximate=False)
        h = jax.nn.gelu(_tlin(h, h2_w, h2_s), approximate=False)
        return _tlin(h, w3_w, w3_s)

    def _L3_attn_ref(query, W_Q, W_K, W_V, W_O):
        import jax, jax.numpy as jnp
        import numpy as np
        PI = float(np.pi)
        EPS = 1e-06
        q = jnp.einsum('btd,hdo->btho', query, W_Q)
        k = jnp.einsum('btd,hdo->btho', query, W_K)
        V = jnp.einsum('btd,hde->bthe', query, W_V)
        q = jnp.tanh(q) * (PI / 4)
        k = jnp.tanh(k) * (PI / 4)
        cos_k, sin_k = (jnp.cos(k), jnp.sin(k))
        cos_q, sin_q = (jnp.cos(q), jnp.sin(q))
        cos_KV = jnp.cumsum(cos_k * V, axis=1)
        sin_KV = jnp.cumsum(sin_k * V, axis=1)
        heads = cos_q * cos_KV + sin_q * sin_KV
        cos_K = jnp.cumsum(cos_k, axis=1)
        sin_K = jnp.cumsum(sin_k, axis=1)
        denom = cos_q * cos_K + sin_q * sin_K + EPS
        heads = heads / denom
        return jnp.einsum('deh,bthe->btd', W_O, heads)

    def _L3_ffn_ref(x, Wg_s, Wu_s, Wd_s, Wg, Wu, Wd, Wr, rb):
        import jax, jax.numpy as jnp
        import numpy as np
        B, S, H, I, E_ROUTED, TOP_K = (8, 256, 128, 256, 8, 2)

        def _expert(x, Wg, Wu, Wd):
            return jax.nn.silu(x @ Wg.T) * (x @ Wu.T) @ Wd.T
        shared = _expert(x, Wg_s, Wu_s, Wd_s)
        logits = jnp.einsum('bsh,eh->bse', x, Wr) + rb
        probs = jax.nn.sigmoid(logits)
        scores, idx = jax.lax.top_k(probs, TOP_K)
        cw = (jax.nn.one_hot(idx, E_ROUTED, dtype=x.dtype) * scores[..., None]).sum(-2)
        out = shared
        for e in range(E_ROUTED):
            out = out + cw[..., e:e + 1] * _expert(x, Wg[e], Wu[e], Wd[e])
        return out
    x = L0_attn_x
    x = _layernorm(x + _L0_attn_ref(x, L0_attn_W), axis=-1)
    x = _layernorm(x + _L0_ffn_ref(x, L0_ffn_gate_w, L0_ffn_gate_b, L0_ffn_expert_bias, L0_ffn_w1, L0_ffn_b1, L0_ffn_w2, L0_ffn_b2), axis=-1)
    x = _layernorm(x + _L1_attn_ref(x, L1_attn_Wd_q_w, L1_attn_Wd_q_b, L1_attn_Wu_q_w, L1_attn_Wu_q_b, L1_attn_Wq_r_w, L1_attn_Wq_r_b, L1_attn_Wk_r_w, L1_attn_Wk_r_b, L1_attn_Wd_kv_w, L1_attn_Wd_kv_b, L1_attn_Wu_k_w, L1_attn_Wu_k_b, L1_attn_Wu_v_w, L1_attn_Wu_v_b, L1_attn_Wo_w, L1_attn_Wo_b), axis=-1)
    x = _layernorm(x + _L1_ffn_ref(x, L1_ffn_wqkv, L1_ffn_q_scale, L1_ffn_k_scale, L1_ffn_wo, L1_ffn_ln_g, L1_ffn_ln_b, L1_ffn_w1, L1_ffn_b1, L1_ffn_w2, L1_ffn_b2), axis=-1)
    x = _layernorm(x + _L2_attn_ref(x, L2_attn_gamma, L2_attn_w_q, L2_attn_w_kv, L2_attn_w_out), axis=-1)
    x = _layernorm(x + _L2_ffn_ref(x, L2_ffn_w1_w, L2_ffn_w1_s, L2_ffn_w2_w, L2_ffn_w2_s, L2_ffn_h1_w, L2_ffn_h1_s, L2_ffn_h2_w, L2_ffn_h2_s, L2_ffn_w3_w, L2_ffn_w3_s), axis=-1)
    x = _layernorm(x + _L3_attn_ref(x, L3_attn_W_Q, L3_attn_W_K, L3_attn_W_V, L3_attn_W_O), axis=-1)
    x = _layernorm(x + _L3_ffn_ref(x, L3_ffn_Wg_s, L3_ffn_Wu_s, L3_ffn_Wd_s, L3_ffn_Wg, L3_ffn_Wu, L3_ffn_Wd, L3_ffn_Wr, L3_ffn_rb), axis=-1)
    return x

_drawn_inputs = setup_inputs


def setup_inputs(seed=0):
    import zlib

    import numpy as np

    out = dict(_drawn_inputs(seed))
    spreads = {'L0_ffn_expert_bias': (0.0, 0.1),
     'L1_attn_Wd_q_b': (0.0, 0.8),
     'L1_attn_Wu_q_b': (0.0, 0.8),
     'L1_attn_Wq_r_b': (0.0, 0.8),
     'L1_attn_Wk_r_b': (0.0, 2.0),
     'L1_attn_Wd_kv_b': (0.0, 0.503),
     'L1_attn_Wu_k_b': (0.0, 2.0),
     'L1_attn_Wu_v_b': (0.0, 0.407),
     'L1_attn_Wo_b': (0.0, 0.1),
     'L1_ffn_q_scale': (1.0, 0.6),
     'L1_ffn_k_scale': (1.0, 0.6),
     'L1_ffn_ln_g': (1.0, 0.6),
     'L1_ffn_ln_b': (0.0, 0.8),
     'L1_ffn_b1': (0.0, 0.8),
     'L1_ffn_b2': (0.0, 0.446),
     'L2_attn_gamma': (1.0, 0.2),
     'L3_ffn_rb': (0.0, 0.8)}
    factors = {'L1_attn_Wd_q_w': 8.0,
     'L1_attn_Wu_q_w': 8.0,
     'L1_attn_Wq_r_w': 8.0,
     'L1_attn_Wk_r_w': 8.0,
     'L1_attn_Wd_kv_w': 8.0,
     'L1_attn_Wu_k_w': 8.0,
     'L1_attn_Wu_v_w': 3.61,
     'L1_ffn_w1': 6.774,
     'L1_ffn_w2': 4.744,
     'L2_ffn_w1_w': 8.0,
     'L2_ffn_w1_s': 8.0,
     'L2_ffn_w2_w': 8.0,
     'L2_ffn_w2_s': 8.0,
     'L2_ffn_h1_w': 8.0,
     'L2_ffn_h1_s': 8.0,
     'L2_ffn_h2_w': 8.0,
     'L2_ffn_h2_s': 8.0,
     'L2_ffn_w3_w': 8.0,
     'L2_ffn_w3_s': 8.0,
     'L3_ffn_Wg_s': 6.637,
     'L3_ffn_Wu_s': 6.422,
     'L3_ffn_Wd_s': 6.297,
     'L3_ffn_Wg': 8.0,
     'L3_ffn_Wu': 8.0,
     'L3_ffn_Wd': 8.0,
     'L3_ffn_Wr': 8.0,
     'L0_ffn_b2': 3.026}
    for name, (base, spread) in spreads.items():
        noise = np.random.default_rng([zlib.crc32(name.encode()), seed]).standard_normal(out[name].shape)
        drawn = base * np.exp(spread * noise) if base else spread * noise
        out[name] = jnp.asarray(drawn.astype(out[name].dtype))
    for name, factor in factors.items():
        out[name] = (out[name] * factor).astype(out[name].dtype)
    return out
```

```python
from contextlib import ExitStack

import concourse.bass as bass
from concourse import mybir
import numpy as np

F32 = mybir.dt.float32
F32R = mybir.dt.float32r
U32 = mybir.dt.uint32
ALU = mybir.AluOpType
ACT = mybir.ActivationFunctionType
X = mybir.AxisListType.X

D = 128
SEQ = 256
NSEQ = 8
STREAMS = 2
TURNS = NSEQ // STREAMS
LN_EPS = 1e-5

E0, F0 = 8, 512
H1, DH1 = 16, 8
LH, LD, HID, WIN = 8, 64, 341, 64
FT = [128, 128, 85]
H2, DH2 = 8, 16
H3, DH3 = 16, 64
E3, I3 = 9, 256


def columns(parts):
    at, out = 0, {}
    for name, n in parts:
        out[name] = (at, n)
        at += n
    return out, at


SMALL, N_SMALL = columns([
    ("l0_w", 384),
    ("l1_gate", E0), ("l1_gb", E0), ("l1_eb", E0), ("l1_b1", E0 * 4), ("l1_b2", D),
    ("l2_down", 128), ("l2_down_b", 1), ("l2_qc", 128), ("l2_qr", 128), ("l2_qrs", 128),
    ("l2_kc", 128), ("l2_kr", 128), ("l2_krs", 128), ("l2_v", 128), ("l2_o", 4 * 128),
    ("l2_qcb", 1), ("l2_qrb", 1), ("l2_qrsb", 1), ("l2_kcb", 1), ("l2_krb", 1), ("l2_krsb", 1),
    ("l2_vb", 128), ("l2_ob", 128),
    ("l3_g", 2), ("l3_b", 2), ("l3_b1", 12), ("l3_b2", 2 * 128), ("l3_scale", 2 * 4 * 64),
    ("l4_gamma", 1), ("l4_w", 384), ("l4_o", 2 * 128),
    ("l5_s1", 4), ("l5_s2", 4), ("l5_h1s", 4), ("l5_h2s", 4), ("l5_s3", 128),
    ("l6_q", 128), ("l6_k", 128), ("l6_v", 1024), ("l6_o", 1024),
    ("l7_gate", 8), ("l7_rb", 8),
])
L3W, N_L3W = columns([("qkv", 1536), ("o", 512), ("w1", 2 * HID), ("w2", 3 * 128)])
L5W, N_L5W = columns([("w1", 512), ("w2", 512), ("h1", 2048), ("h2", 2048), ("w3", 512)])
N_L1W = E0 * (F0 + F0)
N_L7W = E3 * (2 * I3 + 2 * D)
N_REGION_A = max(N_L1W, N_L5W)
N_REGION_B = max(2 * N_L3W, N_L7W)
CONST, N_CONST = columns([
    ("ident", 128), ("iota8", 8), ("rope_c", 256), ("rope_s", 256), ("tri", 384), ("band", 384),
    ("xpos", 512), ("mask2", 4), ("mask4", 2), ("mask6", 16), ("half_pi", 1), ("mhalf", 32), ("ones", 256),
    ("rows8", 128), ("rows16", 128), ("pair_sum", 128), ("half", 1), ("root_half", 1),
])
CONSTR, N_CONSTR = columns([("sel_qh", 512), ("sel_ql", 512), ("sel_kh", 512), ("sel_kl", 512), ("sel_max", 512)])


def shape_constants():
    f = np.float32
    c = np.zeros((128, N_CONST), f)
    cr = np.zeros((128, N_CONSTR), f)
    p = np.arange(128)

    def put(name, a):
        at, n = CONST[name]
        c[:, at:at + n] = np.asarray(a, f).reshape(128, n)

    put("ident", np.eye(128))
    put("iota8", np.tile(np.arange(8), (128, 1)))
    theta = f(10000.0) ** (f(-2.0) * np.arange(64, dtype=f)) / f(64)
    r = np.arange(SEQ, dtype=f)[None, :] * theta[p // 2][:, None]
    put("rope_c", np.cos(r))
    put("rope_s", np.sin(r) * np.where(p % 2 == 0, -1, 1)[:, None])
    tri = (p[None, :] >= p[:, None]).astype(f)
    put("tri", np.concatenate([tri, np.ones((128, 128)), tri], 1))
    band = np.zeros((128, 384), f)
    for t, at, n in ((0, 0, 128), (1, 128, 256)):
        i = t * 128 + p[:, None]
        j = np.arange(n)[None, :]
        band[:, at:at + n] = np.where((i < j) | (i > j + WIN), f(-1e30), f(0))
    put("band", band)
    half = np.arange(0, LD, 2, dtype=f)
    inv = f(1.0) / f(10000.0) ** (half / f(LD))
    t = np.arange(SEQ, dtype=f)
    fr = np.concatenate([t[:, None] * inv[None, :]] * 2, 1)
    base = (half + f(0.4 * LD)) / f(1.4 * LD)
    sc = base[None, :] ** ((t - SEQ // 2) / f(WIN // 2))[:, None]
    sc = np.concatenate([sc, sc], 1)
    sign = np.where(np.arange(LD) < LD // 2, -1, 1)[None, :]
    tabs = [[np.cos(fr) * sc, np.sin(fr) * sc * sign], [np.cos(fr) / sc, np.sin(fr) / sc * sign]]
    x = np.zeros((128, 2, 2, 2, 64), f)
    for w in range(2):
        for k in range(2):
            x[:, w, k] = tabs[w][k].reshape(2, 128, 64).transpose(1, 0, 2)
    put("xpos", x)
    put("mask2", (p % 32 // DH1)[:, None] == np.arange(4)[None])
    put("mask4", (p % 32 // DH2)[:, None] == np.arange(2)[None])
    put("mask6", (p % 16)[:, None] == np.arange(16)[None])
    put("half_pi", np.where(p % 32 < 16, np.pi / 2, 0))
    put("mhalf", np.full((128, 32), -0.5))
    put("ones", np.ones((128, 256)))
    put("rows8", (p[:, None] == (p // 32 * 32 + DH1)[None, :]))
    put("rows16", (p[:, None] == (p // 32 * 32 + DH2)[None, :]))
    put("pair_sum", (p[:, None] < 32) & (p[:, None] % 16 == p[None, :] % 16))
    put("half", np.full((128, 1), 0.5))
    put("root_half", np.full((128, 1), 0.5 ** 0.5))
    for name, quads in (("sel_qh", (0, 2)), ("sel_ql", (1, 3)), ("sel_kh", (0, 1)), ("sel_kl", (2, 3))):
        at = CONSTR[name][0]
        for j in range(4):
            for q in quads:
                for k in range(32):
                    cr[32 * j + k, at + 128 * j + 32 * q + k] = 1
    at = CONSTR["sel_max"][0]
    for j in range(4):
        cr[j, at + 128 * j:at + 128 * (j + 1)] = -1
        cr[32 + j, at + 128 * j:at + 128 * (j + 1)] = -1
    return c, cr


SHARED = {
    "pe_input": ("l0_qkv", "l1_lg", "l2_ct", "l3_qkv", "l4_p", "l6_qk", "l7_lg"),
    "pe_second": ("l0_kv", "l1_mTp", "l2_kp", "l3_tp", "l4_hs", "l5_yd", "l6_dn"),
    "pe_hidden": ("l1_z", "l3_z", "l5_z", "l7_z"),
    "pe_values": ("l2_qp", "l6_vp"),
    "pe_values2": ("l2_v", "l3_hs", "l4_bc"),
    "pe_stack": ("st_full", "l3_pt", "l4_stf"),
    "pe_scores": ("l2_s", "l3_s", "l6_a"),
    "pe_maxima": ("l2_m", "l3_hnp"),
    "pe_scoresT": ("l2_st", "l4_st"),
    "pe_weighted": ("l2_pv", "l3_o", "l4_pv", "l6_o"),
    "pe_spread": ("l2_bc", "l3_y2"),
    "pe_output": ("l0_out", "l1_y", "l2_y", "l3_y", "l4_y", "l6_yd", "l7_y"),
    "act_moved": ("l0_v_in", "l1_mT", "l2_cts", "l3_vin", "l4_oin", "l6_csd"),
    "act_stack": ("st_in", "l3_te", "l4_stin", "l5_sg", "l6_va"),
    "act_hidden": ("l1_ha", "l3_gld", "l5_h1", "l7_sg"),
    "act_probs": ("l2_p", "l3_e", "l4_sq", "l5_h2"),
    "act_out": ("l2_ob", "l3_pte", "l6_ot", "l7_pr"),
    "act_squares": ("l3_sqd",),
    "act_normedT": ("l3_hnTd",),
    "dve_first": ("l0_qk", "l1_mask", "l2_split", "l3_ss", "l4_ss", "l6_pr", "l7_lgb"),
    "dve_second": ("l0_kvs_in", "l1_hd", "l2_vs", "l3_qnd", "l4_xnd", "l5_h0", "l6_qkd", "l7_h"),
    "dve_sums": ("l1_acc", "l3_rs", "l4_hsd", "l6_vd", "l7_acc"),
    "dve_max": ("l2_su", "l3_smd", "l4_split", "l6_atd"),
    "dve_max_all": ("l2_mu", "l3_rot", "l4_vd"),
    "dve_max_tok": ("l2_mtok", "l3_ot"),
    "dve_inverse": ("l2_rb", "l3_hnd", "l4_rb"),
    "dve_hidden": ("l3_h",),
    "pool_first": ("l0_ones", "l2_xb", "l3_rn", "l4_rn"),
    "pool_masked": ("l2_qm", "l3_ad", "l4_qm", "l6_qm"),
    "pool_normed": ("l2_on", "l3_pn", "l4_on"),
    "pool_bias": ("l3_xbd", "l4_vset"),
}


class Track:

    def __init__(self, new, name, before=0):
        self.before = before
        self.sems = [new(f"{name}_{s}") for s in range(STREAMS)]
        self.total = 0


class Signal:

    def __init__(self, track, per_turn=1):
        self.track, self.offset, self.per_turn = track, track.total, per_turn
        track.total += per_turn

    def __getitem__(self, s):
        return self.track.sems[s]

    def at(self, turn, k=0):
        return turn * self.track.total + (self.track.before + self.offset + k + 1)


X_OF = [-1, 0, 1, 2, 6, 7, 8, 9, 10]


def build(nc, x_in, small_in, l1_in, l3_in, l5_in, l7_in, const_in, constr_in, out, links, PHASES=8):
    with ExitStack() as ctx:
        def sb(name, shape, dt=F32):
            return ctx.enter_context(nc.sbuf_tensor(name, shape, dt))

        def sem(name):
            return ctx.enter_context(nc.semaphore(name))

        tracks = {}

        def signal(name, per_turn=1, before=0):
            at = next((t for t, names in SHARED.items() if name in names), name)
            if at not in tracks:
                tracks[at] = Track(sem, at, before)
            return Signal(tracks[at], per_turn)

        def f32(ap):
            return ap.bitcast(F32)

        S2 = range(STREAMS)
        small = sb("small", [128, N_SMALL])
        region_a = sb("region_a", [128, N_REGION_A])
        region_b = sb("region_b", [128, N_REGION_B])
        const = sb("const", [128, N_CONST])
        constr = sb("constr", [128, N_CONSTR], F32R)
        xpos = sb("xpos", [128, 2, 2, 2, 2, 64])

        def W(name, a=0, b=None, rows=128):
            at, n = SMALL[name]
            return small[0:rows, at + a:at + (n if b is None else b)]

        def C(name, a=0, b=None):
            at, n = CONST[name]
            return const[:, at + a:at + (n if b is None else b)]

        def CR(name, j):
            at = CONSTR[name][0]
            return constr[:, at + 128 * j:at + 128 * (j + 1)]

        ident = C("ident")

        x = [sb(f"x{s}", [128, 2, D]) for s in S2]
        res = [sb(f"res{s}", [128, 2, D]) for s in S2]
        xT = [sb(f"xT{s}", [128, SEQ]) for s in S2]
        shT = [sb(f"shT{s}", [128, SEQ]) for s in S2]
        qTm = [sb(f"qTm{s}", [128, 2, SEQ]) for s in S2]
        stats = [sb(f"stats{s}", [128, 2, 6]) for s in S2]
        mv = [sb(f"mv{s}", [128, 2, 2]) for s in S2]
        ve = [sb(f"ve{s}", [128, 2]) for s in S2]
        rstd = [sb(f"rstd{s}", [128, 2]) for s in S2]
        tiny = [sb(f"tiny{s}", [128, 224]) for s in S2]
        idx = [sb(f"idx{s}", [128, 2, 8], U32) for s in S2]
        scr = [sb(f"scr{s}", [128, 6400]) for s in S2]
        opr = [sb(f"opr{s}", [128, 4352], F32R) for s in S2]
        P = [[ctx.enter_context(nc.psum_tensor(f"P{s}{b}", [128, 512], F32)) for b in range(4)] for s in S2]

        def view(s, at, *dims):
            n = int(np.prod(dims))
            ap = scr[s][:, at:at + n]
            if len(dims) == 2:
                return ap.rearrange("p (a b) -> p a b", a=dims[0])
            if len(dims) == 3:
                return ap.rearrange("p (a b c) -> p a b c", a=dims[0], b=dims[1])
            return ap

        kst = [opr[s][:, 0:1024].rearrange("p (j n) -> p j n", j=4) for s in S2]
        qst = [opr[s][:, 1024:2048].rearrange("p (j n) -> p j n", j=4) for s in S2]
        qm = [opr[s][:, 2048:4096].rearrange("p (b j n) -> p b j n", b=2, j=4) for s in S2]
        qm6 = [opr[s][:, 2048:4096].rearrange("p (b n) -> p b n", b=8) for s in S2]
        parts = [opr[s][:, 3072:4096].rearrange("p (j n) -> p j n", j=4) for s in S2]
        mT = [opr[s][:, 4096:4352] for s in S2]

        l0_e = [view(s, 0, 3, 256) for s in S2]
        l0_r = [view(s, 768, 3, 256) for s in S2]
        l0_v = [view(s, 1536, 2, 132) for s in S2]
        l0_kvs = [view(s, 1800, 132) for s in S2]
        ex_h = [view(s, 0, 2, 4, 256) for s in S2]
        ex_g = [view(s, 2048, 2, 256) for s in S2]
        ex_log = [tiny[s][:, 0:16].rearrange("p (t e) -> p t e", t=2) for s in S2]
        ex_mx = [tiny[s][:, 16:32].rearrange("p (t e) -> p t e", t=2) for s in S2]
        ex_ix = [tiny[s][:, 32:48].rearrange("p (t e) -> p t e", t=2) for s in S2]
        ex_mk = [tiny[s][:, 48:64].rearrange("p (t e) -> p t e", t=2) for s in S2]
        ex_m2 = [tiny[s][:, 64:80].rearrange("p (t e) -> p t e", t=2) for s in S2]
        ex_mT = [view(s, 2560, 256) for s in S2]
        at_p = [view(s, 0, 4, 512) for s in S2]
        at_rope = [view(s, 0, 6, 256) for s in S2]
        at_v = [view(s, 2048, 2, 16, 32) for s in S2]
        at_o = [view(s, 3072, 4, 256) for s in S2]
        at_r = [view(s, 4096, 4, 256) for s in S2]
        at_ct = [view(s, 5120, 256) for s in S2]
        at_kq = [view(s, 5376, 2, 256) for s in S2]
        at_xb = [view(s, 5888, 2, 128) for s in S2]
        m_tok = [tiny[s][:, 0:8].rearrange("p (t j) -> p t j", t=2) for s in S2]

        l3_tok = [view(s, 0, 2, 2, 512) for s in S2]
        l3_v = [view(s, 2048, 2, 512) for s in S2]
        l3_sq, l3_qn = [view(s, 3072, 2, 512) for s in S2], [view(s, 4096, 2, 512) for s in S2]
        l3_a, l3_b = [view(s, 5120, 512) for s in S2], [view(s, 5632, 512) for s in S2]
        l3_kT = [view(s, 3072, 256) for s in S2]
        l3_sm, l3_pT = [view(s, 3328, 2, 384) for s in S2], [view(s, 4096, 2, 384) for s in S2]
        l3_oT = [view(s, 4864, 4, 256) for s in S2]
        l3_hn, l3_hnT = [view(s, 3072, 2, 128) for s in S2], [view(s, 3328, 256) for s in S2]
        l3_gl, l3_hh = [view(s, 3584, 3, 256) for s in S2], [view(s, 4352, 3, 256) for s in S2]
        l3_xb = [view(s, 6144, 2, 128) for s in S2]
        l4_xn = [view(s, 0, 2, 128) for s in S2]
        l4_v = [view(s, 2048, 2, 8, 32) for s in S2]
        l5_hA, l5_hB, l5_hC = ([view(s, a, 4, 256) for s in S2] for a in (0, 1024, 3072))
        l5_y = [view(s, 4096, 2, 128) for s in S2]
        l6_v = [view(s, 0, 2, 1024) for s in S2]
        l6_at = [view(s, 2048, 4, 384) for s in S2]
        l6_oT = [view(s, 3584, 8, 256) for s in S2]
        l6_th, l6_cs = [view(s, 3584, 2, 256) for s in S2], [view(s, 4096, 2, 256) for s in S2]
        l6_cum, l6_prod, l6_den, l6_rd, l6_qn = ([view(s, a, 256) for s in S2] for a in (4608, 4864, 5120, 5376, 5632))
        k6 = [opr[s][:, 0:256] for s in S2]
        q6 = [opr[s][:, 1024:1280] for s in S2]

        s_small, s_const, s_stage, s_zero, s_zd = (sem(n) for n in ("s_small", "s_const", "s_stage", "s_zero", "s_zd"))
        s_constr, s_xpos = sem("s_constr"), sem("s_xpos")
        s_wa, s_wb = sem("s_wa"), sem("s_wb")
        x_in_done, out_done = signal("x_in", 16), signal("out_done", 16, before=1)
        settled = {}
        chain = {e: sem(f"{e}_link") for e in ("act", "dve", "pool")}
        n_x = X_OF[PHASES] + 1
        n_ln = PHASES + (2 if PHASES > 3 else 0)
        var_ready, rstd_ready = signal("var_ready", n_ln), signal("rstd_ready", n_ln)
        x_ready = signal("x_ready", n_x, before=1)
        xTp, xT_ready = signal("xTp", n_x), signal("xT_ready", n_x)

        l0_ones = signal("l0_ones")
        l0_qkv, l0_v_in, l0_qk, l0_kv, l0_kvs_in, l0_out = (signal(n) for n in
            ("l0_qkv", "l0_v_in", "l0_qk", "l0_kv", "l0_kvs_in", "l0_out"))
        l1_lg, l1_mask, l1_mTp, l1_mT = (signal(n) for n in ("l1_lg", "l1_mask", "l1_mTp", "l1_mT"))
        l1_z, l1_ha, l1_hd = signal("l1_z", 16), signal("l1_ha", 8), signal("l1_hd", 8)
        l1_y, l1_acc = signal("l1_y", 9), signal("l1_acc", 9)
        l2_ct, l2_cts, l2_kp, l2_qp, l2_split, l2_v, l2_vs, l2_xb = (signal(n) for n in
            ("l2_ct", "l2_cts", "l2_kp", "l2_qp", "l2_split", "l2_v", "l2_vs", "l2_xb"))
        st_full, st_in = signal("st_full", 4), signal("st_in", 4)
        l2_qm = signal("l2_qm", 4)
        l2_s, l2_su, l2_m, l2_mu = signal("l2_s", 16), signal("l2_su", 16), signal("l2_m", 4), signal("l2_mu", 4)
        l2_mtok = signal("l2_mtok", 4)
        l2_st, l2_p, l2_pv = signal("l2_st", 16), signal("l2_p", 16), signal("l2_pv", 4)
        l2_ob, l2_bc, l2_rb, l2_on, l2_y = (signal(n) for n in ("l2_ob", "l2_bc", "l2_rb", "l2_on", "l2_y"))

        if PHASES > 3:
            l3_qkv, l3_sqd, l3_ss, l3_rn, l3_qnd, l3_ad, l3_rot = (signal(n, 2 * k) for n, k in
                (("l3_qkv", 6), ("l3_sqd", 4), ("l3_ss", 4), ("l3_rn", 4), ("l3_qnd", 4), ("l3_ad", 4), ("l3_rot", 4)))
            l3_vin, l3_tp, l3_te = signal("l3_vin", 4), signal("l3_tp", 8), signal("l3_te", 8)
            l3_s, l3_smd, l3_e, l3_rs, l3_pn, l3_pt, l3_pte = (signal(n, 16) for n in
                ("l3_s", "l3_smd", "l3_e", "l3_rs", "l3_pn", "l3_pt", "l3_pte"))
            l3_o, l3_ot = signal("l3_o", 8), signal("l3_ot", 8)
            l3_y, l3_hs, l3_hnd, l3_hnp, l3_hnTd, l3_y2, l3_xbd = (signal(n, 2) for n in
                ("l3_y", "l3_hs", "l3_hnd", "l3_hnp", "l3_hnTd", "l3_y2", "l3_xbd"))
            l3_z, l3_gld, l3_h = signal("l3_z", 6), signal("l3_gld", 6), signal("l3_h", 6)
        if PHASES > 4:
            l4_ss, l4_rn, l4_xnd, l4_p, l4_split, l4_vd, l4_vset, l4_oin, l4_hs, l4_hsd, l4_bc, l4_rb, l4_on, l4_y = (
                signal(n) for n in ("l4_ss", "l4_rn", "l4_xnd", "l4_p", "l4_split", "l4_vd", "l4_vset", "l4_oin",
                                    "l4_hs", "l4_hsd", "l4_bc", "l4_rb", "l4_on", "l4_y"))
            l4_stf, l4_stin, l4_qm = signal("l4_stf", 4), signal("l4_stin", 4), signal("l4_qm", 2)
            l4_st, l4_sq, l4_pv = signal("l4_st", 8), signal("l4_sq", 8), signal("l4_pv", 2)
        if PHASES > 5:
            l5_z, l5_sg, l5_h0 = signal("l5_z", 8), signal("l5_sg", 4), signal("l5_h0", 4)
            l5_h1, l5_h2, l5_yd = signal("l5_h1", 2), signal("l5_h2", 2), signal("l5_yd")
        if PHASES > 6:
            l6_qk, l6_csd, l6_pr, l6_dn, l6_qkd, l6_yd = (signal(n) for n in
                ("l6_qk", "l6_csd", "l6_pr", "l6_dn", "l6_qkd", "l6_yd"))
            l6_vp, l6_va, l6_vd = signal("l6_vp", 4), signal("l6_va", 2), signal("l6_vd", 2)
            l6_qm, l6_a, l6_atd, l6_o, l6_ot = signal("l6_qm", 16), signal("l6_a", 16), signal("l6_atd", 16), signal("l6_o", 16), signal("l6_ot", 8)
        if PHASES > 7:
            l7_lg, l7_lgb, l7_pr = (signal(n) for n in ("l7_lg", "l7_lgb", "l7_pr"))
            l7_z, l7_sg, l7_h = signal("l7_z", 18), signal("l7_sg", 18), signal("l7_h", 18)
            l7_y, l7_acc = signal("l7_y", 9), signal("l7_acc", 9)

        def settle(eng):
            eng.sem_inc(settled[eng], 1)

        class Links:

            def __init__(self, name, eng, turn):
                self.name, self.eng, self.turn, self.n = name, eng, turn, 0

            def __call__(self, ins):
                ins.then_inc(chain[self.name], 1)
                self.n += 1
                self.eng.wait_ge(chain[self.name], self.turn * links[self.name] + self.n)

            def close(self):
                if links[self.name] != max(self.n, 1):
                    raise ValueError(f"LINK {self.name} {max(self.n, 1)}")

        block = ctx.enter_context(nc.Block())

        @block.sync
        def _(sp):
            sp.dma_start(const[:, :], const_in).then_inc(s_const, 16)
            sp.dma_start(scr[0][:, 0:N_CONSTR], constr_in).then_inc(s_stage, 16)
            sp.dma_start(small[:, :], small_in).then_inc(s_small, 16)
            for s in S2:
                sp.sem_inc(out_done[s], 1)
            with sp.Fori(0, TURNS) as c:
                for s in S2:
                    sp.wait_ge(out_done[s], out_done.at(c, -1))
                    sp.dma_start(x[s][:, :, :], x_in[2 * c + s, :, :].rearrange("(t p) d -> p t d", p=128)
                                 ).then_inc(x_in_done[s], 16)
                if PHASES > 1:
                    sp.dma_start(region_a[:, 0:N_L1W], l1_in).then_inc(s_wa, 16)
                if PHASES > 3:
                    sp.dma_start(region_b[:, 0:2 * N_L3W], l3_in).then_inc(s_wb, 16)
                if PHASES > 5:
                    for s in S2:
                        sp.wait_ge(x_ready[s], x_ready.at(c, X_OF[2]))
                    sp.dma_start(region_a[:, 0:N_L5W], l5_in).then_inc(s_wa, 16)
                if PHASES > 7:
                    for s in S2:
                        sp.wait_ge(x_ready[s], x_ready.at(c, X_OF[4]))
                    sp.dma_start(region_b[:, 0:N_L7W], l7_in).then_inc(s_wb, 16)
                for s in S2:
                    sp.wait_ge(x_ready[s], x_ready.at(c, n_x - 1))
                    sp.dma_start(out[2 * c + s, :, :].rearrange("(t p) d -> p t d", p=128), x[s][:, :, :]
                                 ).then_inc(out_done[s], 16)
            for s in S2:
                sp.wait_ge(out_done[s], out_done.per_turn * TURNS + 1)

        n_wa = 16 * ((PHASES > 1) + (PHASES > 5))
        n_wb = 16 * ((PHASES > 3) + (PHASES > 7))

        @block.tensor
        def _(pe):
            pe.wait_ge(s_const, 16)
            pe.wait_ge(s_small, 16)
            pe.wait_ge(s_constr, 1)
            pe.wait_ge(s_zero, 1)
            pe.wait_ge(s_zd, 1)
            with pe.Fori(0, TURNS) as c:

                def mm(out_, lhsT, rhs, start=True, stop=True):
                    return pe.matmul(out_, lhsT, rhs, start=start, stop=stop)

                def transpose_x(s, k, src=x, ready=None):
                    if ready is not None:
                        pe.wait_ge(ready[s], ready.at(c))
                    if k == 0:
                        pe.wait_ge(x_in_done[s], x_in_done.at(c, 15))
                        pe.wait_ge(x_ready[s], x_ready.at(c, -1))
                    else:
                        pe.wait_ge(x_ready[s], x_ready.at(c, k - 1))
                    for t in range(2):
                        ins = pe.transpose(P[s][0][:, 128 * t:128 * t + 128], src[s][:, t, :], ident)
                    ins.then_inc(xTp[s], 1)
                    pe.wait_ge(xT_ready[s], xT_ready.at(c, k))

                def l0_project(s):
                    ins = mm(P[s][1][:, 0:256], W("l0_w", 0, 128), xT[s][:, :])
                    for t in range(2):
                        ins = mm(P[s][2][:, 256 * t:256 * t + 256], xT[s][:, 128 * t:128 * t + 128], W("l0_w", 128, 384))
                    ins.then_inc(l0_qkv[s], 1)

                def l0_state(s):
                    pe.wait_ge(l0_qk[s], l0_qk.at(c))
                    pe.wait_ge(l0_v_in[s], l0_v_in.at(c))
                    pe.wait_ge(l0_ones[s], l0_ones.at(c))
                    for t in range(2):
                        ins = mm(P[s][3][:, 0:129], l0_r[s][:, 1, 128 * t:128 * t + 128], l0_v[s][:, t, 0:129], t == 0, t == 1)
                    ins.then_inc(l0_kv[s], 1)

                def l0_read(s):
                    pe.wait_ge(l0_kvs_in[s], l0_kvs_in.at(c))
                    for t in range(2):
                        ins = mm(P[s][1][:, 129 * t:129 * t + 129], l0_r[s][:, 0, 128 * t:128 * t + 128], l0_kvs[s][:, 0:129])
                    ins.then_inc(l0_out[s], 1)

                def l1(s):
                    w1 = region_a[:, 0:E0 * F0].rearrange("p (e f) -> p e f", e=E0)
                    w2 = region_a[:, E0 * F0:N_L1W].rearrange("p (e f d) -> p e f d", e=E0, f=4)
                    for t in range(2):
                        ins = mm(P[s][3][:, 8 * t:8 * t + 8], xT[s][:, 128 * t:128 * t + 128], W("l1_gate"))
                    ins.then_inc(l1_lg[s], 1)
                    pe.wait_ge(s_wa, n_wa * c + 16)

                    def up(n):
                        e, p = divmod(n, 2)
                        if n >= 3:
                            m = n - 3
                            reader = l1_hd if m % 2 else l1_ha
                            pe.wait_ge(reader[s], reader.at(c, m // 2))
                        for f in range(2):
                            ins = mm(P[s][n % 3][:, 256 * f:256 * f + 256],
                                     w1[:, e, 128 * (2 * p + f):128 * (2 * p + f) + 128], xT[s][:, :])
                        ins.then_inc(l1_z[s], 1)

                    def down(e):
                        pe.wait_ge(l1_ha[s], l1_ha.at(c, e))
                        pe.wait_ge(l1_hd[s], l1_hd.at(c, e))
                        if e == 0:
                            pe.wait_ge(l1_mask[s], l1_mask.at(c))
                        else:
                            pe.wait_ge(l1_acc[s], l1_acc.at(c, e - 1))
                        for t in range(2):
                            for f in range(4):
                                ins = mm(P[s][3][:, 128 * t:128 * t + 128],
                                         ex_h[s][:, e % 2, f, 128 * t:128 * t + 128], w2[:, e, f, :], f == 0, f == 3)
                        ins.then_inc(l1_y[s], 1)

                    up(0)
                    up(1)
                    for e in range(E0):
                        if e + 1 < E0:
                            up(2 * e + 2)
                            up(2 * e + 3)
                        down(e)
                    for t in range(2):
                        ins = pe.transpose(P[s][0][0:8, 128 * t:128 * t + 128], ex_mk[s][:, t, :], ident)
                    ins.then_inc(l1_mTp[s], 1)
                    pe.wait_ge(l1_mT[s], l1_mT.at(c))
                    pe.wait_ge(l1_acc[s], l1_acc.at(c, E0 - 1))
                    for t in range(2):
                        ins = mm(P[s][3][:, 128 * t:128 * t + 128], ex_mT[s][0:8, 128 * t:128 * t + 128], W("l1_b2", rows=8))
                    ins.then_inc(l1_y[s], 1)

                def l2_down(s):
                    mm(P[s][1][:, 0:256], W("l2_down"), xT[s][:, :]).then_inc(l2_ct[s], 1)
                    mm(P[s][2][:, 0:256], W("l2_kr"), xT[s][:, :])
                    mm(P[s][2][:, 256:512], W("l2_krs"), xT[s][:, :]).then_inc(l2_kp[s], 1)

                def l2_up(s):
                    pe.wait_ge(l2_cts[s], l2_cts.at(c))
                    mm(P[s][3][:, 0:256], W("l2_qr"), at_ct[s])
                    mm(P[s][3][:, 256:512], W("l2_qrs"), at_ct[s])
                    mm(P[s][0][:, 0:256], W("l2_qc"), at_ct[s])
                    mm(P[s][0][:, 256:512], W("l2_kc"), at_ct[s]).then_inc(l2_qp[s], 1)
                    for t in range(2):
                        ins = mm(P[s][1][:, 128 * t:128 * t + 128], at_ct[s][:, 128 * t:128 * t + 128], W("l2_v"))
                    ins.then_inc(l2_v[s], 1)

                def stack(s, full):
                    for w, (hi, lo, names) in enumerate(((0, 1, ("sel_kh", "sel_kl")), (2, 3, ("sel_qh", "sel_ql")))):
                        for b in range(2):
                            bank = P[s][2 * w + b]
                            for j in (2 * b, 2 * b + 1):
                                o = bank[:, 256 * (j % 2):256 * (j % 2) + 256]
                                mm(o, CR(names[0], j), parts[s][:, hi, :], True, False)
                                ins = mm(o, CR(names[1], j), parts[s][:, lo, :], False, True)
                            ins.then_inc(full[s], 1)

                def l2_scores(s, i):
                    pe.wait_ge(l2_qm[s], l2_qm.at(c, i))
                    for j in range(4):
                        if i or j > 1:
                            r, k = ((l2_p, 4 * i - 2 + j) if j < 2 else (l2_su, 4 * i + j - 2))
                            pe.wait_ge(r[s], r.at(c, k))
                        for t in range(2):
                            ins = mm(P[s][(9 * i + j) % 2][:, 256 * t:256 * t + 256],
                                     qm[s][:, i % 2, j, 128 * t:128 * t + 128], kst[s][:, j, :])
                        ins.then_inc(l2_s[s], 1)

                def l2_max(s, i):
                    pe.wait_ge(l2_mtok[s], l2_mtok.at(c, i))
                    for t in range(2):
                        ins = pe.transpose(P[s][(9 * i + 4) % 2][0:4, 128 * t:128 * t + 128], m_tok[s][:, t, :], ident)
                    ins.then_inc(l2_m[s], 1)

                def l2_shifted(s, i):
                    for j in range(4):
                        if j == 0:
                            pe.wait_ge(l2_su[s], l2_su.at(c, 4 * i + 3))
                        if j == 1:
                            pe.wait_ge(l2_mu[s], l2_mu.at(c, i))
                        if j > 1:
                            pe.wait_ge(l2_p[s], l2_p.at(c, 4 * i + j - 2))
                        if j == 0:
                            pe.wait_ge(l2_mu[s], l2_mu.at(c, i))
                        for t in range(2):
                            o = P[s][(9 * i + 5 + j) % 2][:, 256 * t:256 * t + 256]
                            mm(o, kst[s][:, j, 128 * t:128 * t + 128], qm[s][:, i % 2, j, :], True, False)
                            ins = mm(o, CR("sel_max", j), mT[s], False, True)
                        ins.then_inc(l2_st[s], 1)

                def l2_values(s, i):
                    pe.wait_ge(l2_p[s], l2_p.at(c, 4 * i + 3))
                    o = P[s][2 + i // 2][:, 256 * (i % 2):256 * (i % 2) + 256]
                    for t in range(2):
                        for j in range(4):
                            ins = mm(o[32 * j:32 * j + 32, :], at_v[s][:, t, 4 * j + i, :],
                                     at_p[s][:, j, 256 * t:256 * t + 256], t == 0, t == 1)
                    ins.then_inc(l2_pv[s], 1)

                def l2_sums(s):
                    pe.wait_ge(l2_ob[s], l2_ob.at(c))
                    for b in range(2):
                        ins = mm(P[s][b][:, :], C("rows8"), at_o[s][:, 2 * b:2 * b + 2, :])
                    ins.then_inc(l2_bc[s], 1)

                def l2_out(s):
                    pe.wait_ge(l2_on[s], l2_on.at(c))
                    for t in range(2):
                        for i in range(4):
                            ins = mm(P[s][2][:, 128 * t:128 * t + 128], at_o[s][:, i, 128 * t:128 * t + 128],
                                     W("l2_o", 128 * i, 128 * i + 128), i == 0, i == 3)
                    ins.then_inc(l2_y[s], 1)

                def l3_project(s, L):
                    w = region_b[:, L * N_L3W:(L + 1) * N_L3W]
                    pe.wait_ge(s_wb, n_wb * c + 16)
                    for n, (t, k) in enumerate(((0, 0), (0, 1), (1, 0), (1, 1), (0, 2), (1, 2))):
                        if n > 3:
                            pe.wait_ge(l3_qnd[s], l3_qnd.at(c, 4 * L + n - 4))
                        mm(P[s][n % 4][:, :], shT[s][:, 128 * t:128 * t + 128], w[:, 512 * k:512 * k + 512]
                           ).then_inc(l3_qkv[s], 1)

                def l3_pair(s, L, p):
                    if p == 0:
                        pe.wait_ge(l3_rot[s], l3_rot.at(c, 4 * L + 3))
                        pe.wait_ge(l3_vin[s], l3_vin.at(c, 2 * L + 1))
                    else:
                        pe.wait_ge(l3_pte[s], l3_pte.at(c, 8 * L + 2 * p - 2))
                    for k in range(2):
                        for t in range(2):
                            ins = pe.transpose(P[s][0][:, 256 * k + 128 * t:256 * k + 128 * t + 128],
                                               l3_tok[s][:, k, t, 128 * p:128 * p + 128], ident)
                    ins.then_inc(l3_tp[s], 1)

                def l3_scores(s, L, h):
                    pe.wait_ge(l3_te[s], l3_te.at(c, 4 * L + h // 2))
                    if h > 1:
                        pe.wait_ge(l3_smd[s], l3_smd.at(c, 8 * L + h - 2))
                    q, o = qTm[s][:, h % 2, :], P[s][1 + h % 2]
                    mm(o[:, 0:128], q[:, 0:128], l3_kT[s][:, 0:128])
                    mm(o[:, 128:384], q[:, 128:256], l3_kT[s]).then_inc(l3_s[s], 1)

                def l3_turn(s, L, h):
                    pe.wait_ge(l3_pn[s], l3_pn.at(c, 8 * L + h))
                    if h:
                        pe.wait_ge(l3_pte[s], l3_pte.at(c, 8 * L + h - 1))
                    pe.wait_ge(l3_te[s], l3_te.at(c, 4 * L + min(h + 1, 7) // 2))
                    for b in range(3):
                        ins = pe.transpose(P[s][0][:, 128 * b:128 * b + 128], l3_sm[s][:, h % 2, 128 * b:128 * b + 128], ident)
                    ins.then_inc(l3_pt[s], 1)

                def l3_values(s, L, h):
                    pe.wait_ge(l3_pte[s], l3_pte.at(c, 8 * L + h))
                    if h % 2 == 0 and h:
                        pe.wait_ge(l3_ot[s], l3_ot.at(c, 4 * L + h // 2 - 1))
                    o, pT = P[s][3][64 * (h % 2):64 * (h % 2) + 64, :], l3_pT[s][:, h % 2, :]
                    mm(o[:, 0:256], l3_v[s][:, 0, 64 * h:64 * h + 64], pT[:, 0:256], True, False)
                    ins = mm(o[:, 128:256], l3_v[s][:, 1, 64 * h:64 * h + 64], pT[:, 256:384], False, True)
                    if h % 2:
                        ins.then_inc(l3_o[s], 1)

                def l3_out(s, L):
                    at, _ = L3W["o"]
                    w = region_b[:, L * N_L3W + at:L * N_L3W + at + 512].rearrange("p (j d) -> p j d", j=4)
                    pe.wait_ge(l3_ot[s], l3_ot.at(c, 4 * L + 3))
                    for t in range(2):
                        for p in range(4):
                            ins = mm(P[s][2][:, 128 * t:128 * t + 128], l3_oT[s][:, p, 128 * t:128 * t + 128], w[:, p, :], p == 0, p == 3)
                    ins.then_inc(l3_y[s], 1)

                def l3_back(s, L):
                    for t in range(2):
                        ins = pe.transpose(P[s][1][:, 128 * t:128 * t + 128], shT[s][:, 128 * t:128 * t + 128], ident)
                    ins.then_inc(l3_hs[s], 1)

                def l3_normed(s, L):
                    pe.wait_ge(l3_hnd[s], l3_hnd.at(c, L))
                    for t in range(2):
                        ins = pe.transpose(P[s][2][:, 128 * t:128 * t + 128], l3_hn[s][:, t, :], ident)
                    ins.then_inc(l3_hnp[s], 1)

                def l3_ffn(s, L):
                    at, _ = L3W["w1"]
                    w = region_b[:, L * N_L3W + at:L * N_L3W + at + 2 * HID]
                    pe.wait_ge(l3_hnTd[s], l3_hnTd.at(c, L))
                    for f, (b, M) in enumerate(zip((0, 1, 3), FT)):
                        for k in range(2):
                            ins = mm(P[s][b][0:M, 256 * k:256 * k + 256], w[:, HID * k + 128 * f:HID * k + 128 * f + M], l3_hnT[s])
                        ins.then_inc(l3_z[s], 1)

                def l3_ffn_out(s, L):
                    at, _ = L3W["w2"]
                    w = region_b[:, L * N_L3W + at:L * N_L3W + at + 384].rearrange("p (j d) -> p j d", j=3)
                    pe.wait_ge(l3_h[s], l3_h.at(c, 3 * L + 2))
                    for t in range(2):
                        for f, M in enumerate(FT):
                            ins = mm(P[s][2][:, 128 * t:128 * t + 128], l3_hh[s][0:M, f, 128 * t:128 * t + 128], w[0:M, f, :], f == 0, f == 2)
                    ins.then_inc(l3_y2[s], 1)

                def l4_project(s):
                    mm(P[s][1][:, 0:256], W("l4_w", 128, 256), xT[s][:, :])
                    mm(P[s][1][:, 256:512], W("l4_w", 0, 128), xT[s][:, :])
                    for t in range(2):
                        ins = mm(P[s][2][:, 128 * t:128 * t + 128], xT[s][:, 128 * t:128 * t + 128], W("l4_w", 256, 384))
                    ins.then_inc(l4_p[s], 1)

                def l4_scores(s, i, j):
                    n = 4 * i + j
                    pe.wait_ge(l4_qm[s], l4_qm.at(c, i))
                    if n > 1:
                        pe.wait_ge(l4_sq[s], l4_sq.at(c, n - 2))
                    for t in range(2):
                        ins = mm(P[s][n % 2][:, 256 * t:256 * t + 256], kst[s][:, j, 128 * t:128 * t + 128], qm[s][:, i, j, :])
                    ins.then_inc(l4_st[s], 1)

                def l4_values(s, i):
                    pe.wait_ge(l4_sq[s], l4_sq.at(c, 4 * i + 3))
                    for t in range(2):
                        for j in range(4):
                            ins = mm(P[s][2][32 * j:32 * j + 32, 256 * i:256 * i + 256], l4_v[s][:, t, 2 * j + i, :],
                                     at_p[s][:, j, 256 * t:256 * t + 256], t == 0, t == 1)
                    ins.then_inc(l4_pv[s], 1)

                def l4_halves(s):
                    for i in range(2):
                        for j in range(4):
                            for t in range(2):
                                ins = mm(P[s][3][32 * j:32 * j + 32, i:i + 1], l4_v[s][:, t, 2 * j + i, :], C("half"), t == 0, t == 1)
                    ins.then_inc(l4_hs[s], 1)

                def l4_sums(s):
                    pe.wait_ge(l4_oin[s], l4_oin.at(c))
                    mm(P[s][0][:, :], C("rows16"), at_o[s][:, 0:2, :]).then_inc(l4_bc[s], 1)

                def l4_out(s):
                    pe.wait_ge(l4_on[s], l4_on.at(c))
                    for t in range(2):
                        for i in range(2):
                            ins = mm(P[s][3][:, 128 * t:128 * t + 128], at_o[s][:, i, 128 * t:128 * t + 128],
                                     W("l4_o", 128 * i, 128 * i + 128), i == 0, i == 1)
                    ins.then_inc(l4_y[s], 1)

                def L5(name, *dims):
                    at, n = L5W[name]
                    return region_a[:, at:at + n]

                def l5_gates(s):
                    pe.wait_ge(s_wa, n_wa * c + 32)
                    for f in range(4):
                        if f == 3:
                            pe.wait_ge(l5_h0[s], l5_h0.at(c, 0))
                        for k, w in enumerate(("w1", "w2")):
                            ins = mm(P[s][f % 3][:, 256 * k:256 * k + 256], L5(w)[:, 128 * f:128 * f + 128], xT[s][:, :])
                        ins.then_inc(l5_z[s], 1)

                def l5_hidden(s, w, src, n0, ready, last):
                    m = L5(w).rearrange("p (k o) -> p k o", k=4)
                    pe.wait_ge(ready[s], ready.at(c, ready.per_turn - 1))
                    for p in range(2):
                        n = n0 + p
                        if n > 5:
                            pe.wait_ge(last[s], last.at(c, n - 7))
                        for f in range(2):
                            for k in range(4):
                                ins = mm(P[s][n % 3][:, 256 * f:256 * f + 256],
                                         m[:, k, 128 * (2 * p + f):128 * (2 * p + f) + 128], src[s][:, k, :], k == 0, k == 3)
                        ins.then_inc(l5_z[s], 1)

                def l5_out(s):
                    m = L5("w3").rearrange("p (k o) -> p k o", k=4)
                    pe.wait_ge(l5_h2[s], l5_h2.at(c, 1))
                    for t in range(2):
                        for k in range(4):
                            ins = mm(P[s][3][:, 128 * t:128 * t + 128], l5_hC[s][:, k, 128 * t:128 * t + 128], m[:, k, :], k == 0, k == 3)
                    ins.then_inc(l5_yd[s], 1)

                def l6_project(s):
                    mm(P[s][0][:, 0:256], W("l6_q"), xT[s][:, :])
                    mm(P[s][0][:, 256:512], W("l6_k"), xT[s][:, :]).then_inc(l6_qk[s], 1)
                    l6_project_v(s, range(3))

                def l6_project_v(s, steps):
                    for n in steps:
                        t, k = divmod(n, 2)
                        if n == 3:
                            pe.wait_ge(l6_csd[s], l6_csd.at(c))
                        mm(P[s][(n + 1) % 4][:, :], xT[s][:, 128 * t:128 * t + 128], W("l6_v", 512 * k, 512 * k + 512)
                           ).then_inc(l6_vp[s], 1)

                def l6_denominator(s):
                    pe.wait_ge(l6_pr[s], l6_pr.at(c))
                    pe.wait_ge(l6_va[s], l6_va.at(c, 0))
                    mm(P[s][1][:, 0:256], C("pair_sum"), l6_prod[s]).then_inc(l6_dn[s], 1)

                def l6_scores(s, h):
                    if h == 0:
                        pe.wait_ge(l6_vd[s], l6_vd.at(c, 1))
                        pe.wait_ge(l6_va[s], l6_va.at(c, 1))
                    pe.wait_ge(l6_qm[s], l6_qm.at(c, h))
                    if h > 1:
                        pe.wait_ge(l6_atd[s], l6_atd.at(c, h - 2))
                    o, q = P[s][h % 2], qm6[s][:, h % 8, :]
                    mm(o[:, 0:256], k6[s][:, 0:128], q)
                    mm(o[:, 256:384], k6[s][:, 128:256], q[:, 128:256]).then_inc(l6_a[s], 1)

                def l6_values(s, h):
                    p = h // 2
                    pe.wait_ge(l6_atd[s], l6_atd.at(c, h))
                    if p > 1 and h % 2 == 0:
                        pe.wait_ge(l6_ot[s], l6_ot.at(c, p - 2))
                    o, a = P[s][2 + p % 2][64 * (h % 2):64 * (h % 2) + 64, :], l6_at[s][:, h % 4, :]
                    mm(o[:, 0:256], l6_v[s][:, 0, 64 * h:64 * h + 64], a[:, 0:256], True, False)
                    mm(o[:, 128:256], l6_v[s][:, 1, 64 * h:64 * h + 64], a[:, 256:384], False, True).then_inc(l6_o[s], 1)

                def l6_out(s):
                    pe.wait_ge(l6_ot[s], l6_ot.at(c, 7))
                    for t in range(2):
                        for p in range(8):
                            ins = mm(P[s][0][:, 128 * t:128 * t + 128], l6_oT[s][:, p, 128 * t:128 * t + 128],
                                     W("l6_o", 128 * p, 128 * p + 128), p == 0, p == 7)
                    ins.then_inc(l6_yd[s], 1)

                def l7(s):
                    n_e = 2 * I3 + 2 * D
                    for t in range(2):
                        ins = mm(P[s][3][:, 8 * t:8 * t + 8], xT[s][:, 128 * t:128 * t + 128], W("l7_gate"))
                    ins.then_inc(l7_lg[s], 1)
                    pe.wait_ge(s_wb, n_wb * c + 32)

                    def up(n):
                        e, f = divmod(n, 2)
                        if n >= 3:
                            pe.wait_ge(l7_h[s], l7_h.at(c, n - 3))
                        for k in range(2):
                            ins = mm(P[s][n % 3][:, 256 * k:256 * k + 256],
                                     region_b[:, e * n_e + I3 * k + 128 * f:e * n_e + I3 * k + 128 * f + 128], xT[s][:, :])
                        ins.then_inc(l7_z[s], 1)

                    def down(e):
                        pe.wait_ge(l7_h[s], l7_h.at(c, 2 * e + 1))
                        if e == 0:
                            pe.wait_ge(l7_lgb[s], l7_lgb.at(c))
                        else:
                            pe.wait_ge(l7_acc[s], l7_acc.at(c, e - 1))
                        for t in range(2):
                            for f in range(2):
                                ins = mm(P[s][3][:, 128 * t:128 * t + 128], ex_h[s][:, e % 2, f, 128 * t:128 * t + 128],
                                         region_b[:, e * n_e + 2 * I3 + D * f:e * n_e + 2 * I3 + D * f + D], f == 0, f == 1)
                        ins.then_inc(l7_y[s], 1)

                    up(0)
                    up(1)
                    for e in range(E3):
                        if e + 1 < E3:
                            up(2 * e + 2)
                            up(2 * e + 3)
                        down(e)

                for s in S2:
                    transpose_x(s, 0)
                    l0_project(s)
                for s in S2:
                    l0_state(s)
                for s in S2:
                    l0_read(s)
                if PHASES > 1:
                    for s in S2:
                        transpose_x(s, 1)
                        l1(s)
                if PHASES > 2:
                    for s in S2:
                        transpose_x(s, 2)
                        l2_down(s)
                    for s in S2:
                        l2_up(s)
                    for s in S2:
                        pe.wait_ge(l2_split[s], l2_split.at(c))
                        pe.wait_ge(l2_vs[s], l2_vs.at(c))
                        stack(s, st_full)
                    for s in S2:
                        pe.wait_ge(st_in[s], st_in.at(c, 3))
                    for i in range(4):
                        for s in S2:
                            l2_scores(s, i)
                        for s in S2:
                            l2_max(s, i)
                        for s in S2:
                            l2_shifted(s, i)
                        for s in S2:
                            l2_values(s, i)
                    for s in S2:
                        l2_sums(s)
                    for s in S2:
                        l2_out(s)
                if PHASES > 3:
                    for L in range(2):
                        for s in S2:
                            transpose_x(s, 3 + 2 * L)
                            l3_project(s, L)
                        for h in range(LH + 1):
                            if h < LH:
                                for s in S2:
                                    if h % 2 == 0:
                                        l3_pair(s, L, h // 2)
                                    l3_scores(s, L, h)
                            if h:
                                for s in S2:
                                    l3_turn(s, L, h - 1)
                                for s in S2:
                                    l3_values(s, L, h - 1)
                        for s in S2:
                            l3_out(s, L)
                        for s in S2:
                            transpose_x(s, 4 + 2 * L)
                            l3_back(s, L)
                        for s in S2:
                            l3_normed(s, L)
                        for s in S2:
                            l3_ffn(s, L)
                        for s in S2:
                            l3_ffn_out(s, L)
                if PHASES > 4:
                    for s in S2:
                        transpose_x(s, 7, l4_xn, l4_xnd)
                        l4_project(s)
                    for s in S2:
                        pe.wait_ge(l4_split[s], l4_split.at(c))
                        pe.wait_ge(l4_vd[s], l4_vd.at(c))
                        stack(s, l4_stf)
                    for s in S2:
                        pe.wait_ge(l4_stin[s], l4_stin.at(c, 3))
                        l4_halves(s)
                    for i in range(2):
                        for j in range(4):
                            for s in S2:
                                l4_scores(s, i, j)
                        for s in S2:
                            l4_values(s, i)
                    for s in S2:
                        l4_sums(s)
                    for s in S2:
                        l4_out(s)
                if PHASES > 5:
                    for s in S2:
                        transpose_x(s, 8)
                        l5_gates(s)
                    for s in S2:
                        l5_hidden(s, "h1", l5_hA, 4, l5_h0, None)
                    for s in S2:
                        l5_hidden(s, "h2", l5_hB, 6, l5_h1, l5_h1)
                    for s in S2:
                        l5_out(s)
                if PHASES > 6:
                    for s in S2:
                        transpose_x(s, 9)
                        l6_project(s)
                    for s in S2:
                        l6_project_v(s, (3,))
                    for s in S2:
                        l6_denominator(s)
                    for h in range(H3 + 2):
                        for s in S2:
                            if h > 1:
                                l6_values(s, h - 2)
                            if h < H3:
                                l6_scores(s, h)
                    for s in S2:
                        l6_out(s)
                if PHASES > 7:
                    for s in S2:
                        transpose_x(s, 10)
                        l7(s)

        @block.scalar
        def _(act):
            act.wait_ge(s_const, 16)
            act.wait_ge(s_small, 16)
            with act.Fori(0, TURNS) as c:
                link = Links("act", act, c)

                def keep_xT(s, k):
                    act.wait_ge(xTp[s], xTp.at(c, k))
                    nc.scalar.copy(xT[s][:, :], P[s][0][:, 0:256]).then_inc(xT_ready[s], 1)

                def l0_exps(s):
                    act.wait_ge(l0_qkv[s], l0_qkv.at(c))
                    nc.scalar.activation(l0_e[s][:, 0, :], P[s][1][:, 0:256], ACT.Exp)
                    kv = P[s][2][:, :].rearrange("p (t w d) -> p t w d", t=2, w=2)
                    nc.scalar.activation(l0_e[s][:, 1, :].rearrange("p (t d) -> p t d", t=2), kv[:, :, 0, :], ACT.Exp)
                    nc.scalar.copy(l0_v[s][:, :, 0:128], kv[:, :, 1, :]).then_inc(l0_v_in[s], 1)

                def l1_relu(s):
                    for e in range(E0):
                        act.wait_ge(l1_z[s], l1_z.at(c, 2 * e))
                        if e >= 2:
                            act.wait_ge(l1_y[s], l1_y.at(c, e - 2))
                        for f in range(2):
                            ins = nc.scalar.activation(ex_h[s][:, e % 2, f, :], P[s][2 * e % 3][:, 256 * f:256 * f + 256],
                                                       ACT.Relu, bias=W("l1_b1", 4 * e + f, 4 * e + f + 1))
                        ins.then_inc(l1_ha[s], 1)
                    act.wait_ge(l1_mTp[s], l1_mTp.at(c))
                    nc.scalar.copy(ex_mT[s][0:8, :], P[s][0][0:8, 0:256]).then_inc(l1_mT[s], 1)

                def l2_latent(s):
                    act.wait_ge(l2_ct[s], l2_ct.at(c))
                    nc.scalar.activation(at_ct[s], P[s][1][:, 0:256], ACT.Identity, bias=W("l2_down_b")
                                         ).then_inc(l2_cts[s], 1)

                def keep_stacks(s):
                    for n in range(4):
                        act.wait_ge(st_full[s], st_full.at(c, n))
                        dst = (kst if n < 2 else qst)[s]
                        nc.scalar.copy(dst[:, 2 * (n % 2):2 * (n % 2) + 2, :],
                                       P[s][n][:, :].rearrange("p (j n) -> p j n", j=2)).then_inc(st_in[s], 1)

                def l2_exps(s, i):
                    for j in range(4):
                        act.wait_ge(l2_st[s], l2_st.at(c, 4 * i + j))
                        if i and j == 0:
                            act.wait_ge(l2_pv[s], l2_pv.at(c, i - 1))
                        nc.scalar.activation(at_p[s][:, j, :], P[s][(9 * i + 5 + j) % 2][:, :], ACT.Exp,
                                             scale=1.0 / 12.0).then_inc(l2_p[s], 1)

                def l2_keep_o(s):
                    act.wait_ge(l2_pv[s], l2_pv.at(c, 3))
                    for b in range(2):
                        ins = nc.scalar.copy(at_o[s][:, 2 * b:2 * b + 2, :],
                                             P[s][2 + b][:, :].rearrange("p (i n) -> p i n", i=2))
                    ins.then_inc(l2_ob[s], 1)

                def keep_shifted(s, k):
                    act.wait_ge(xTp[s], xTp.at(c, k))
                    nc.scalar.copy(shT[s][0:64, :], P[s][0][0:64, 0:256])
                    nc.scalar.copy(shT[s][64:128, 1:256], P[s][0][64:128, 0:255]).then_inc(xT_ready[s], 1)

                def l3_square(s, L, i):
                    act.wait_ge(l3_qkv[s], l3_qkv.at(c, 6 * L + i))
                    if i > 1:
                        act.wait_ge(l3_ss[s], l3_ss.at(c, 4 * L + i - 2))
                    nc.scalar.activation(l3_sq[s][:, i % 2, :], P[s][i][:, :], ACT.Square).then_inc(l3_sqd[s], 1)

                def l3_keep_v(s, L):
                    for t in range(2):
                        act.wait_ge(l3_qkv[s], l3_qkv.at(c, 6 * L + 4 + t))
                        nc.scalar.copy(l3_v[s][:, t, :], P[s][t][:, :]).then_inc(l3_vin[s], 1)

                def l3_keep_pair(s, L, p):
                    act.wait_ge(l3_tp[s], l3_tp.at(c, 4 * L + p))
                    nc.scalar.copy(qTm[s][0:64, 0, :], P[s][0][0:64, 0:256])
                    nc.scalar.copy(qTm[s][64:128, 1, :], P[s][0][64:128, 0:256])
                    nc.scalar.copy(l3_kT[s], P[s][0][:, 256:512]).then_inc(l3_te[s], 1)

                def l3_exp(s, L, h):
                    act.wait_ge(l3_smd[s], l3_smd.at(c, 8 * L + h))
                    a = 96 + 8 * (h % 2)
                    for t, (lo, hi) in enumerate(((0, 128), (128, 384))):
                        b = l3_sm[s][:, h % 2, lo:hi]
                        ins = nc.scalar.activation(b, b, ACT.Exp, scale=8.0, bias=tiny[s][:, a + 2 + t:a + 3 + t],
                                                   accum_out=tiny[s][:, a + 4 + t:a + 5 + t])
                    ins.then_inc(l3_e[s], 1)

                def l3_keep_pT(s, L, h):
                    act.wait_ge(l3_pt[s], l3_pt.at(c, 8 * L + h))
                    nc.scalar.copy(l3_pT[s][:, h % 2, :], P[s][0][:, 0:384]).then_inc(l3_pte[s], 1)

                def l3_affine(s, L):
                    act.wait_ge(l3_hnp[s], l3_hnp.at(c, L))
                    nc.scalar.activation(l3_hnT[s], P[s][2][:, 0:256], ACT.Identity, scale=W("l3_g", L, L + 1),
                                         bias=W("l3_b", L, L + 1)).then_inc(l3_hnTd[s], 1)

                def l3_gelu(s, L):
                    for f, (b, M) in enumerate(zip((0, 1, 3), FT)):
                        act.wait_ge(l3_z[s], l3_z.at(c, 3 * L + f))
                        k = 6 * L + 3 + f
                        nc.scalar.activation(l3_gl[s][0:M, f, :], P[s][b][0:M, 256:512], ACT.Gelu,
                                             bias=W("l3_b1", k, k + 1, rows=M)).then_inc(l3_gld[s], 1)

                def l4_keep_xT(s):
                    act.wait_ge(xTp[s], xTp.at(c, 7))
                    nc.scalar.mul(xT[s][:, :], P[s][0][:, 0:256], W("l4_gamma")).then_inc(xT_ready[s], 1)

                def l4_keep_stacks(s):
                    for n in range(4):
                        act.wait_ge(l4_stf[s], l4_stf.at(c, n))
                        dst = (kst if n < 2 else qst)[s]
                        nc.scalar.copy(dst[:, 2 * (n % 2):2 * (n % 2) + 2, :],
                                       P[s][n][:, :].rearrange("p (j n) -> p j n", j=2)).then_inc(l4_stin[s], 1)

                def l4_square(s, i, j):
                    n = 4 * i + j
                    act.wait_ge(l4_st[s], l4_st.at(c, n))
                    if i and j == 0:
                        act.wait_ge(l4_pv[s], l4_pv.at(c, i - 1))
                    nc.scalar.activation(at_p[s][:, j, :], P[s][n % 2][:, :], ACT.Square, scale=0.25 * 0.5 ** 0.5,
                                         bias=C("root_half")).then_inc(l4_sq[s], 1)

                def l4_keep_o(s):
                    act.wait_ge(l4_pv[s], l4_pv.at(c, 1))
                    act.wait_ge(l4_hsd[s], l4_hsd.at(c))
                    for i in range(2):
                        ins = nc.scalar.activation(at_o[s][:, i, :], P[s][2][:, 256 * i:256 * i + 256], ACT.Identity,
                                                   bias=tiny[s][:, 112 + i:113 + i])
                    ins.then_inc(l4_oin[s], 1)

                def l5_silu(s):
                    for f in range(4):
                        act.wait_ge(l5_z[s], l5_z.at(c, f))
                        if f > 1:
                            act.wait_ge(l5_h0[s], l5_h0.at(c, f - 2))
                        nc.scalar.activation(ex_g[s][:, f % 2, :], P[s][f % 3][:, 0:256], ACT.Silu,
                                             scale=W("l5_s1", f, f + 1)).then_inc(l5_sg[s], 1)

                def l5_gelu(s, n0, dst, scale, done):
                    for p in range(2):
                        act.wait_ge(l5_z[s], l5_z.at(c, n0 + p))
                        for f in range(2):
                            k = 2 * p + f
                            ins = nc.scalar.activation(dst[s][:, k, :], P[s][(n0 + p) % 3][:, 256 * f:256 * f + 256],
                                                       ACT.Gelu, scale=W(scale, k, k + 1))
                        ins.then_inc(done[s], 1)

                def l6_angles(s, step):
                    if step == 0:
                        act.wait_ge(l6_qk[s], l6_qk.at(c))
                        link(nc.scalar.activation(l6_th[s], P[s][0][:, :].rearrange("p (w n) -> p w n", w=2), ACT.Tanh))
                    else:
                        nc.scalar.activation(l6_cs[s], l6_th[s], ACT.Sin, scale=float(np.pi / 4),
                                             bias=C("half_pi")).then_inc(l6_csd[s], 1)

                def l6_keep_v(s):
                    for n in (0, 2):
                        act.wait_ge(l6_vp[s], l6_vp.at(c, n))
                        nc.scalar.copy(l6_v[s][:, n // 2, 0:512], P[s][n + 1][:, :]).then_inc(l6_va[s], 1)

                def l6_keep_o(s, p):
                    act.wait_ge(l6_o[s], l6_o.at(c, 2 * p + 1))
                    if p == 0:
                        act.wait_ge(l6_qkd[s], l6_qkd.at(c))
                    nc.scalar.copy(l6_oT[s][:, p, :], P[s][2 + p % 2][:, 0:256]).then_inc(l6_ot[s], 1)

                def l7_sigmoid(s):
                    act.wait_ge(l7_lgb[s], l7_lgb.at(c))
                    nc.scalar.activation(ex_m2[s], ex_log[s], ACT.Sigmoid).then_inc(l7_pr[s], 1)

                def l7_silu(s):
                    for n in range(18):
                        act.wait_ge(l7_z[s], l7_z.at(c, n))
                        if n > 1:
                            act.wait_ge(l7_h[s], l7_h.at(c, n - 2))
                        nc.scalar.activation(ex_g[s][:, n % 2, :], P[s][n % 3][:, 0:256], ACT.Silu).then_inc(l7_sg[s], 1)

                for s in S2:
                    keep_xT(s, 0)
                    l0_exps(s)
                if PHASES > 1:
                    for s in S2:
                        keep_xT(s, 1)
                        l1_relu(s)
                if PHASES > 2:
                    for s in S2:
                        keep_xT(s, 2)
                        l2_latent(s)
                    for s in S2:
                        keep_stacks(s)
                    for i in range(4):
                        for s in S2:
                            l2_exps(s, i)
                    for s in S2:
                        l2_keep_o(s)
                if PHASES > 3:
                    for L in range(2):
                        for s in S2:
                            keep_shifted(s, 3 + 2 * L)
                            for i in range(4):
                                l3_square(s, L, i)
                        for s in S2:
                            l3_keep_v(s, L)
                        for h in range(LH + 1):
                            if h < LH:
                                for s in S2:
                                    if h % 2 == 0:
                                        l3_keep_pair(s, L, h // 2)
                                for s in S2:
                                    l3_exp(s, L, h)
                            if h:
                                for s in S2:
                                    l3_keep_pT(s, L, h - 1)
                        for s in S2:
                            keep_shifted(s, 4 + 2 * L)
                        for s in S2:
                            l3_affine(s, L)
                        for s in S2:
                            l3_gelu(s, L)
                if PHASES > 4:
                    for s in S2:
                        l4_keep_xT(s)
                    for s in S2:
                        l4_keep_stacks(s)
                    for i in range(2):
                        for j in range(4):
                            for s in S2:
                                l4_square(s, i, j)
                    for s in S2:
                        l4_keep_o(s)
                if PHASES > 5:
                    for s in S2:
                        keep_xT(s, 8)
                        l5_silu(s)
                    for s in S2:
                        l5_gelu(s, 4, l5_hB, "l5_h1s", l5_h1)
                    for s in S2:
                        l5_gelu(s, 6, l5_hC, "l5_h2s", l5_h2)
                if PHASES > 6:
                    for s in S2:
                        keep_xT(s, 9)
                        l6_angles(s, 0)
                    for s in S2:
                        l6_angles(s, 1)
                    for s in S2:
                        l6_keep_v(s)
                    for p in range(8):
                        for s in S2:
                            l6_keep_o(s, p)
                if PHASES > 7:
                    for s in S2:
                        keep_xT(s, 10)
                        l7_sigmoid(s)
                        l7_silu(s)
                link.close()

        @block.vector
        def _(dve):
            v = nc.vector
            dve.wait_ge(s_const, 16)
            dve.wait_ge(s_small, 16)
            dve.wait_ge(s_stage, 16)
            v.tensor_copy(constr[:, :], scr[0][:, 0:N_CONSTR]).then_inc(s_constr, 1)
            for s in S2:
                v.memset(qTm[s][:, :, :], 0.0)
                ins = v.memset(shT[s][64:128, 0:1], 0.0)
            ins.then_inc(s_zd, 1)
            for L in range(2):
                for w in range(2):
                    for k in range(2):
                        at = ((2 * L + w) * 2 + k) * 64
                        v.tensor_tensor(xpos[:, L, w, k, :, :], C("xpos").rearrange("p (w k t d) -> p w k t d", w=2, k=2, t=2)[:, w, k, :, :],
                                        W("l3_scale", at, at + 64).unsqueeze(1).to_broadcast([128, 2, 64]), ALU.mult
                                        ).then_inc(s_xpos, 1)
            dve.wait_ge(s_xpos, 8)
            settled[dve] = sem("dve_settled")
            for s in S2:
                dve.sem_inc(x_ready[s], 1)
            with dve.Fori(0, TURNS) as c:
                link = Links("dve", dve, c)

                def norm(s, n, k):
                    for t in range(2):
                        ins = v.bn_stats(stats[s][:, t, :], res[s][:, t, :])
                    link(ins)
                    settle(dve)
                    for t in range(2):
                        ins = v.bn_aggr(mv[s][:, t, :], stats[s][:, t, :])
                    link(ins)
                    v.tensor_scalar(ve[s][:, :], mv[s][:, :, 1], LN_EPS, None, ALU.add).then_inc(var_ready[s], 1)
                    dve.wait_ge(rstd_ready[s], rstd_ready.at(c, n))
                    for t in range(2):
                        ins = v.tensor_scalar(x[s][:, t, :], res[s][:, t, :], mv[s][:, t, 0:1], rstd[s][:, t:t + 1],
                                              ALU.subtract, ALU.mult)
                    ins.then_inc(x_ready[s], 1)

                def l0_elu(s):
                    dve.wait_ge(l0_v_in[s], l0_v_in.at(c))
                    v.tensor_scalar(l0_r[s][:, 0, :], P[s][1][:, 0:256], 0.0, None, ALU.max)
                    kv = P[s][2][:, :].rearrange("p (t w d) -> p t w d", t=2, w=2)
                    link(v.tensor_scalar(l0_r[s][:, 1, :].rearrange("p (t d) -> p t d", t=2), kv[:, :, 0, :], 0.0, None, ALU.max))
                    v.scalar_tensor_tensor(out=l0_r[s][:, 0:2, :], in0=l0_e[s][:, 0:2, :], scalar=1.0,
                                           in1=l0_r[s][:, 0:2, :], op0=ALU.min, op1=ALU.add).then_inc(l0_qk[s], 1)

                def l0_keep(s):
                    dve.wait_ge(l0_kv[s], l0_kv.at(c))
                    v.tensor_copy(l0_kvs[s][:, 0:129], P[s][3][:, 0:129]).then_inc(l0_kvs_in[s], 1)

                def l0_mix(s):
                    dve.wait_ge(l0_out[s], l0_out.at(c))
                    y = P[s][1][:, 0:258].rearrange("p (t d) -> p t d", t=2)
                    link(v.tensor_scalar(tiny[s][:, 0:2], y[:, :, 128], 1e-6, None, ALU.add))
                    link(v.reciprocal(tiny[s][:, 2:4], tiny[s][:, 0:2]))
                    for t in range(2):
                        ins = v.scalar_tensor_tensor(out=res[s][:, t, :], in0=y[:, t, 0:128], scalar=tiny[s][:, 2 + t:3 + t],
                                                     in1=x[s][:, t, :], op0=ALU.mult, op1=ALU.add)
                    link(ins)

                def l1_route(s):
                    dve.wait_ge(l1_lg[s], l1_lg.at(c))
                    lg = P[s][3][:, 0:16].rearrange("p (t e) -> p t e", t=2)
                    for t in range(2):
                        ins = v.tensor_tensor(ex_m2[s][:, t, :], lg[:, t, :], W("l1_gb"), ALU.add)
                    link(ins)
                    for t in range(2):
                        ins = v.tensor_tensor(ex_log[s][:, t, :], ex_m2[s][:, t, :], W("l1_eb"), ALU.add)
                    link(ins)
                    settle(dve)
                    for t in range(2):
                        ins = v.max(ex_mx[s][:, t, :], ex_log[s][:, t, :])
                    link(ins)
                    settle(dve)
                    for t in range(2):
                        ins = v.max_index(idx[s][:, t, :], ex_mx[s][:, t, :], ex_log[s][:, t, :])
                    link(ins)
                    link(v.tensor_copy(ex_ix[s][:, :, :], idx[s][:, :, :]))
                    for t in range(2):
                        ins = v.tensor_scalar(ex_mk[s][:, t, :], C("iota8"), ex_ix[s][:, t, 0:1], None, ALU.is_equal)
                    ins.then_inc(l1_mask[s], 1)
                    dve.wait_ge(l1_mask[s], l1_mask.at(c))

                def l1_relu(s, e):
                    dve.wait_ge(l1_z[s], l1_z.at(c, 2 * e + 1))
                    if e >= 2:
                        dve.wait_ge(l1_y[s], l1_y.at(c, e - 2))
                    for f in range(2):
                        ins = v.tensor_scalar(ex_h[s][:, e % 2, 2 + f, :], P[s][(2 * e + 1) % 3][:, 256 * f:256 * f + 256],
                                              W("l1_b1", 4 * e + 2 + f, 4 * e + 3 + f), 0.0, ALU.add, ALU.max)
                    ins.then_inc(l1_hd[s], 1)

                def l1_add(s, e):
                    dve.wait_ge(l1_y[s], l1_y.at(c, e))
                    if e:
                        dve.wait_ge(l1_acc[s], l1_acc.at(c, e - 1))
                    for t in range(2):
                        y = P[s][3][:, 128 * t:128 * t + 128]
                        if e < E0:
                            ins = v.scalar_tensor_tensor(out=res[s][:, t, :], in0=y, scalar=ex_mk[s][:, t, e:e + 1],
                                                         in1=(res if e else x)[s][:, t, :], op0=ALU.mult, op1=ALU.add)
                        else:
                            ins = v.tensor_tensor(res[s][:, t, :], y, res[s][:, t, :], ALU.add)
                    ins.then_inc(l1_acc[s], 1)

                def l1(s):
                    l1_route(s)
                    l1_relu(s, 0)
                    for e in range(E0):
                        if e + 1 < E0:
                            l1_relu(s, e + 1)
                        l1_add(s, e)
                    l1_add(s, E0)
                    dve.wait_ge(l1_acc[s], l1_acc.at(c, E0))

                def rope(s, pair, plain, b_r, b_rs, b_c, w, src_ready):
                    t = at_rope[s]
                    v.scalar_tensor_tensor(out=t[:, 3 * w, :], in0=pair[:, 0:256], scalar=W(b_r), in1=C("rope_c"),
                                           op0=ALU.add, op1=ALU.mult)
                    link(v.scalar_tensor_tensor(out=t[:, 3 * w + 1, :], in0=pair[:, 256:512], scalar=W(b_rs), in1=C("rope_s"),
                                                op0=ALU.add, op1=ALU.mult))
                    if src_ready is not None:
                        dve.wait_ge(src_ready[s], src_ready.at(c))
                    link(v.scalar_tensor_tensor(out=t[:, 3 * w + 2, :], in0=plain, scalar=W(b_c), in1=t[:, 3 * w, :],
                                                op0=ALU.add, op1=ALU.add))
                    link(v.tensor_tensor(at_kq[s][:, w, :], t[:, 3 * w + 2, :], t[:, 3 * w + 1, :], ALU.add))

                def split(s, n):
                    for w in range(2):
                        ins = v.tensor_copy(parts[s][:, 2 * w, :], at_kq[s][:, w, :])
                    link(ins)
                    for w in range(2):
                        ins = v.tensor_tensor(parts[s][:, 2 * w + 1, :], at_kq[s][:, w, :], f32(parts[s][:, 2 * w, :]), ALU.subtract)
                    return ins

                def l2_kq(s):
                    dve.wait_ge(l2_kp[s], l2_kp.at(c))
                    rope(s, P[s][2], P[s][0][:, 256:512], "l2_krb", "l2_krsb", "l2_kcb", 0, l2_qp)
                    rope(s, P[s][3], P[s][0][:, 0:256], "l2_qrb", "l2_qrsb", "l2_qcb", 1, None)
                    split(s, 0).then_inc(l2_split[s], 1)

                def l2_vals(s):
                    dve.wait_ge(l2_v[s], l2_v.at(c))
                    dve.wait_ge(l2_xb[s], l2_xb.at(c))
                    for t in range(2):
                        ins = v.tensor_tensor(at_v[s][:, t, :, 0:DH1],
                                              P[s][1][:, 128 * t:128 * t + 128].rearrange("p (h d) -> p h d", h=H1),
                                              W("l2_vb").rearrange("p (h d) -> p h d", h=H1), ALU.add)
                    ins.then_inc(l2_vs[s], 1)

                def l2_maxes(s, i):
                    for j in range(4):
                        dve.wait_ge(l2_s[s], l2_s.at(c, 4 * i + j))
                        if i and j == 0:
                            dve.wait_ge(l2_m[s], l2_m.at(c, i - 1))
                        ins = v.tensor_reduce(m_tok[s][:, :, j], P[s][(9 * i + j) % 2][:, :].rearrange("p (t k) -> p t k", t=2),
                                              X, ALU.max)
                        ins.then_inc(l2_su[s], 1)
                    dve.wait_ge(l2_su[s], l2_su.at(c, 4 * i + 3))
                    v.tensor_copy(tiny[s][:, 8:9], m_tok[s][:, 0, 0:1]).then_inc(l2_mtok[s], 1)

                def l2_max_rows(s, i):
                    dve.wait_ge(l2_m[s], l2_m.at(c, i))
                    if i:
                        dve.wait_ge(l2_st[s], l2_st.at(c, 4 * i - 1))
                    bank = P[s][(9 * i + 4) % 2]
                    link(v.tensor_copy(mT[s][0:4, :], bank[0:4, 0:256]))
                    v.tensor_tensor(mT[s][32:36, :], bank[0:4, 0:256], f32(mT[s][0:4, :]), ALU.subtract).then_inc(l2_mu[s], 1)

                def l2_recip(s):
                    dve.wait_ge(l2_bc[s], l2_bc.at(c))
                    for b in range(2):
                        ins = v.reciprocal(at_r[s][:, 2 * b:2 * b + 2, :], P[s][b][:, :].rearrange("p (i n) -> p i n", i=2))
                    ins.then_inc(l2_rb[s], 1)

                def l2_sum(s):
                    dve.wait_ge(l2_y[s], l2_y.at(c))
                    dve.wait_ge(l2_xb[s], l2_xb.at(c))
                    link(v.tensor_tensor(res[s][:, :, :], P[s][2][:, 0:256].rearrange("p (t d) -> p t d", t=2), at_xb[s], ALU.add))

                def l3_reduce(s, L, i):
                    dve.wait_ge(l3_sqd[s], l3_sqd.at(c, 4 * L + i))
                    v.tensor_reduce(tiny[s][:, 8 * i:8 * i + 8], l3_sq[s][:, i % 2, :].rearrange("p (h d) -> p h d", h=LH),
                                    X, ALU.add).then_inc(l3_ss[s], 1)

                def l3_unit(s, L, i):
                    dve.wait_ge(l3_rn[s], l3_rn.at(c, 4 * L + i))
                    if i > 1:
                        dve.wait_ge(l3_ad[s], l3_ad.at(c, 4 * L + i - 2))
                    rn = tiny[s][:, 32 + 8 * i:40 + 8 * i].unsqueeze(2).to_broadcast([128, LH, LD])
                    v.tensor_tensor(l3_qn[s][:, i % 2, :].rearrange("p (h d) -> p h d", h=LH),
                                    P[s][i][:, :].rearrange("p (h d) -> p h d", h=LH), rn, ALU.mult).then_inc(l3_qnd[s], 1)

                def l3_rotate(s, L, i):
                    t, w = divmod(i, 2)
                    dve.wait_ge(l3_qnd[s], l3_qnd.at(c, 4 * L + i))
                    if i:
                        dve.wait_ge(l3_rot[s], l3_rot.at(c, 4 * L + i - 1))
                    qn = l3_qn[s][:, i % 2, :].rearrange("p (h k d) -> p h k d", h=LH, k=2)
                    b = l3_b[s].rearrange("p (h k d) -> p h k d", h=LH, k=2)
                    for k in range(2):
                        sin = xpos[:, L, w, 1, t, 32 * k:32 * k + 32].unsqueeze(1).to_broadcast([128, LH, 32])
                        ins = v.tensor_tensor(b[:, :, k, :], qn[:, :, 1 - k, :], sin, ALU.mult)
                    link(ins)
                    dve.wait_ge(l3_ad[s], l3_ad.at(c, 4 * L + i))
                    v.tensor_tensor(l3_tok[s][:, w, t, :], l3_a[s], l3_b[s], ALU.add).then_inc(l3_rot[s], 1)

                def l3_mask(s, L, h):
                    dve.wait_ge(l3_s[s], l3_s.at(c, 8 * L + h))
                    if h > 1:
                        dve.wait_ge(l3_pt[s], l3_pt.at(c, 8 * L + h - 2))
                    a = 96 + 8 * (h % 2)
                    settle(dve)
                    for t, (lo, hi) in enumerate(((0, 128), (128, 384))):
                        ins = v.tensor_tensor_reduce(l3_sm[s][:, h % 2, lo:hi], P[s][1 + h % 2][:, lo:hi], C("band", lo, hi),
                                                     1.0, -3.0e38, ALU.add, ALU.max, tiny[s][:, a + t:a + t + 1])
                    link(ins)
                    v.tensor_scalar(tiny[s][:, a + 2:a + 4], tiny[s][:, a:a + 2], -8.0, None, ALU.mult).then_inc(l3_smd[s], 1)

                def l3_recip(s, L, h):
                    dve.wait_ge(l3_e[s], l3_e.at(c, 8 * L + h))
                    if h > 1:
                        dve.wait_ge(l3_pn[s], l3_pn.at(c, 8 * L + h - 2))
                    a = 96 + 8 * (h % 2)
                    v.reciprocal(tiny[s][:, a + 6:a + 8], tiny[s][:, a + 4:a + 6]).then_inc(l3_rs[s], 1)

                def l3_keep_o(s, L, p):
                    dve.wait_ge(l3_o[s], l3_o.at(c, 4 * L + p))
                    v.tensor_copy(l3_oT[s][:, p, :], P[s][3][:, 0:256]).then_inc(l3_ot[s], 1)

                def l3_mid(s, L):
                    dve.wait_ge(l3_y[s], l3_y.at(c, L))
                    if L == 0:
                        v.tensor_copy(res[s][:, :, :], x[s][:, :, :])
                    v.tensor_tensor(x[s][:, :, :], P[s][2][:, 0:256].rearrange("p (t d) -> p t d", t=2), x[s][:, :, :],
                                    ALU.add).then_inc(x_ready[s], 1)

                def l3_norm(s, L):
                    dve.wait_ge(l3_hs[s], l3_hs.at(c, L))
                    for t in range(2):
                        ins = v.bn_stats(stats[s][:, t, :], P[s][1][:, 128 * t:128 * t + 128])
                    link(ins)
                    settle(dve)
                    for t in range(2):
                        ins = v.bn_aggr(mv[s][:, t, :], stats[s][:, t, :])
                    link(ins)
                    v.tensor_scalar(ve[s][:, :], mv[s][:, :, 1], LN_EPS, None, ALU.add).then_inc(var_ready[s], 1)
                    dve.wait_ge(rstd_ready[s], rstd_ready.at(c, 3 + L))
                    for t in range(2):
                        ins = v.tensor_scalar(l3_hn[s][:, t, :], P[s][1][:, 128 * t:128 * t + 128], mv[s][:, t, 0:1],
                                              rstd[s][:, t:t + 1], ALU.subtract, ALU.mult)
                    ins.then_inc(l3_hnd[s], 1)

                def l3_glu(s, L):
                    for f, (b, M) in enumerate(zip((0, 1, 3), FT)):
                        dve.wait_ge(l3_gld[s], l3_gld.at(c, 3 * L + f))
                        k = 6 * L + f
                        v.scalar_tensor_tensor(out=l3_hh[s][0:M, f, :], in0=P[s][b][0:M, 0:256], scalar=W("l3_b1", k, k + 1, rows=M),
                                               in1=l3_gl[s][0:M, f, :], op0=ALU.add, op1=ALU.mult).then_inc(l3_h[s], 1)

                def l3_end(s, L):
                    dve.wait_ge(l3_y2[s], l3_y2.at(c, L))
                    dve.wait_ge(l3_xbd[s], l3_xbd.at(c, L))
                    y = P[s][2][:, 0:256].rearrange("p (t d) -> p t d", t=2)
                    if L == 0:
                        v.tensor_tensor(x[s][:, :, :], y, l3_xb[s], ALU.add).then_inc(x_ready[s], 1)
                    else:
                        link(v.tensor_tensor(res[s][:, :, :], y, l3_xb[s], ALU.add))

                def l4_sumsq(s):
                    dve.wait_ge(x_ready[s], x_ready.at(c, 6))
                    settle(dve)
                    for t in range(2):
                        ins = v.tensor_tensor_reduce(res[s][:, t, :], x[s][:, t, :], x[s][:, t, :], 1.0, 0.0, ALU.mult, ALU.add,
                                                     tiny[s][:, t:t + 1])
                    ins.then_inc(l4_ss[s], 1)

                def l4_normed(s):
                    dve.wait_ge(l4_rn[s], l4_rn.at(c))
                    for t in range(2):
                        ins = v.tensor_scalar(l4_xn[s][:, t, :], x[s][:, t, :], tiny[s][:, 4 + t:5 + t], float(D) ** 0.5,
                                              ALU.mult, ALU.mult)
                    ins.then_inc(l4_xnd[s], 1)

                def l4_parts(s):
                    dve.wait_ge(l4_p[s], l4_p.at(c))
                    for w in range(2):
                        ins = v.tensor_copy(parts[s][:, 2 * w, :], P[s][1][:, 256 * w:256 * w + 256])
                    link(ins)
                    for w in range(2):
                        ins = v.tensor_tensor(parts[s][:, 2 * w + 1, :], P[s][1][:, 256 * w:256 * w + 256],
                                              f32(parts[s][:, 2 * w, :]), ALU.subtract)
                    ins.then_inc(l4_split[s], 1)
                    dve.wait_ge(l4_vset[s], l4_vset.at(c))
                    for t in range(2):
                        ins = v.tensor_copy(l4_v[s][:, t, :, 0:DH2], P[s][2][:, 128 * t:128 * t + 128].rearrange("p (h d) -> p h d", h=H2))
                    ins.then_inc(l4_vd[s], 1)

                def l4_halves(s):
                    dve.wait_ge(l4_hs[s], l4_hs.at(c))
                    v.tensor_copy(tiny[s][:, 112:114], P[s][3][:, 0:2]).then_inc(l4_hsd[s], 1)

                def l4_recip(s):
                    dve.wait_ge(l4_bc[s], l4_bc.at(c))
                    link(v.tensor_scalar(at_r[s][:, 2:4, :], P[s][0][:, :].rearrange("p (i n) -> p i n", i=2), 1e-5, None, ALU.max))
                    v.reciprocal(at_r[s][:, 0:2, :], at_r[s][:, 2:4, :]).then_inc(l4_rb[s], 1)

                def l4_sum(s):
                    dve.wait_ge(l4_y[s], l4_y.at(c))
                    link(v.tensor_tensor(res[s][:, :, :], P[s][3][:, 0:256].rearrange("p (t d) -> p t d", t=2), x[s][:, :, :], ALU.add))

                def l5_gate(s):
                    for f in range(4):
                        dve.wait_ge(l5_sg[s], l5_sg.at(c, f))
                        v.scalar_tensor_tensor(out=l5_hA[s][:, f, :], in0=P[s][f % 3][:, 256:512], scalar=W("l5_s2", f, f + 1),
                                               in1=ex_g[s][:, f % 2, :], op0=ALU.mult, op1=ALU.mult).then_inc(l5_h0[s], 1)

                def l5_sum(s):
                    dve.wait_ge(l5_yd[s], l5_yd.at(c))
                    link(v.tensor_tensor(l5_y[s], P[s][3][:, 0:256].rearrange("p (t d) -> p t d", t=2),
                                         W("l5_s3").unsqueeze(1).to_broadcast([128, 2, 128]), ALU.mult))
                    link(v.tensor_tensor(res[s][:, :, :], l5_y[s], x[s][:, :, :], ALU.add))

                def l6_cumulate(s):
                    dve.wait_ge(l6_csd[s], l6_csd.at(c))
                    link(v.tensor_tensor_scan(l6_cum[s], C("ones"), l6_cs[s][:, 1, :], 0.0, ALU.mult, ALU.add))
                    v.tensor_tensor(l6_prod[s], l6_cum[s], l6_cs[s][:, 0, :], ALU.mult).then_inc(l6_pr[s], 1)

                def l6_keep_v(s):
                    for n in (1, 3):
                        dve.wait_ge(l6_vp[s], l6_vp.at(c, n))
                        v.tensor_copy(l6_v[s][:, n // 2, 512:1024], P[s][(n + 1) % 4][:, :]).then_inc(l6_vd[s], 1)

                def l6_parts(s):
                    v.tensor_copy(k6[s], l6_cs[s][:, 1, :])
                    dve.wait_ge(l6_dn[s], l6_dn.at(c))
                    link(v.tensor_scalar(l6_den[s], P[s][1][:, 0:256], 1e-6, None, ALU.add))
                    link(v.reciprocal(l6_rd[s], l6_den[s]))
                    link(v.tensor_tensor(l6_qn[s], l6_cs[s][:, 0, :], l6_rd[s], ALU.mult))
                    link(v.tensor_copy(q6[s], l6_qn[s]))
                    v.tensor_tensor(k6[s][64:128, :], l6_cs[s][64:128, 1, :], f32(k6[s][64:128, :]), ALU.subtract)
                    for a in (32, 96):
                        ins = v.tensor_tensor(q6[s][a:a + 32, :], l6_qn[s][a:a + 32, :], f32(q6[s][a:a + 32, :]), ALU.subtract)
                    ins.then_inc(l6_qkd[s], 1)

                def l6_causal(s, h):
                    dve.wait_ge(l6_a[s], l6_a.at(c, h))
                    if h > 3:
                        dve.wait_ge(l6_o[s], l6_o.at(c, h - 4))
                    v.tensor_tensor(l6_at[s][:, h % 4, :], P[s][h % 2][:, 0:384], C("tri"), ALU.mult).then_inc(l6_atd[s], 1)

                def l6_sum(s):
                    dve.wait_ge(l6_yd[s], l6_yd.at(c))
                    link(v.tensor_tensor(res[s][:, :, :], P[s][0][:, 0:256].rearrange("p (t d) -> p t d", t=2), x[s][:, :, :], ALU.add))

                def l7_route(s):
                    dve.wait_ge(l7_lg[s], l7_lg.at(c))
                    v.tensor_tensor(ex_log[s], P[s][3][:, 0:16].rearrange("p (t e) -> p t e", t=2),
                                    W("l7_rb").unsqueeze(1).to_broadcast([128, 2, 8]), ALU.add).then_inc(l7_lgb[s], 1)
                    dve.wait_ge(l7_pr[s], l7_pr.at(c))
                    settle(dve)
                    for t in range(2):
                        ins = v.max(ex_mx[s][:, t, :], ex_m2[s][:, t, :])
                    link(ins)
                    settle(dve)
                    for t in range(2):
                        ins = v.max_index(idx[s][:, t, :], ex_mx[s][:, t, :], ex_m2[s][:, t, :])
                    link(ins)
                    link(v.tensor_copy(ex_ix[s], idx[s][:, :, :]))
                    for t in range(2):
                        ins = v.tensor_scalar(ex_log[s][:, t, :], C("iota8"), ex_ix[s][:, t, 0:1], None, ALU.is_equal)
                    link(ins)
                    for t in range(2):
                        ins = v.scalar_tensor_tensor(out=ex_mx[s][:, t, :], in0=C("iota8"), scalar=ex_ix[s][:, t, 1:2],
                                                     in1=ex_log[s][:, t, :], op0=ALU.is_equal, op1=ALU.add)
                    link(ins)
                    link(v.tensor_tensor(ex_mk[s], ex_mx[s], ex_m2[s], ALU.mult))

                def l7_gate(s, n):
                    dve.wait_ge(l7_sg[s], l7_sg.at(c, n))
                    if n > 3:
                        dve.wait_ge(l7_y[s], l7_y.at(c, n // 2 - 2))
                    v.tensor_tensor(ex_h[s][:, n // 2 % 2, n % 2, :], P[s][n % 3][:, 256:512], ex_g[s][:, n % 2, :], ALU.mult
                                    ).then_inc(l7_h[s], 1)

                def l7_add(s, e):
                    dve.wait_ge(l7_y[s], l7_y.at(c, e))
                    if e:
                        dve.wait_ge(l7_acc[s], l7_acc.at(c, e - 1))
                    for t in range(2):
                        y = P[s][3][:, 128 * t:128 * t + 128]
                        if e:
                            ins = v.scalar_tensor_tensor(out=res[s][:, t, :], in0=y, scalar=ex_mk[s][:, t, e - 1:e],
                                                         in1=res[s][:, t, :], op0=ALU.mult, op1=ALU.add)
                        else:
                            ins = v.tensor_tensor(res[s][:, t, :], y, x[s][:, t, :], ALU.add)
                    ins.then_inc(l7_acc[s], 1)

                def l7(s):
                    l7_route(s)
                    for n in range(2):
                        l7_gate(s, n)
                    for e in range(E3):
                        if e + 1 < E3:
                            l7_gate(s, 2 * e + 2)
                            l7_gate(s, 2 * e + 3)
                        l7_add(s, e)
                    dve.wait_ge(l7_acc[s], l7_acc.at(c, E3 - 1))

                for s in S2:
                    l0_elu(s)
                for s in S2:
                    l0_keep(s)
                for s in S2:
                    l0_mix(s)
                    norm(s, 0, 0)
                if PHASES > 1:
                    for s in S2:
                        l1(s)
                        norm(s, 1, 1)
                if PHASES > 2:
                    for s in S2:
                        l2_kq(s)
                        l2_vals(s)
                    for i in range(4):
                        for s in S2:
                            l2_maxes(s, i)
                        for s in S2:
                            l2_max_rows(s, i)
                    for s in S2:
                        l2_recip(s)
                    for s in S2:
                        l2_sum(s)
                        norm(s, 2, 2)
                if PHASES > 3:
                    for L in range(2):
                        for s in S2:
                            for i in range(4):
                                l3_reduce(s, L, i)
                                if i:
                                    l3_unit(s, L, i - 1)
                                    l3_rotate(s, L, i - 1)
                            l3_unit(s, L, 3)
                            l3_rotate(s, L, 3)
                        for h in range(LH + 1):
                            for s in S2:
                                if h < LH:
                                    l3_mask(s, L, h)
                            for s in S2:
                                if h < LH:
                                    l3_recip(s, L, h)
                            for s in S2:
                                if h and h % 2 == 0:
                                    l3_keep_o(s, L, h // 2 - 1)
                        for s in S2:
                            l3_mid(s, L)
                        for s in S2:
                            l3_norm(s, L)
                        for s in S2:
                            l3_glu(s, L)
                        for s in S2:
                            l3_end(s, L)
                            if L:
                                norm(s, 5, 6)
                if PHASES > 4:
                    for s in S2:
                        l4_sumsq(s)
                    for s in S2:
                        l4_normed(s)
                    for s in S2:
                        l4_parts(s)
                    for s in S2:
                        l4_halves(s)
                    for s in S2:
                        l4_recip(s)
                    for s in S2:
                        l4_sum(s)
                        norm(s, 6, 7)
                if PHASES > 5:
                    for s in S2:
                        l5_gate(s)
                    for s in S2:
                        l5_sum(s)
                        norm(s, 7, 8)
                if PHASES > 6:
                    for s in S2:
                        l6_cumulate(s)
                    for s in S2:
                        l6_keep_v(s)
                    for s in S2:
                        l6_parts(s)
                    for h in range(H3):
                        for s in S2:
                            l6_causal(s, h)
                    for s in S2:
                        l6_sum(s)
                        norm(s, 8, 9)
                if PHASES > 7:
                    for s in S2:
                        l7(s)
                        norm(s, 9, 10)
                link.close()

        @block.gpsimd
        def _(pool):
            g = nc.gpsimd
            pool.wait_ge(s_const, 16)
            pool.wait_ge(s_small, 16)
            for s in S2:
                ins = g.memset(f32(mT[s]), 0.0)
            ins.then_inc(s_zero, 1)
            pool.wait_ge(s_constr, 1)
            settled[pool] = sem("pool_settled")
            with pool.Fori(0, TURNS) as c:
                link = Links("pool", pool, c)

                def rsqrt(s, n):
                    pool.wait_ge(var_ready[s], var_ready.at(c, n))
                    g.tensor_tensor(rstd[s][:, :], ve[s][:, :], C("mhalf", 0, 2), ALU.pow).then_inc(rstd_ready[s], 1)

                def l2_prepare(s):
                    pool.wait_ge(x_ready[s], x_ready.at(c, X_OF[2]))
                    g.tensor_tensor(at_xb[s], x[s][:, :, :], W("l2_ob").unsqueeze(1).to_broadcast([128, 2, 128]), ALU.add)
                    link(g.memset(at_v[s], 0.0))
                    settle(pool)
                    g.memset(at_v[s][:, :, :, DH1:DH1 + 1], 1.0).then_inc(l2_xb[s], 1)

                def l2_masked(s, i):
                    if i == 0:
                        pool.wait_ge(st_in[s], st_in.at(c, 3))
                    if i >= 2:
                        pool.wait_ge(l2_st[s], l2_st.at(c, 4 * (i - 2) + 3))
                    settle(pool)
                    g.tensor_scalar(qm[s][:, i % 2, :, :], f32(qst[s]), C("mask2", i, i + 1), None, ALU.mult).then_inc(l2_qm[s], 1)

                def l2_scale(s):
                    pool.wait_ge(l2_rb[s], l2_rb.at(c))
                    g.tensor_tensor(at_o[s], at_o[s], at_r[s], ALU.mult).then_inc(l2_on[s], 1)

                def l3_norms(s, L, i):
                    t, w = divmod(i, 2)
                    pool.wait_ge(l3_ss[s], l3_ss.at(c, 4 * L + i))
                    settle(pool)
                    link(g.tensor_scalar(tiny[s][:, 64 + 8 * i:72 + 8 * i], tiny[s][:, 8 * i:8 * i + 8], 1e-24, None, ALU.max))
                    g.tensor_tensor(tiny[s][:, 32 + 8 * i:40 + 8 * i], tiny[s][:, 64 + 8 * i:72 + 8 * i], C("mhalf", 0, 8), ALU.pow
                                    ).then_inc(l3_rn[s], 1)

                def l3_cos(s, L, i):
                    t, w = divmod(i, 2)
                    pool.wait_ge(l3_qnd[s], l3_qnd.at(c, 4 * L + i))
                    if i:
                        pool.wait_ge(l3_rot[s], l3_rot.at(c, 4 * L + i - 1))
                    cos = xpos[:, L, w, 0, t, :].unsqueeze(1).to_broadcast([128, LH, LD])
                    g.tensor_tensor(l3_a[s].rearrange("p (h d) -> p h d", h=LH), l3_qn[s][:, i % 2, :].rearrange("p (h d) -> p h d", h=LH),
                                    cos, ALU.mult).then_inc(l3_ad[s], 1)

                def l3_scale(s, L, h):
                    pool.wait_ge(l3_rs[s], l3_rs.at(c, 8 * L + h))
                    a = 96 + 8 * (h % 2)
                    settle(pool)
                    for t, (lo, hi) in enumerate(((0, 128), (128, 384))):
                        b = l3_sm[s][:, h % 2, lo:hi]
                        ins = g.tensor_scalar(b, b, tiny[s][:, a + 6 + t:a + 7 + t], None, ALU.mult)
                    ins.then_inc(l3_pn[s], 1)

                def l3_bias(s, L):
                    pool.wait_ge(x_ready[s], x_ready.at(c, 3 + 2 * L))
                    ins = g.tensor_tensor(l3_xb[s], x[s][:, :, :], W("l3_b2", 128 * L, 128 * L + 128).unsqueeze(1).to_broadcast([128, 2, 128]),
                                          ALU.add)
                    if L:
                        link(ins)
                        ins = g.tensor_tensor(l3_xb[s], l3_xb[s], res[s][:, :, :], ALU.add)
                    ins.then_inc(l3_xbd[s], 1)

                def l4_norms(s):
                    pool.wait_ge(l4_ss[s], l4_ss.at(c))
                    settle(pool)
                    link(g.tensor_scalar(tiny[s][:, 2:4], tiny[s][:, 0:2], 1e-24, None, ALU.max))
                    g.tensor_tensor(tiny[s][:, 4:6], tiny[s][:, 2:4], C("mhalf", 0, 2), ALU.pow).then_inc(l4_rn[s], 1)
                    link(g.memset(l4_v[s], 0.0))
                    settle(pool)
                    g.memset(l4_v[s][:, :, :, DH2:DH2 + 1], 1.0).then_inc(l4_vset[s], 1)

                def l4_masked(s, i):
                    if i == 0:
                        pool.wait_ge(l4_stin[s], l4_stin.at(c, 3))
                    settle(pool)
                    g.tensor_scalar(qm[s][:, i, :, :], f32(qst[s]), C("mask4", i, i + 1), None, ALU.mult).then_inc(l4_qm[s], 1)

                def l4_scale(s):
                    pool.wait_ge(l4_rb[s], l4_rb.at(c))
                    g.tensor_tensor(at_o[s][:, 0:2, :], at_o[s][:, 0:2, :], at_r[s][:, 0:2, :], ALU.mult).then_inc(l4_on[s], 1)

                def l6_masked(s, h):
                    if h == 0:
                        pool.wait_ge(l6_qkd[s], l6_qkd.at(c))
                    if h > 7:
                        pool.wait_ge(l6_a[s], l6_a.at(c, h - 8))
                    settle(pool)
                    g.tensor_scalar(qm6[s][:, h % 8, :], f32(q6[s]), C("mask6", h, h + 1), None, ALU.mult).then_inc(l6_qm[s], 1)

                for s in S2:
                    pool.wait_ge(out_done[s], out_done.at(c, -1))
                    settle(pool)
                    g.memset(l0_v[s][:, :, 128:129], 1.0).then_inc(l0_ones[s], 1)
                for s in S2:
                    rsqrt(s, 0)
                if PHASES > 1:
                    for s in S2:
                        rsqrt(s, 1)
                if PHASES > 2:
                    for s in S2:
                        l2_prepare(s)
                    for i in range(4):
                        for s in S2:
                            l2_masked(s, i)
                    for s in S2:
                        l2_scale(s)
                    for s in S2:
                        rsqrt(s, 2)
                if PHASES > 3:
                    for L in range(2):
                        for s in S2:
                            for i in range(4):
                                l3_norms(s, L, i)
                                if i:
                                    l3_cos(s, L, i - 1)
                            l3_cos(s, L, 3)
                        for h in range(LH):
                            for s in S2:
                                l3_scale(s, L, h)
                        for s in S2:
                            l3_bias(s, L)
                            rsqrt(s, 3 + L)
                    for s in S2:
                        rsqrt(s, 5)
                if PHASES > 4:
                    for s in S2:
                        l4_norms(s)
                    for i in range(2):
                        for s in S2:
                            l4_masked(s, i)
                    for s in S2:
                        l4_scale(s)
                    for s in S2:
                        rsqrt(s, 6)
                if PHASES > 5:
                    for s in S2:
                        rsqrt(s, 7)
                if PHASES > 6:
                    for h in range(H3):
                        for s in S2:
                            l6_masked(s, h)
                    for s in S2:
                        rsqrt(s, 8)
                if PHASES > 7:
                    for s in S2:
                        rsqrt(s, 9)
                link.close()


def pack(a):
    f = np.float32
    small = np.zeros((128, N_SMALL), f)

    def put(name, v, rows=128):
        at, n = SMALL[name]
        small[:rows, at:at + n] = np.asarray(v, f).reshape(rows, n)

    def bc(v):
        return np.broadcast_to(np.asarray(v, f).reshape(1, -1), (128, np.size(v)))

    put("l0_w", a["L0_attn_W"])
    put("l1_gate", a["L0_ffn_gate_w"].T)
    put("l1_gb", bc(a["L0_ffn_gate_b"]))
    put("l1_eb", bc(a["L0_ffn_expert_bias"]))
    put("l1_b1", a["L0_ffn_b1"].reshape(E0, 4, 128).transpose(2, 0, 1))
    put("l1_b2", a["L0_ffn_b2"], 8)
    l1 = np.concatenate([a["L0_ffn_w1"].transpose(1, 0, 2).reshape(128, -1),
                         a["L0_ffn_w2"].reshape(E0, 4, 128, D).transpose(2, 0, 1, 3).reshape(128, -1)], 1)
    swap = np.arange(128) ^ 1
    q_rows = lambda w: np.concatenate([w, np.zeros((64, w.shape[1]), f)], 0)
    kv_rows = lambda w: np.concatenate([np.zeros((64, w.shape[1]), f), w], 0)
    put("l2_down", np.concatenate([a["L1_attn_Wd_q_w"], a["L1_attn_Wd_kv_w"]], 1))
    put("l2_down_b", np.concatenate([a["L1_attn_Wd_q_b"], a["L1_attn_Wd_kv_b"]]))
    put("l2_qc", q_rows(a["L1_attn_Wu_q_w"]))
    put("l2_qr", q_rows(a["L1_attn_Wq_r_w"]))
    put("l2_qrs", q_rows(a["L1_attn_Wq_r_w"][:, swap]))
    put("l2_kc", kv_rows(a["L1_attn_Wu_k_w"]))
    put("l2_kr", a["L1_attn_Wk_r_w"])
    put("l2_krs", a["L1_attn_Wk_r_w"][:, swap])
    put("l2_v", kv_rows(a["L1_attn_Wu_v_w"]))
    put("l2_qcb", a["L1_attn_Wu_q_b"])
    put("l2_qrb", a["L1_attn_Wq_r_b"])
    put("l2_qrsb", a["L1_attn_Wq_r_b"][swap])
    put("l2_kcb", a["L1_attn_Wu_k_b"])
    put("l2_krb", a["L1_attn_Wk_r_b"])
    put("l2_krsb", a["L1_attn_Wk_r_b"][swap])
    put("l2_vb", bc(a["L1_attn_Wu_v_b"]))
    put("l2_ob", bc(a["L1_attn_Wo_b"]))
    o = np.zeros((4, 32, 4, D), f)
    o[:, 0:DH1] = a["L1_attn_Wo_w"].reshape(4, 4, DH1, D).transpose(0, 2, 1, 3)
    put("l2_o", o)
    l3 = np.zeros((128, 2, N_L3W), f)
    for L in range(2):
        at, n = L3W["qkv"]
        l3[:, L, at:at + n] = a["L1_ffn_wqkv"][L]
        at, n = L3W["o"]
        l3[:, L, at:at + n] = a["L1_ffn_wo"][L].reshape(4, 128, D).transpose(1, 0, 2).reshape(128, -1)
        at, n = L3W["w1"]
        l3[:, L, at:at + n] = a["L1_ffn_w1"][L]
        at, n = L3W["w2"]
        w2 = np.zeros((3, 128, D), f)
        w2.reshape(384, D)[0:HID] = a["L1_ffn_w2"][L]
        l3[:, L, at:at + n] = w2.transpose(1, 0, 2).reshape(128, -1)
    put("l3_g", a["L1_ffn_ln_g"].T)
    put("l3_b", a["L1_ffn_ln_b"].T)
    b1 = np.zeros((2, 2, 384), f)
    b1[:, :, 0:HID] = a["L1_ffn_b1"].reshape(2, 2, HID)
    put("l3_b1", b1.reshape(2, 2, 3, 128).transpose(3, 0, 1, 2))
    put("l3_b2", bc(a["L1_ffn_b2"]))
    rot = (np.arange(LD) + LD // 2) % LD
    qk = np.stack([a["L1_ffn_q_scale"], a["L1_ffn_k_scale"]], 1)
    put("l3_scale", bc(np.stack([qk, qk[:, :, rot]], 2)))
    put("l4_gamma", a["L2_attn_gamma"])
    put("l4_w", np.concatenate([a["L2_attn_w_q"], a["L2_attn_w_kv"]], 1))
    o = np.zeros((4, 32, 2, D), f)
    o[:, 0:DH2] = a["L2_attn_w_out"].reshape(4, 2, DH2, D).transpose(0, 2, 1, 3)
    put("l4_o", o)
    blocks = lambda w: w.T.reshape(w.shape[1] // 128, 128, w.shape[0]).transpose(1, 0, 2).reshape(128, -1)
    l5 = np.concatenate([blocks(a[f"L2_ffn_{n}_w"]) for n in ("w1", "w2", "h1", "h2", "w3")], 1)
    for n, k in (("l5_s1", "w1"), ("l5_s2", "w2"), ("l5_h1s", "h1"), ("l5_h2s", "h2")):
        put(n, a[f"L2_ffn_{k}_s"].reshape(4, 128).T)
    put("l5_s3", bc(a["L2_ffn_w3_s"]))
    wq, wk = a["L3_attn_W_Q"][:, :, 0].T, a["L3_attn_W_K"][:, :, 0].T
    put("l6_q", np.concatenate([wq] * 8, 1))
    put("l6_k", np.concatenate([wk] * 8, 1))
    put("l6_v", a["L3_attn_W_V"].transpose(1, 0, 2))
    put("l6_o", a["L3_attn_W_O"].transpose(2, 1, 0).reshape(8, 128, D).transpose(1, 0, 2))
    wg = np.concatenate([a["L3_ffn_Wg_s"][None], a["L3_ffn_Wg"]], 0)
    wu = np.concatenate([a["L3_ffn_Wu_s"][None], a["L3_ffn_Wu"]], 0)
    wd = np.concatenate([a["L3_ffn_Wd_s"][None], a["L3_ffn_Wd"]], 0)
    l7 = np.concatenate([wg.transpose(2, 0, 1), wu.transpose(2, 0, 1),
                         wd.transpose(0, 2, 1).reshape(E3, 2, 128, D).transpose(2, 0, 1, 3).reshape(128, E3, 2 * D)],
                        2).reshape(128, -1)
    put("l7_gate", a["L3_ffn_Wr"].T)
    put("l7_rb", bc(a["L3_ffn_rb"]))
    const, constr = shape_constants()
    out = dict(x=a["L0_attn_x"], small=small, l1=l1, l3=l3.reshape(128, -1), l5=l5, l7=l7, const=const, constr=constr)
    return {k: np.ascontiguousarray(v, f) for k, v in out.items()}


LINKS = {"act": 2, "dve": 166, "pool": 24}


def kernel(**inputs):
    import concourse.bacc as bacc
    from concourse.bass_utils import run_bass_kernel_spmd

    nc = bacc.Bacc("TRN2", target_bir_lowering=False, num_devices=1)
    arrays = pack({k: np.asarray(v) for k, v in inputs.items()})
    args = [nc.dram_tensor(f"in_{k}", v.shape, F32, kind="ExternalInput").ap() for k, v in arrays.items()]
    out = nc.dram_tensor("out", (NSEQ, SEQ, D), F32, kind="ExternalOutput").ap()
    build(nc, *args, out, LINKS)
    r = run_bass_kernel_spmd(nc, [{f"in_{k}": v for k, v in arrays.items()}], core_ids=[0])
    return r.results[0]["out"]
```

```python
from contextlib import ExitStack

import concourse.bass as bass
from concourse import mybir
import numpy as np

F32 = mybir.dt.float32
F32R = mybir.dt.float32r
U32 = mybir.dt.uint32
ALU = mybir.AluOpType
ACT = mybir.ActivationFunctionType
X = mybir.AxisListType.X

D = 128
SEQ = 256
NSEQ = 8
STREAMS = 2
TURNS = NSEQ // STREAMS
LN_EPS = 1e-5

E0, F0 = 8, 512
H1, DH1 = 16, 8
LH, LD, HID, WIN = 8, 64, 341, 64
FT = [128, 128, 85]
L3_PAIR = {1: 1, 2: 2, 4: 3}
H2, DH2 = 8, 16
H3, DH3 = 16, 64
E3, I3 = 9, 256


def columns(parts):
    at, out = 0, {}
    for name, n in parts:
        out[name] = (at, n)
        at += n
    return out, at


SMALL, N_SMALL = columns([
    ("l0_w", 384),
    ("l1_gate", E0), ("l1_gb", E0), ("l1_eb", E0), ("l1_b1", E0 * 4), ("l1_b2", D),
    ("l2_down", 128), ("l2_down_b", 1), ("l2_qc", 128), ("l2_qr", 128), ("l2_qrs", 128),
    ("l2_kc", 128), ("l2_kr", 128), ("l2_krs", 128), ("l2_v", 128), ("l2_o", 4 * 128),
    ("l2_qcb", 1), ("l2_qrb", 1), ("l2_qrsb", 1), ("l2_kcb", 1), ("l2_krb", 1), ("l2_krsb", 1),
    ("l2_vb", 128), ("l2_ob", 128),
    ("l3_g", 2), ("l3_b", 2), ("l3_b1", 12), ("l3_b2", 2 * 128), ("l3_scale", 2 * 4 * 64),
    ("l4_gamma", 1), ("l4_w", 384), ("l4_o", 2 * 128),
    ("l5_s1", 4), ("l5_s2", 4), ("l5_h1s", 4), ("l5_h2s", 4), ("l5_s3", 128),
    ("l6_q", 128), ("l6_k", 128), ("l6_v", 1024), ("l6_o", 1024),
    ("l7_gate", 8), ("l7_rb", 8),
])
L3W, N_L3W = columns([("qkv", 1536), ("o", 512), ("w1", 2 * HID), ("w2", 3 * 128)])
L5W, N_L5W = columns([("w1", 512), ("w2", 512), ("h1", 2048), ("h2", 2048), ("w3", 512)])
N_L1W = E0 * (F0 + F0)
N_L7W = E3 * (2 * I3 + 2 * D)
N_REGION_A = max(N_L1W, N_L5W)
N_REGION_B = max(2 * N_L3W, N_L7W)
CONST, N_CONST = columns([
    ("ident", 128), ("iota8", 8), ("rope_c", 256), ("rope_s", 256), ("tri", 384), ("band", 384),
    ("xpos", 512), ("mask2", 4), ("mask4", 2), ("mask6", 16), ("half_pi", 1), ("mhalf", 16), ("ones", 256),
    ("rows8", 128), ("rows16", 128), ("pair_sum", 128), ("half", 1), ("root_half", 1),
])
CONSTR, N_CONSTR = columns([("sel_qh", 512), ("sel_ql", 512), ("sel_kh", 512), ("sel_kl", 512), ("sel_max", 512)])


def shape_constants():
    f = np.float32
    c = np.zeros((128, N_CONST), f)
    cr = np.zeros((128, N_CONSTR), f)
    p = np.arange(128)

    def put(name, a):
        at, n = CONST[name]
        c[:, at:at + n] = np.asarray(a, f).reshape(128, n)

    put("ident", np.eye(128))
    put("iota8", np.tile(np.arange(8), (128, 1)))
    theta = f(10000.0) ** (f(-2.0) * np.arange(64, dtype=f)) / f(64)
    r = np.arange(SEQ, dtype=f)[None, :] * theta[p // 2][:, None]
    put("rope_c", np.cos(r))
    put("rope_s", np.sin(r) * np.where(p % 2 == 0, -1, 1)[:, None])
    tri = (p[None, :] >= p[:, None]).astype(f)
    put("tri", np.concatenate([tri, np.ones((128, 128)), tri], 1))
    band = np.zeros((128, 384), f)
    for t, at, n in ((0, 0, 128), (1, 128, 256)):
        i = t * 128 + p[:, None]
        j = np.arange(n)[None, :]
        band[:, at:at + n] = np.where((i < j) | (i > j + WIN), f(1e25), f(0))
    put("band", band)
    half = np.arange(0, LD, 2, dtype=f)
    inv = f(1.0) / f(10000.0) ** (half / f(LD))
    t = np.arange(SEQ, dtype=f)
    fr = np.concatenate([t[:, None] * inv[None, :]] * 2, 1)
    base = (half + f(0.4 * LD)) / f(1.4 * LD)
    sc = base[None, :] ** ((t - SEQ // 2) / f(WIN // 2))[:, None]
    sc = np.concatenate([sc, sc], 1)
    sign = np.where(np.arange(LD) < LD // 2, -1, 1)[None, :]
    tabs = [[np.cos(fr) * sc, np.sin(fr) * sc * sign], [np.cos(fr) / sc * f(-0.125), np.sin(fr) / sc * sign * f(-0.125)]]
    x = np.zeros((128, 2, 2, 2, 64), f)
    for w in range(2):
        for k in range(2):
            x[:, w, k] = tabs[w][k].reshape(2, 128, 64).transpose(1, 0, 2)
    put("xpos", x)
    put("mask2", (p % 32 // DH1)[:, None] == np.arange(4)[None])
    put("mask4", (p % 32 // DH2)[:, None] == np.arange(2)[None])
    put("mask6", (p % 16)[:, None] == np.arange(16)[None])
    put("half_pi", np.where(p % 32 < 16, np.pi / 2, 0))
    put("mhalf", np.full((128, 16), -0.5))
    put("ones", np.ones((128, 256)))
    put("rows8", (p[:, None] == (p // 32 * 32 + DH1)[None, :]))
    put("rows16", (p[:, None] == (p // 32 * 32 + DH2)[None, :]))
    put("pair_sum", (p[:, None] < 32) & (p[:, None] % 16 == p[None, :] % 16))
    put("half", np.full((128, 1), 0.5))
    put("root_half", np.full((128, 1), 0.5 ** 0.5))
    for name, quads in (("sel_qh", (0, 2)), ("sel_ql", (1, 3)), ("sel_kh", (0, 1)), ("sel_kl", (2, 3))):
        at = CONSTR[name][0]
        for j in range(4):
            for q in quads:
                for k in range(32):
                    cr[32 * j + k, at + 128 * j + 32 * q + k] = 1
    at = CONSTR["sel_max"][0]
    for j in range(4):
        cr[j, at + 128 * j:at + 128 * (j + 1)] = -1
        cr[32 + j, at + 128 * j:at + 128 * (j + 1)] = -1
    return c, cr


SHARED = {
    "pe_input": ("l0_qkv", "l1_lg", "l2_ct", "l3_qkv", "l4_p", "l6_qk", "l7_lg"),
    "pe_second": ("l0_kv", "l1_mTp", "l2_kp", "l3_tp", "l4_hs", "l5_yd", "l6_dn"),
    "pe_hidden": ("l1_z", "l3_z", "l5_z", "l7_z"),
    "pe_values": ("l2_qp", "l3_otp", "l6_vp"),
    "pe_values2": ("l2_v", "l3_hs", "l4_bc"),
    "pe_stack": ("st_full", "l3_pt", "l4_stf"),
    "pe_scores": ("l2_s", "l3_s", "l6_a"),
    "pe_maxima": ("l2_m", "l3_hnp"),
    "pe_scoresT": ("l2_st", "l4_st"),
    "pe_weighted": ("l2_pv", "l3_o", "l4_pv", "l6_o"),
    "pe_spread": ("l2_bc", "l3_y2"),
    "pe_output": ("l0_out", "l1_y", "l2_y", "l3_y", "l4_y", "l6_yd", "l7_y"),
    "act_moved": ("l0_v_in", "l1_mT", "l2_cts", "l3_vin", "l4_oin", "l6_csd"),
    "act_stack": ("st_in", "l3_te", "l4_stin", "l5_sg", "l6_va"),
    "act_hidden": ("l1_ha", "l3_gld", "l5_h1", "l7_sg"),
    "act_probs": ("l2_p", "l3_e", "l4_sq", "l5_h2"),
    "act_out": ("l2_ob", "l3_ot", "l6_ot", "l7_pr"),
    "act_squares": ("l3_sqd",),
    "act_normedT": ("l3_hnTd",),
    "dve_first": ("l0_qk", "l1_mask", "l2_split", "l3_ss", "l4_ss", "l6_pr", "l7_lgb"),
    "dve_second": ("l0_kvs_in", "l1_hd", "l2_vs", "l3_qnd", "l4_xnd", "l5_h0", "l6_qkd", "l7_h"),
    "dve_sums": ("l1_acc", "l3_on", "l4_hsd", "l6_vd", "l7_acc"),
    "dve_max": ("l2_su", "l3_smd", "l4_split", "l6_atd"),
    "dve_max_all": ("l2_mu", "l3_rot", "l4_vd"),
    "dve_max_tok": ("l2_mtok", "l3_pte"),
    "dve_inverse": ("l2_rb", "l3_hnd", "l4_rb"),
    "dve_hidden": ("l3_h",),
    "dve_lengths": ("l3_len",),
    "pool_first": ("l0_ones", "l2_xb", "l3_rn", "l4_rn"),
    "pool_masked": ("l2_qm", "l3_ad", "l4_qm", "l6_qm"),
    "dve_normed": ("l2_on", "l4_on"),
    "pe_sums": ("l2_dn", "l4_dn"),
    "act_queries": ("l3_qin",),
    "pool_bias": ("l3_xbd", "l4_vset"),
}


class Track:

    def __init__(self, new, name, before=0):
        self.before = before
        self.sems = [new(f"{name}_{s}") for s in range(STREAMS)]
        self.total = 0


class Signal:

    def __init__(self, track, per_turn=1):
        self.track, self.offset, self.per_turn = track, track.total, per_turn
        track.total += per_turn

    def __getitem__(self, s):
        return self.track.sems[s]

    def at(self, turn, k=0):
        return turn * self.track.total + (self.track.before + self.offset + k + 1)


X_OF = [-1, 0, 1, 2, 6, 7, 8, 9, 10]


def build(nc, x_in, small_in, l1_in, l3_in, l5_in, l7_in, const_in, constr_in, out, links, PHASES=8):
    with ExitStack() as ctx:
        def sb(name, shape, dt=F32):
            return ctx.enter_context(nc.sbuf_tensor(name, shape, dt))

        def sem(name):
            return ctx.enter_context(nc.semaphore(name))

        tracks = {}

        def signal(name, per_turn=1, before=0):
            at = next((t for t, names in SHARED.items() if name in names), name)
            if at not in tracks:
                tracks[at] = Track(sem, at, before)
            return Signal(tracks[at], per_turn)

        def f32(ap):
            return ap.bitcast(F32)

        S2 = range(STREAMS)
        small = sb("small", [128, N_SMALL])
        region_a = sb("region_a", [128, N_REGION_A])
        region_b = sb("region_b", [128, N_REGION_B])
        const = sb("const", [128, N_CONST])
        constr = sb("constr", [128, N_CONSTR], F32R)
        xpos = sb("xpos", [128, 2, 2, 2, 2, 64])

        def W(name, a=0, b=None, rows=128):
            at, n = SMALL[name]
            return small[0:rows, at + a:at + (n if b is None else b)]

        def C(name, a=0, b=None):
            at, n = CONST[name]
            return const[:, at + a:at + (n if b is None else b)]

        def CR(name, j):
            at = CONSTR[name][0]
            return constr[:, at + 128 * j:at + 128 * (j + 1)]

        ident = C("ident")

        x = [sb(f"x{s}", [128, 2, D]) for s in S2]
        res = [sb(f"res{s}", [128, 2, D]) for s in S2]
        xT = [sb(f"xT{s}", [128, SEQ]) for s in S2]
        shT = [sb(f"shT{s}", [128, SEQ]) for s in S2]
        qTm = [sb(f"qTm{s}", [128, 2, 2, SEQ]) for s in S2]
        stats = [sb(f"stats{s}", [128, 2, 6]) for s in S2]
        mv = [sb(f"mv{s}", [128, 2, 2]) for s in S2]
        ve = [sb(f"ve{s}", [128, 2]) for s in S2]
        rstd = [sb(f"rstd{s}", [128, 2]) for s in S2]
        tiny = [sb(f"tiny{s}", [128, 224]) for s in S2]
        idx = [sb(f"idx{s}", [128, 2, 8], U32) for s in S2]
        scr = [sb(f"scr{s}", [128, 6144]) for s in S2]
        opr = [sb(f"opr{s}", [128, 4352], F32R) for s in S2]
        P = [[ctx.enter_context(nc.psum_tensor(f"P{s}{b}", [128, 512], F32)) for b in range(4)] for s in S2]

        def view(s, at, *dims):
            n = int(np.prod(dims))
            ap = scr[s][:, at:at + n]
            if len(dims) == 2:
                return ap.rearrange("p (a b) -> p a b", a=dims[0])
            if len(dims) == 3:
                return ap.rearrange("p (a b c) -> p a b c", a=dims[0], b=dims[1])
            return ap

        kst = [opr[s][:, 0:1024].rearrange("p (j n) -> p j n", j=4) for s in S2]
        qst = [opr[s][:, 1024:2048].rearrange("p (j n) -> p j n", j=4) for s in S2]
        qm = [opr[s][:, 2048:4096].rearrange("p (b j n) -> p b j n", b=2, j=4) for s in S2]
        qm6 = [opr[s][:, 2048:4096].rearrange("p (b n) -> p b n", b=8) for s in S2]
        parts = [opr[s][:, 3072:4096].rearrange("p (j n) -> p j n", j=4) for s in S2]
        mT = [opr[s][:, 4096:4352] for s in S2]

        l0_e = [view(s, 0, 3, 256) for s in S2]
        l0_r = [view(s, 768, 3, 256) for s in S2]
        l0_v = [view(s, 1536, 2, 132) for s in S2]
        l0_kvs = [view(s, 1800, 132) for s in S2]
        ex_h = [view(s, 0, 2, 4, 256) for s in S2]
        ex_g = [view(s, 2048, 2, 256) for s in S2]
        ex_log = [tiny[s][:, 0:16].rearrange("p (t e) -> p t e", t=2) for s in S2]
        ex_mx = [tiny[s][:, 16:32].rearrange("p (t e) -> p t e", t=2) for s in S2]
        ex_ix = [tiny[s][:, 32:48].rearrange("p (t e) -> p t e", t=2) for s in S2]
        ex_mk = [tiny[s][:, 48:64].rearrange("p (t e) -> p t e", t=2) for s in S2]
        ex_m2 = [tiny[s][:, 64:80].rearrange("p (t e) -> p t e", t=2) for s in S2]
        ex_mT = [view(s, 2560, 256) for s in S2]
        at_p = [view(s, 0, 4, 512) for s in S2]
        at_rope = [view(s, 0, 6, 256) for s in S2]
        at_v = [view(s, 2048, 2, 16, 32) for s in S2]
        at_o = [view(s, 3072, 4, 256) for s in S2]
        at_r = [view(s, 4096, 4, 256) for s in S2]
        at_ct = [view(s, 5120, 256) for s in S2]
        at_kq = [view(s, 5376, 2, 256) for s in S2]
        at_xb = [view(s, 5888, 2, 128) for s in S2]
        inverse = [tiny[s][:, 160:192] for s in S2]
        m_tok = [tiny[s][:, 0:8].rearrange("p (t j) -> p t j", t=2) for s in S2]

        l3_tok = [view(s, 0, 2, 2, 512) for s in S2]
        l3_v = [view(s, 2048, 2, 512) for s in S2]
        l3_sq, l3_qn = [view(s, 3072, 2, 512) for s in S2], [view(s, 4096, 2, 512) for s in S2]
        l3_a, l3_b = [view(s, 5120, 512) for s in S2], [view(s, 5632, 512) for s in S2]
        l3_kT = [view(s, 3072, 2, 256) for s in S2]
        l3_sm, l3_pT = [view(s, 3584, 2, 384) for s in S2], [view(s, 4352, 2, 384) for s in S2]
        l3_o_tok, l3_oT = [view(s, 0, 2, 512) for s in S2], [view(s, 1024, 4, 256) for s in S2]
        l3_hn, l3_hnT = [view(s, 3072, 2, 128) for s in S2], [view(s, 3328, 256) for s in S2]
        l3_gl, l3_hh = [view(s, 3584, 3, 256) for s in S2], [view(s, 4352, 3, 256) for s in S2]
        l3_xb = [view(s, 5120, 2, 128) for s in S2]
        l4_xn = [view(s, 0, 2, 128) for s in S2]
        l4_v = [view(s, 2048, 2, 8, 32) for s in S2]
        l5_hA, l5_hB, l5_hC = ([view(s, a, 4, 256) for s in S2] for a in (0, 1024, 3072))
        l5_y = [view(s, 4096, 2, 128) for s in S2]
        l6_v = [view(s, 0, 2, 1024) for s in S2]
        l6_at = [view(s, 2048, 4, 384) for s in S2]
        l6_oT = [view(s, 3584, 8, 256) for s in S2]
        l6_th, l6_cs = [view(s, 3584, 2, 256) for s in S2], [view(s, 4096, 2, 256) for s in S2]
        l6_cum, l6_prod, l6_den, l6_rd, l6_qn = ([view(s, a, 256) for s in S2] for a in (4608, 4864, 5120, 5376, 5632))
        k6 = [opr[s][:, 0:256] for s in S2]
        q6 = [opr[s][:, 1024:1280] for s in S2]

        s_small, s_const, s_stage, s_zero, s_zd = (sem(n) for n in ("s_small", "s_const", "s_stage", "s_zero", "s_zd"))
        s_constr, s_xpos = sem("s_constr"), sem("s_xpos")
        s_wa, s_wb = sem("s_wa"), sem("s_wb")
        x_in_done, out_done = signal("x_in", 16), signal("out_done", 16, before=1)
        settled = {}
        chain = {e: sem(f"{e}_link") for e in ("act", "dve", "pool")}
        n_x = X_OF[PHASES] + 1
        n_ln = PHASES + (2 if PHASES > 3 else 0)
        var_ready, rstd_ready = signal("var_ready", n_ln), signal("rstd_ready", n_ln)
        x_ready = signal("x_ready", n_x, before=1)
        xTp, xT_ready = signal("xTp", n_x), signal("xT_ready", n_x)

        l0_ones = signal("l0_ones")
        l0_qkv, l0_v_in, l0_qk, l0_kv, l0_kvs_in, l0_out = (signal(n) for n in
            ("l0_qkv", "l0_v_in", "l0_qk", "l0_kv", "l0_kvs_in", "l0_out"))
        l1_lg, l1_mask, l1_mTp, l1_mT = (signal(n) for n in ("l1_lg", "l1_mask", "l1_mTp", "l1_mT"))
        l1_z, l1_ha, l1_hd = signal("l1_z", 16), signal("l1_ha", 8), signal("l1_hd", 8)
        l1_y, l1_acc = signal("l1_y", 9), signal("l1_acc", 9)
        l2_ct, l2_cts, l2_kp, l2_qp, l2_split, l2_v, l2_vs, l2_xb = (signal(n) for n in
            ("l2_ct", "l2_cts", "l2_kp", "l2_qp", "l2_split", "l2_v", "l2_vs", "l2_xb"))
        st_full, st_in = signal("st_full", 4), signal("st_in", 4)
        l2_qm = signal("l2_qm", 4)
        l2_s, l2_su, l2_m, l2_mu = signal("l2_s", 16), signal("l2_su", 16), signal("l2_m", 4), signal("l2_mu", 4)
        l2_mtok = signal("l2_mtok", 4)
        l2_st, l2_p, l2_pv = signal("l2_st", 16), signal("l2_p", 16), signal("l2_pv", 4)
        l2_ob, l2_dn, l2_bc, l2_rb, l2_on, l2_y = (signal(n) for n in ("l2_ob", "l2_dn", "l2_bc", "l2_rb", "l2_on", "l2_y"))

        if PHASES > 3:
            l3_qkv, l3_sqd, l3_ss, l3_rn, l3_qnd, l3_ad, l3_rot, l3_qin, l3_len = (signal(n, 2 * k) for n, k in
                (("l3_qkv", 6), ("l3_sqd", 4), ("l3_ss", 4), ("l3_rn", 2), ("l3_qnd", 2), ("l3_ad", 4), ("l3_rot", 4),
                 ("l3_qin", 2), ("l3_len", 2)))
            l3_vin, l3_tp, l3_te = signal("l3_vin", 4), signal("l3_tp", 8), signal("l3_te", 8)
            l3_s, l3_smd, l3_e, l3_pt, l3_pte = (signal(n, 16) for n in
                ("l3_s", "l3_smd", "l3_e", "l3_pt", "l3_pte"))
            l3_o, l3_on, l3_otp, l3_ot = (signal(n, 4) for n in ("l3_o", "l3_on", "l3_otp", "l3_ot"))
            l3_y, l3_hs, l3_hnd, l3_hnp, l3_hnTd, l3_y2, l3_xbd = (signal(n, 2) for n in
                ("l3_y", "l3_hs", "l3_hnd", "l3_hnp", "l3_hnTd", "l3_y2", "l3_xbd"))
            l3_z, l3_gld, l3_h = signal("l3_z", 6), signal("l3_gld", 6), signal("l3_h", 6)
        if PHASES > 4:
            l4_ss, l4_rn, l4_xnd, l4_p, l4_split, l4_vd, l4_vset, l4_oin, l4_hs, l4_hsd, l4_dn, l4_bc, l4_rb, l4_on, l4_y = (
                signal(n) for n in ("l4_ss", "l4_rn", "l4_xnd", "l4_p", "l4_split", "l4_vd", "l4_vset", "l4_oin",
                                    "l4_hs", "l4_hsd", "l4_dn", "l4_bc", "l4_rb", "l4_on", "l4_y"))
            l4_stf, l4_stin, l4_qm = signal("l4_stf", 4), signal("l4_stin", 4), signal("l4_qm", 2)
            l4_st, l4_sq, l4_pv = signal("l4_st", 8), signal("l4_sq", 8), signal("l4_pv", 2)
        if PHASES > 5:
            l5_z, l5_sg, l5_h0 = signal("l5_z", 8), signal("l5_sg", 4), signal("l5_h0", 4)
            l5_h1, l5_h2, l5_yd = signal("l5_h1", 2), signal("l5_h2", 2), signal("l5_yd")
        if PHASES > 6:
            l6_qk, l6_csd, l6_pr, l6_dn, l6_qkd, l6_yd = (signal(n) for n in
                ("l6_qk", "l6_csd", "l6_pr", "l6_dn", "l6_qkd", "l6_yd"))
            l6_vp, l6_va, l6_vd = signal("l6_vp", 4), signal("l6_va", 2), signal("l6_vd", 2)
            l6_qm, l6_a, l6_atd, l6_o, l6_ot = signal("l6_qm", 16), signal("l6_a", 16), signal("l6_atd", 16), signal("l6_o", 16), signal("l6_ot", 8)
        if PHASES > 7:
            l7_lg, l7_lgb, l7_pr = (signal(n) for n in ("l7_lg", "l7_lgb", "l7_pr"))
            l7_z, l7_sg, l7_h = signal("l7_z", 18), signal("l7_sg", 18), signal("l7_h", 18)
            l7_y, l7_acc = signal("l7_y", 9), signal("l7_acc", 9)

        def settle(eng):
            eng.sem_inc(settled[eng], 1)

        class Links:

            def __init__(self, name, eng, turn):
                self.name, self.eng, self.turn, self.n = name, eng, turn, 0

            def __call__(self, ins):
                ins.then_inc(chain[self.name], 1)
                self.n += 1
                self.eng.wait_ge(chain[self.name], self.turn * links[self.name] + self.n)

            def close(self):
                if links[self.name] != max(self.n, 1):
                    raise ValueError(f"LINK {self.name} {max(self.n, 1)}")

        block = ctx.enter_context(nc.Block())

        @block.sync
        def _(sp):
            sp.dma_start(const[:, :], const_in).then_inc(s_const, 16)
            sp.dma_start(scr[0][:, 0:N_CONSTR], constr_in).then_inc(s_stage, 16)
            sp.dma_start(small[:, :], small_in).then_inc(s_small, 16)
            for s in S2:
                sp.sem_inc(out_done[s], 1)
            with sp.Fori(0, TURNS) as c:
                for s in S2:
                    sp.wait_ge(out_done[s], out_done.at(c, -1))
                    sp.dma_start(x[s][:, :, :], x_in[2 * c + s, :, :].rearrange("(t p) d -> p t d", p=128)
                                 ).then_inc(x_in_done[s], 16)
                if PHASES > 1:
                    sp.dma_start(region_a[:, 0:N_L1W], l1_in).then_inc(s_wa, 16)
                if PHASES > 3:
                    sp.dma_start(region_b[:, 0:2 * N_L3W], l3_in).then_inc(s_wb, 16)
                if PHASES > 5:
                    for s in S2:
                        sp.wait_ge(x_ready[s], x_ready.at(c, X_OF[2]))
                    sp.dma_start(region_a[:, 0:N_L5W], l5_in).then_inc(s_wa, 16)
                if PHASES > 7:
                    for s in S2:
                        sp.wait_ge(x_ready[s], x_ready.at(c, X_OF[4]))
                    sp.dma_start(region_b[:, 0:N_L7W], l7_in).then_inc(s_wb, 16)
                for s in S2:
                    sp.wait_ge(x_ready[s], x_ready.at(c, n_x - 1))
                    sp.dma_start(out[2 * c + s, :, :].rearrange("(t p) d -> p t d", p=128), x[s][:, :, :]
                                 ).then_inc(out_done[s], 16)
            for s in S2:
                sp.wait_ge(out_done[s], out_done.per_turn * TURNS + 1)

        n_wa = 16 * ((PHASES > 1) + (PHASES > 5))
        n_wb = 16 * ((PHASES > 3) + (PHASES > 7))

        @block.tensor
        def _(pe):
            pe.wait_ge(s_const, 16)
            pe.wait_ge(s_small, 16)
            pe.wait_ge(s_constr, 1)
            pe.wait_ge(s_zero, 1)
            pe.wait_ge(s_zd, 1)
            with pe.Fori(0, TURNS) as c:

                def mm(out_, lhsT, rhs, start=True, stop=True):
                    return pe.matmul(out_, lhsT, rhs, start=start, stop=stop)

                def transpose_x(s, k, src=x, ready=None):
                    if ready is not None:
                        pe.wait_ge(ready[s], ready.at(c))
                    if k == 0:
                        pe.wait_ge(x_in_done[s], x_in_done.at(c, 15))
                        pe.wait_ge(x_ready[s], x_ready.at(c, -1))
                    else:
                        pe.wait_ge(x_ready[s], x_ready.at(c, k - 1))
                    for t in range(2):
                        ins = pe.transpose(P[s][0][:, 128 * t:128 * t + 128], src[s][:, t, :], ident)
                    ins.then_inc(xTp[s], 1)
                    pe.wait_ge(xT_ready[s], xT_ready.at(c, k))

                def l0_project(s):
                    ins = mm(P[s][1][:, 0:256], W("l0_w", 0, 128), xT[s][:, :])
                    for t in range(2):
                        ins = mm(P[s][2][:, 256 * t:256 * t + 256], xT[s][:, 128 * t:128 * t + 128], W("l0_w", 128, 384))
                    ins.then_inc(l0_qkv[s], 1)

                def l0_state(s):
                    pe.wait_ge(l0_qk[s], l0_qk.at(c))
                    pe.wait_ge(l0_v_in[s], l0_v_in.at(c))
                    pe.wait_ge(l0_ones[s], l0_ones.at(c))
                    for t in range(2):
                        ins = mm(P[s][3][:, 0:129], l0_r[s][:, 1, 128 * t:128 * t + 128], l0_v[s][:, t, 0:129], t == 0, t == 1)
                    ins.then_inc(l0_kv[s], 1)

                def l0_read(s):
                    pe.wait_ge(l0_kvs_in[s], l0_kvs_in.at(c))
                    for t in range(2):
                        ins = mm(P[s][1][:, 129 * t:129 * t + 129], l0_r[s][:, 0, 128 * t:128 * t + 128], l0_kvs[s][:, 0:129])
                    ins.then_inc(l0_out[s], 1)

                def l1(s):
                    w1 = region_a[:, 0:E0 * F0].rearrange("p (e f) -> p e f", e=E0)
                    w2 = region_a[:, E0 * F0:N_L1W].rearrange("p (e f d) -> p e f d", e=E0, f=4)
                    for t in range(2):
                        ins = mm(P[s][3][:, 8 * t:8 * t + 8], xT[s][:, 128 * t:128 * t + 128], W("l1_gate"))
                    ins.then_inc(l1_lg[s], 1)
                    pe.wait_ge(s_wa, n_wa * c + 16)

                    def up(n):
                        e, p = divmod(n, 2)
                        if n >= 3:
                            m = n - 3
                            reader = l1_hd if m % 2 else l1_ha
                            pe.wait_ge(reader[s], reader.at(c, m // 2))
                        for f in range(2):
                            ins = mm(P[s][n % 3][:, 256 * f:256 * f + 256],
                                     w1[:, e, 128 * (2 * p + f):128 * (2 * p + f) + 128], xT[s][:, :])
                        ins.then_inc(l1_z[s], 1)

                    def down(e):
                        pe.wait_ge(l1_ha[s], l1_ha.at(c, e))
                        pe.wait_ge(l1_hd[s], l1_hd.at(c, e))
                        if e == 0:
                            pe.wait_ge(l1_mask[s], l1_mask.at(c))
                        else:
                            pe.wait_ge(l1_acc[s], l1_acc.at(c, e - 1))
                        for t in range(2):
                            for f in range(4):
                                ins = mm(P[s][3][:, 128 * t:128 * t + 128],
                                         ex_h[s][:, e % 2, f, 128 * t:128 * t + 128], w2[:, e, f, :], f == 0, f == 3)
                        ins.then_inc(l1_y[s], 1)

                    up(0)
                    up(1)
                    for e in range(E0):
                        if e + 1 < E0:
                            up(2 * e + 2)
                            up(2 * e + 3)
                        down(e)
                    for t in range(2):
                        ins = pe.transpose(P[s][0][0:8, 128 * t:128 * t + 128], ex_mk[s][:, t, :], ident)
                    ins.then_inc(l1_mTp[s], 1)
                    pe.wait_ge(l1_mT[s], l1_mT.at(c))
                    pe.wait_ge(l1_acc[s], l1_acc.at(c, E0 - 1))
                    for t in range(2):
                        ins = mm(P[s][3][:, 128 * t:128 * t + 128], ex_mT[s][0:8, 128 * t:128 * t + 128], W("l1_b2", rows=8))
                    ins.then_inc(l1_y[s], 1)

                def l2_down(s):
                    mm(P[s][1][:, 0:256], W("l2_down"), xT[s][:, :]).then_inc(l2_ct[s], 1)
                    mm(P[s][2][:, 0:256], W("l2_kr"), xT[s][:, :])
                    mm(P[s][2][:, 256:512], W("l2_krs"), xT[s][:, :]).then_inc(l2_kp[s], 1)

                def l2_up(s):
                    pe.wait_ge(l2_cts[s], l2_cts.at(c))
                    mm(P[s][3][:, 0:256], W("l2_qr"), at_ct[s])
                    mm(P[s][3][:, 256:512], W("l2_qrs"), at_ct[s])
                    mm(P[s][0][:, 0:256], W("l2_qc"), at_ct[s])
                    mm(P[s][0][:, 256:512], W("l2_kc"), at_ct[s]).then_inc(l2_qp[s], 1)
                    for t in range(2):
                        ins = mm(P[s][1][:, 128 * t:128 * t + 128], at_ct[s][:, 128 * t:128 * t + 128], W("l2_v"))
                    ins.then_inc(l2_v[s], 1)

                def stack(s, full):
                    for w, (hi, lo, names) in enumerate(((0, 1, ("sel_kh", "sel_kl")), (2, 3, ("sel_qh", "sel_ql")))):
                        for b in range(2):
                            bank = P[s][2 * w + b]
                            for j in (2 * b, 2 * b + 1):
                                o = bank[:, 256 * (j % 2):256 * (j % 2) + 256]
                                mm(o, CR(names[0], j), parts[s][:, hi, :], True, False)
                                ins = mm(o, CR(names[1], j), parts[s][:, lo, :], False, True)
                            ins.then_inc(full[s], 1)

                def l2_scores(s, i):
                    pe.wait_ge(l2_qm[s], l2_qm.at(c, i))
                    for j in range(4):
                        if i or j > 1:
                            r, k = ((l2_p, 4 * i - 2 + j) if j < 2 else (l2_su, 4 * i + j - 2))
                            pe.wait_ge(r[s], r.at(c, k))
                        for t in range(2):
                            ins = mm(P[s][(9 * i + j) % 2][:, 256 * t:256 * t + 256],
                                     qm[s][:, i % 2, j, 128 * t:128 * t + 128], kst[s][:, j, :])
                        ins.then_inc(l2_s[s], 1)

                def l2_max(s, i):
                    pe.wait_ge(l2_mtok[s], l2_mtok.at(c, i))
                    for t in range(2):
                        ins = pe.transpose(P[s][(9 * i + 4) % 2][0:4, 128 * t:128 * t + 128], m_tok[s][:, t, :], ident)
                    ins.then_inc(l2_m[s], 1)

                def l2_shifted(s, i):
                    for j in range(4):
                        if j == 0:
                            pe.wait_ge(l2_su[s], l2_su.at(c, 4 * i + 3))
                        if j == 1:
                            pe.wait_ge(l2_mu[s], l2_mu.at(c, i))
                        if j > 1:
                            pe.wait_ge(l2_p[s], l2_p.at(c, 4 * i + j - 2))
                        if j == 0:
                            pe.wait_ge(l2_mu[s], l2_mu.at(c, i))
                        for t in range(2):
                            o = P[s][(9 * i + 5 + j) % 2][:, 256 * t:256 * t + 256]
                            mm(o, kst[s][:, j, 128 * t:128 * t + 128], qm[s][:, i % 2, j, :], True, False)
                            ins = mm(o, CR("sel_max", j), mT[s], False, True)
                        ins.then_inc(l2_st[s], 1)

                def l2_values(s, i):
                    pe.wait_ge(l2_p[s], l2_p.at(c, 4 * i + 3))
                    o = P[s][2 + i // 2][:, 256 * (i % 2):256 * (i % 2) + 256]
                    for t in range(2):
                        for j in range(4):
                            ins = mm(o[32 * j:32 * j + 32, :], at_v[s][:, t, 4 * j + i, :],
                                     at_p[s][:, j, 256 * t:256 * t + 256], t == 0, t == 1)
                    ins.then_inc(l2_pv[s], 1)

                def sums(s, n, rows, src, done):
                    pe.wait_ge(src[s], src.at(c))
                    for t in range(2):
                        for i in range(n):
                            at = 4 * (n * t + i)
                            ins = mm(P[s][0][:, at:at + 4], at_o[s][:, i, 128 * t:128 * t + 128], C(rows)[:, 0:128:32])
                    ins.then_inc(done[s], 1)

                def spread(s, n, src, done):
                    pe.wait_ge(src[s], src.at(c))
                    for t in range(2):
                        for i in range(n):
                            at = 4 * (n * t + i)
                            o = P[s][i // 2][:, 256 * (i % 2) + 128 * t:256 * (i % 2) + 128 * t + 128]
                            for j in range(4):
                                ins = mm(o[32 * j:32 * j + 32, :], inverse[s][:, at + j:at + j + 1].to_broadcast([128, 32]), ident)
                    ins.then_inc(done[s], 1)

                def l2_out(s):
                    pe.wait_ge(l2_on[s], l2_on.at(c))
                    for t in range(2):
                        for i in range(4):
                            ins = mm(P[s][2][:, 128 * t:128 * t + 128], at_o[s][:, i, 128 * t:128 * t + 128],
                                     W("l2_o", 128 * i, 128 * i + 128), i == 0, i == 3)
                    ins.then_inc(l2_y[s], 1)

                def l3_project(s, L):
                    w = region_b[:, L * N_L3W:(L + 1) * N_L3W]
                    pe.wait_ge(s_wb, n_wb * c + 16)
                    for n, (t, k) in enumerate(((0, 0), (0, 1), (1, 0), (1, 1))):
                        mm(P[s][n][:, :], shT[s][:, 128 * t:128 * t + 128], w[:, 512 * k:512 * k + 512]).then_inc(l3_qkv[s], 1)

                def l3_project_v(s, L):
                    w = region_b[:, L * N_L3W + 1024:L * N_L3W + 1536]
                    for t, left in enumerate((l3_qin, l3_qnd)):
                        pe.wait_ge(left[s], left.at(c, 2 * L))
                        mm(P[s][t][:, :], shT[s][:, 128 * t:128 * t + 128], w).then_inc(l3_qkv[s], 1)

                def l3_pair(s, L, p):
                    if p == 0:
                        pe.wait_ge(l3_rot[s], l3_rot.at(c, 4 * L + 3))
                    else:
                        pe.wait_ge(l3_te[s], l3_te.at(c, 4 * L + p - 1))
                    for k in range(2):
                        for t in range(2):
                            ins = pe.transpose(P[s][3][:, 256 * k + 128 * t:256 * k + 128 * t + 128],
                                               l3_tok[s][:, k, t, 128 * p:128 * p + 128], ident)
                    ins.then_inc(l3_tp[s], 1)

                def l3_scores(s, L, h):
                    pe.wait_ge(l3_te[s], l3_te.at(c, 4 * L + h // 2))
                    if h == 0:
                        pe.wait_ge(l3_vin[s], l3_vin.at(c, 2 * L + 1))
                    if h > 1:
                        pe.wait_ge(l3_pte[s], l3_pte.at(c, 8 * L + h - 2))
                    q, k, o = qTm[s][:, h // 2 % 2, h % 2, :], l3_kT[s][:, h // 2 % 2, :], P[s][h % 2]
                    mm(o[:, 0:128], q[:, 0:128], k[:, 0:128])
                    mm(o[:, 128:384], q[:, 128:256], k).then_inc(l3_s[s], 1)

                def l3_turn(s, L, h):
                    pe.wait_ge(l3_e[s], l3_e.at(c, 8 * L + h))
                    for b in range(3):
                        ins = pe.transpose(P[s][h % 2][:, 128 * b:128 * b + 128], l3_sm[s][:, h % 2, 128 * b:128 * b + 128], ident)
                    ins.then_inc(l3_pt[s], 1)

                def l3_values(s, L, h):
                    pe.wait_ge(l3_pte[s], l3_pte.at(c, 8 * L + h))
                    if h == 4:
                        pe.wait_ge(l3_te[s], l3_te.at(c, 4 * L + 3))
                    at, pT, vh = 64 * (h % 4), l3_pT[s][:, h % 2, :], l3_v[s][:, :, 64 * h:64 * h + 64]
                    o = P[s][2 + h // 4]
                    mm(o[:, at:at + 64], pT[:, 0:128], vh[:, 0, :])
                    mm(o[:, 256 + at:320 + at], pT[:, 128:256], vh[:, 0, :], True, False)
                    ins = mm(o[:, 256 + at:320 + at], pT[:, 256:384], vh[:, 1, :], False, True)
                    if h % 4 == 3:
                        ins.then_inc(l3_o[s], 1)

                def l3_o_turn(s, L, g):
                    pe.wait_ge(l3_on[s], l3_on.at(c, 2 * L + g))
                    for j in range(2):
                        for t in range(2):
                            at = 128 * (2 * g + j)
                            ins = pe.transpose(P[s][2 + g][:, 256 * j + 128 * t:256 * j + 128 * t + 128],
                                               l3_o_tok[s][:, t, at:at + 128], ident)
                    ins.then_inc(l3_otp[s], 1)

                def l3_out(s, L):
                    at, _ = L3W["o"]
                    w = region_b[:, L * N_L3W + at:L * N_L3W + at + 512].rearrange("p (j d) -> p j d", j=4)
                    pe.wait_ge(l3_ot[s], l3_ot.at(c, 2 * L + 1))
                    for t in range(2):
                        for p in range(4):
                            ins = mm(P[s][2][:, 128 * t:128 * t + 128], l3_oT[s][:, p, 128 * t:128 * t + 128], w[:, p, :], p == 0, p == 3)
                    ins.then_inc(l3_y[s], 1)

                def l3_back(s, L):
                    for t in range(2):
                        ins = pe.transpose(P[s][1][:, 128 * t:128 * t + 128], shT[s][:, 128 * t:128 * t + 128], ident)
                    ins.then_inc(l3_hs[s], 1)

                def l3_normed(s, L):
                    pe.wait_ge(l3_hnd[s], l3_hnd.at(c, L))
                    for t in range(2):
                        ins = pe.transpose(P[s][2][:, 128 * t:128 * t + 128], l3_hn[s][:, t, :], ident)
                    ins.then_inc(l3_hnp[s], 1)

                def l3_ffn(s, L):
                    at, _ = L3W["w1"]
                    w = region_b[:, L * N_L3W + at:L * N_L3W + at + 2 * HID]
                    pe.wait_ge(l3_hnTd[s], l3_hnTd.at(c, L))
                    for f, (b, M) in enumerate(zip((0, 1, 3), FT)):
                        for k in range(2):
                            ins = mm(P[s][b][0:M, 256 * k:256 * k + 256], w[:, HID * k + 128 * f:HID * k + 128 * f + M], l3_hnT[s])
                        ins.then_inc(l3_z[s], 1)

                def l3_ffn_out(s, L):
                    at, _ = L3W["w2"]
                    w = region_b[:, L * N_L3W + at:L * N_L3W + at + 384].rearrange("p (j d) -> p j d", j=3)
                    pe.wait_ge(l3_h[s], l3_h.at(c, 3 * L + 2))
                    for t in range(2):
                        for f, M in enumerate(FT):
                            ins = mm(P[s][2][:, 128 * t:128 * t + 128], l3_hh[s][0:M, f, 128 * t:128 * t + 128], w[0:M, f, :], f == 0, f == 2)
                    ins.then_inc(l3_y2[s], 1)

                def l4_project(s):
                    mm(P[s][1][:, 0:256], W("l4_w", 128, 256), xT[s][:, :])
                    mm(P[s][1][:, 256:512], W("l4_w", 0, 128), xT[s][:, :])
                    for t in range(2):
                        ins = mm(P[s][2][:, 128 * t:128 * t + 128], xT[s][:, 128 * t:128 * t + 128], W("l4_w", 256, 384))
                    ins.then_inc(l4_p[s], 1)

                def l4_scores(s, i, j):
                    n = 4 * i + j
                    pe.wait_ge(l4_qm[s], l4_qm.at(c, i))
                    if n > 1:
                        pe.wait_ge(l4_sq[s], l4_sq.at(c, n - 2))
                    for t in range(2):
                        ins = mm(P[s][n % 2][:, 256 * t:256 * t + 256], kst[s][:, j, 128 * t:128 * t + 128], qm[s][:, i, j, :])
                    ins.then_inc(l4_st[s], 1)

                def l4_values(s, i):
                    pe.wait_ge(l4_sq[s], l4_sq.at(c, 4 * i + 3))
                    for t in range(2):
                        for j in range(4):
                            ins = mm(P[s][2][32 * j:32 * j + 32, 256 * i:256 * i + 256], l4_v[s][:, t, 2 * j + i, :],
                                     at_p[s][:, j, 256 * t:256 * t + 256], t == 0, t == 1)
                    ins.then_inc(l4_pv[s], 1)

                def l4_halves(s):
                    for i in range(2):
                        for j in range(4):
                            for t in range(2):
                                ins = mm(P[s][3][32 * j:32 * j + 32, i:i + 1], l4_v[s][:, t, 2 * j + i, :], C("half"), t == 0, t == 1)
                    ins.then_inc(l4_hs[s], 1)

                def l4_out(s):
                    pe.wait_ge(l4_on[s], l4_on.at(c))
                    for t in range(2):
                        for i in range(2):
                            ins = mm(P[s][3][:, 128 * t:128 * t + 128], at_o[s][:, i, 128 * t:128 * t + 128],
                                     W("l4_o", 128 * i, 128 * i + 128), i == 0, i == 1)
                    ins.then_inc(l4_y[s], 1)

                def L5(name, *dims):
                    at, n = L5W[name]
                    return region_a[:, at:at + n]

                def l5_gates(s):
                    pe.wait_ge(s_wa, n_wa * c + 32)
                    for f in range(4):
                        if f == 3:
                            pe.wait_ge(l5_h0[s], l5_h0.at(c, 0))
                        for k, w in enumerate(("w1", "w2")):
                            ins = mm(P[s][f % 3][:, 256 * k:256 * k + 256], L5(w)[:, 128 * f:128 * f + 128], xT[s][:, :])
                        ins.then_inc(l5_z[s], 1)

                def l5_hidden(s, w, src, n0, ready, last):
                    m = L5(w).rearrange("p (k o) -> p k o", k=4)
                    pe.wait_ge(ready[s], ready.at(c, ready.per_turn - 1))
                    for p in range(2):
                        n = n0 + p
                        if n > 5:
                            pe.wait_ge(last[s], last.at(c, n - 7))
                        for f in range(2):
                            for k in range(4):
                                ins = mm(P[s][n % 3][:, 256 * f:256 * f + 256],
                                         m[:, k, 128 * (2 * p + f):128 * (2 * p + f) + 128], src[s][:, k, :], k == 0, k == 3)
                        ins.then_inc(l5_z[s], 1)

                def l5_out(s):
                    m = L5("w3").rearrange("p (k o) -> p k o", k=4)
                    pe.wait_ge(l5_h2[s], l5_h2.at(c, 1))
                    for t in range(2):
                        for k in range(4):
                            ins = mm(P[s][3][:, 128 * t:128 * t + 128], l5_hC[s][:, k, 128 * t:128 * t + 128], m[:, k, :], k == 0, k == 3)
                    ins.then_inc(l5_yd[s], 1)

                def l6_project(s):
                    mm(P[s][0][:, 0:256], W("l6_q"), xT[s][:, :])
                    mm(P[s][0][:, 256:512], W("l6_k"), xT[s][:, :]).then_inc(l6_qk[s], 1)
                    l6_project_v(s, range(3))

                def l6_project_v(s, steps):
                    for n in steps:
                        t, k = divmod(n, 2)
                        if n == 3:
                            pe.wait_ge(l6_csd[s], l6_csd.at(c))
                        mm(P[s][(n + 1) % 4][:, :], xT[s][:, 128 * t:128 * t + 128], W("l6_v", 512 * k, 512 * k + 512)
                           ).then_inc(l6_vp[s], 1)

                def l6_denominator(s):
                    pe.wait_ge(l6_pr[s], l6_pr.at(c))
                    pe.wait_ge(l6_va[s], l6_va.at(c, 0))
                    mm(P[s][1][:, 0:256], C("pair_sum"), l6_prod[s]).then_inc(l6_dn[s], 1)

                def l6_scores(s, h):
                    if h == 0:
                        pe.wait_ge(l6_vd[s], l6_vd.at(c, 1))
                        pe.wait_ge(l6_va[s], l6_va.at(c, 1))
                    pe.wait_ge(l6_qm[s], l6_qm.at(c, h))
                    if h > 1:
                        pe.wait_ge(l6_atd[s], l6_atd.at(c, h - 2))
                    o, q = P[s][h % 2], qm6[s][:, h % 8, :]
                    mm(o[:, 0:256], k6[s][:, 0:128], q)
                    mm(o[:, 256:384], k6[s][:, 128:256], q[:, 128:256]).then_inc(l6_a[s], 1)

                def l6_values(s, h):
                    p = h // 2
                    pe.wait_ge(l6_atd[s], l6_atd.at(c, h))
                    if p > 1 and h % 2 == 0:
                        pe.wait_ge(l6_ot[s], l6_ot.at(c, p - 2))
                    o, a = P[s][2 + p % 2][64 * (h % 2):64 * (h % 2) + 64, :], l6_at[s][:, h % 4, :]
                    mm(o[:, 0:256], l6_v[s][:, 0, 64 * h:64 * h + 64], a[:, 0:256], True, False)
                    mm(o[:, 128:256], l6_v[s][:, 1, 64 * h:64 * h + 64], a[:, 256:384], False, True).then_inc(l6_o[s], 1)

                def l6_out(s):
                    pe.wait_ge(l6_ot[s], l6_ot.at(c, 7))
                    for t in range(2):
                        for p in range(8):
                            ins = mm(P[s][0][:, 128 * t:128 * t + 128], l6_oT[s][:, p, 128 * t:128 * t + 128],
                                     W("l6_o", 128 * p, 128 * p + 128), p == 0, p == 7)
                    ins.then_inc(l6_yd[s], 1)

                def l7(s):
                    n_e = 2 * I3 + 2 * D
                    for t in range(2):
                        ins = mm(P[s][3][:, 8 * t:8 * t + 8], xT[s][:, 128 * t:128 * t + 128], W("l7_gate"))
                    ins.then_inc(l7_lg[s], 1)
                    pe.wait_ge(s_wb, n_wb * c + 32)

                    def up(n):
                        e, f = divmod(n, 2)
                        if n >= 3:
                            pe.wait_ge(l7_h[s], l7_h.at(c, n - 3))
                        for k in range(2):
                            ins = mm(P[s][n % 3][:, 256 * k:256 * k + 256],
                                     region_b[:, e * n_e + I3 * k + 128 * f:e * n_e + I3 * k + 128 * f + 128], xT[s][:, :])
                        ins.then_inc(l7_z[s], 1)

                    def down(e):
                        pe.wait_ge(l7_h[s], l7_h.at(c, 2 * e + 1))
                        if e == 0:
                            pe.wait_ge(l7_lgb[s], l7_lgb.at(c))
                        else:
                            pe.wait_ge(l7_acc[s], l7_acc.at(c, e - 1))
                        for t in range(2):
                            for f in range(2):
                                ins = mm(P[s][3][:, 128 * t:128 * t + 128], ex_h[s][:, e % 2, f, 128 * t:128 * t + 128],
                                         region_b[:, e * n_e + 2 * I3 + D * f:e * n_e + 2 * I3 + D * f + D], f == 0, f == 1)
                        ins.then_inc(l7_y[s], 1)

                    up(0)
                    up(1)
                    for e in range(E3):
                        if e + 1 < E3:
                            up(2 * e + 2)
                            up(2 * e + 3)
                        down(e)

                for s in S2:
                    transpose_x(s, 0)
                    l0_project(s)
                for s in S2:
                    l0_state(s)
                for s in S2:
                    l0_read(s)
                if PHASES > 1:
                    for s in S2:
                        transpose_x(s, 1)
                        l1(s)
                if PHASES > 2:
                    for s in S2:
                        transpose_x(s, 2)
                        l2_down(s)
                    for s in S2:
                        l2_up(s)
                    for s in S2:
                        pe.wait_ge(l2_split[s], l2_split.at(c))
                        pe.wait_ge(l2_vs[s], l2_vs.at(c))
                        stack(s, st_full)
                    for s in S2:
                        pe.wait_ge(st_in[s], st_in.at(c, 3))
                    for i in range(4):
                        for s in S2:
                            l2_scores(s, i)
                        for s in S2:
                            l2_max(s, i)
                        for s in S2:
                            l2_shifted(s, i)
                        for s in S2:
                            l2_values(s, i)
                    for s in S2:
                        sums(s, 4, "rows8", l2_ob, l2_dn)
                    for s in S2:
                        spread(s, 4, l2_rb, l2_bc)
                    for s in S2:
                        l2_out(s)
                if PHASES > 3:
                    for L in range(2):
                        for s in S2:
                            transpose_x(s, 3 + 2 * L)
                            l3_project(s, L)
                        for s in S2:
                            l3_project_v(s, L)
                        for s in S2:
                            l3_pair(s, L, 0)
                        for h in range(LH + 2):
                            if h < LH:
                                for s in S2:
                                    l3_scores(s, L, h)
                            if 0 < h <= LH:
                                for s in S2:
                                    l3_turn(s, L, h - 1)
                            if h > 1:
                                for s in S2:
                                    l3_values(s, L, h - 2)
                            if h in L3_PAIR:
                                for s in S2:
                                    l3_pair(s, L, L3_PAIR[h])
                            if h == 7:
                                for s in S2:
                                    l3_o_turn(s, L, 0)
                        for s in S2:
                            l3_o_turn(s, L, 1)
                        for s in S2:
                            l3_out(s, L)
                        for s in S2:
                            transpose_x(s, 4 + 2 * L)
                            l3_back(s, L)
                        for s in S2:
                            l3_normed(s, L)
                        for s in S2:
                            l3_ffn(s, L)
                        for s in S2:
                            l3_ffn_out(s, L)
                if PHASES > 4:
                    for s in S2:
                        transpose_x(s, 7, l4_xn, l4_xnd)
                        l4_project(s)
                    for s in S2:
                        pe.wait_ge(l4_split[s], l4_split.at(c))
                        pe.wait_ge(l4_vd[s], l4_vd.at(c))
                        stack(s, l4_stf)
                    for s in S2:
                        pe.wait_ge(l4_stin[s], l4_stin.at(c, 3))
                        l4_halves(s)
                    for i in range(2):
                        for j in range(4):
                            for s in S2:
                                l4_scores(s, i, j)
                        for s in S2:
                            l4_values(s, i)
                    for s in S2:
                        sums(s, 2, "rows16", l4_oin, l4_dn)
                    for s in S2:
                        spread(s, 2, l4_rb, l4_bc)
                    for s in S2:
                        l4_out(s)
                if PHASES > 5:
                    for s in S2:
                        transpose_x(s, 8)
                        l5_gates(s)
                    for s in S2:
                        l5_hidden(s, "h1", l5_hA, 4, l5_h0, None)
                    for s in S2:
                        l5_hidden(s, "h2", l5_hB, 6, l5_h1, l5_h1)
                    for s in S2:
                        l5_out(s)
                if PHASES > 6:
                    for s in S2:
                        transpose_x(s, 9)
                        l6_project(s)
                    for s in S2:
                        l6_project_v(s, (3,))
                    for s in S2:
                        l6_denominator(s)
                    for h in range(H3 + 2):
                        for s in S2:
                            if h > 1:
                                l6_values(s, h - 2)
                            if h < H3:
                                l6_scores(s, h)
                    for s in S2:
                        l6_out(s)
                if PHASES > 7:
                    for s in S2:
                        transpose_x(s, 10)
                        l7(s)

        @block.scalar
        def _(act):
            act.wait_ge(s_const, 16)
            act.wait_ge(s_small, 16)
            with act.Fori(0, TURNS) as c:
                link = Links("act", act, c)

                def keep_xT(s, k):
                    act.wait_ge(xTp[s], xTp.at(c, k))
                    nc.scalar.copy(xT[s][:, :], P[s][0][:, 0:256]).then_inc(xT_ready[s], 1)

                def l0_exps(s):
                    act.wait_ge(l0_qkv[s], l0_qkv.at(c))
                    nc.scalar.activation(l0_e[s][:, 0, :], P[s][1][:, 0:256], ACT.Exp)
                    kv = P[s][2][:, :].rearrange("p (t w d) -> p t w d", t=2, w=2)
                    nc.scalar.activation(l0_e[s][:, 1, :].rearrange("p (t d) -> p t d", t=2), kv[:, :, 0, :], ACT.Exp)
                    nc.scalar.copy(l0_v[s][:, :, 0:128], kv[:, :, 1, :]).then_inc(l0_v_in[s], 1)

                def l1_relu(s):
                    for e in range(E0):
                        act.wait_ge(l1_z[s], l1_z.at(c, 2 * e))
                        if e >= 2:
                            act.wait_ge(l1_y[s], l1_y.at(c, e - 2))
                        for f in range(2):
                            ins = nc.scalar.activation(ex_h[s][:, e % 2, f, :], P[s][2 * e % 3][:, 256 * f:256 * f + 256],
                                                       ACT.Relu, bias=W("l1_b1", 4 * e + f, 4 * e + f + 1))
                        ins.then_inc(l1_ha[s], 1)
                    act.wait_ge(l1_mTp[s], l1_mTp.at(c))
                    nc.scalar.copy(ex_mT[s][0:8, :], P[s][0][0:8, 0:256]).then_inc(l1_mT[s], 1)

                def l2_latent(s):
                    act.wait_ge(l2_ct[s], l2_ct.at(c))
                    nc.scalar.activation(at_ct[s], P[s][1][:, 0:256], ACT.Identity, bias=W("l2_down_b")
                                         ).then_inc(l2_cts[s], 1)

                def keep_stacks(s):
                    for n in range(4):
                        act.wait_ge(st_full[s], st_full.at(c, n))
                        dst = (kst if n < 2 else qst)[s]
                        nc.scalar.copy(dst[:, 2 * (n % 2):2 * (n % 2) + 2, :],
                                       P[s][n][:, :].rearrange("p (j n) -> p j n", j=2)).then_inc(st_in[s], 1)

                def l2_exps(s, i):
                    for j in range(4):
                        act.wait_ge(l2_st[s], l2_st.at(c, 4 * i + j))
                        if i and j == 0:
                            act.wait_ge(l2_pv[s], l2_pv.at(c, i - 1))
                        nc.scalar.activation(at_p[s][:, j, :], P[s][(9 * i + 5 + j) % 2][:, :], ACT.Exp,
                                             scale=1.0 / 12.0).then_inc(l2_p[s], 1)

                def l2_keep_o(s):
                    act.wait_ge(l2_pv[s], l2_pv.at(c, 3))
                    for b in range(2):
                        ins = nc.scalar.copy(at_o[s][:, 2 * b:2 * b + 2, :],
                                             P[s][2 + b][:, :].rearrange("p (i n) -> p i n", i=2))
                    ins.then_inc(l2_ob[s], 1)

                def keep_shifted(s, k):
                    act.wait_ge(xTp[s], xTp.at(c, k))
                    nc.scalar.copy(shT[s][0:64, :], P[s][0][0:64, 0:256])
                    nc.scalar.copy(shT[s][64:128, 1:256], P[s][0][64:128, 0:255]).then_inc(xT_ready[s], 1)

                def l3_square(s, L, i):
                    act.wait_ge(l3_qkv[s], l3_qkv.at(c, 6 * L + i))
                    if i > 1:
                        act.wait_ge(l3_ss[s], l3_ss.at(c, 4 * L + i - 2))
                    nc.scalar.activation(l3_sq[s][:, i % 2, :], P[s][i][:, :], ACT.Square, scale=0.125).then_inc(l3_sqd[s], 1)

                def l3_keep_q(s, L, t):
                    if t:
                        act.wait_ge(l3_rot[s], l3_rot.at(c, 4 * L))
                    nc.scalar.copy(l3_qn[s][:, 0, :], P[s][2 * t][:, :]).then_inc(l3_qin[s], 1)

                def l3_keep_v(s, L):
                    for t in range(2):
                        act.wait_ge(l3_qkv[s], l3_qkv.at(c, 6 * L + 4 + t))
                        nc.scalar.copy(l3_v[s][:, t, :], P[s][t][:, :]).then_inc(l3_vin[s], 1)

                def l3_keep_pair(s, L, p):
                    act.wait_ge(l3_tp[s], l3_tp.at(c, 4 * L + p))
                    if p > 1:
                        act.wait_ge(l3_s[s], l3_s.at(c, 8 * L + 2 * p - 3))
                    nc.scalar.copy(qTm[s][0:64, p % 2, 0, :], P[s][3][0:64, 0:256])
                    nc.scalar.copy(qTm[s][64:128, p % 2, 1, :], P[s][3][64:128, 0:256])
                    nc.scalar.copy(l3_kT[s][:, p % 2, :], P[s][3][:, 256:512]).then_inc(l3_te[s], 1)

                def l3_exp(s, L, h):
                    act.wait_ge(l3_smd[s], l3_smd.at(c, 8 * L + h))
                    a = 96 + 2 * (h % 2)
                    for t, (lo, hi) in enumerate(((0, 128), (128, 384))):
                        b = l3_sm[s][:, h % 2, lo:hi]
                        ins = nc.scalar.activation(b, b, ACT.Exp, scale=-1.0, bias=tiny[s][:, a + t:a + t + 1],
                                                   accum_out=tiny[s][:, 128 + 8 * t + h:129 + 8 * t + h])
                    ins.then_inc(l3_e[s], 1)

                def l3_keep_oT(s, L, g):
                    act.wait_ge(l3_otp[s], l3_otp.at(c, 2 * L + g))
                    nc.scalar.copy(l3_oT[s][:, 2 * g:2 * g + 2, :], P[s][2 + g][:, :].rearrange("p (j n) -> p j n", j=2)
                                   ).then_inc(l3_ot[s], 1)

                def l3_affine(s, L):
                    act.wait_ge(l3_hnp[s], l3_hnp.at(c, L))
                    nc.scalar.activation(l3_hnT[s], P[s][2][:, 0:256], ACT.Identity, scale=W("l3_g", L, L + 1),
                                         bias=W("l3_b", L, L + 1)).then_inc(l3_hnTd[s], 1)

                def l3_gelu(s, L):
                    for f, (b, M) in enumerate(zip((0, 1, 3), FT)):
                        act.wait_ge(l3_z[s], l3_z.at(c, 3 * L + f))
                        k = 6 * L + 3 + f
                        nc.scalar.activation(l3_gl[s][0:M, f, :], P[s][b][0:M, 256:512], ACT.Gelu,
                                             bias=W("l3_b1", k, k + 1, rows=M)).then_inc(l3_gld[s], 1)

                def l4_keep_xT(s):
                    act.wait_ge(xTp[s], xTp.at(c, 7))
                    nc.scalar.mul(xT[s][:, :], P[s][0][:, 0:256], W("l4_gamma")).then_inc(xT_ready[s], 1)

                def l4_keep_stacks(s):
                    for n in range(4):
                        act.wait_ge(l4_stf[s], l4_stf.at(c, n))
                        dst = (kst if n < 2 else qst)[s]
                        nc.scalar.copy(dst[:, 2 * (n % 2):2 * (n % 2) + 2, :],
                                       P[s][n][:, :].rearrange("p (j n) -> p j n", j=2)).then_inc(l4_stin[s], 1)

                def l4_square(s, i, j):
                    n = 4 * i + j
                    act.wait_ge(l4_st[s], l4_st.at(c, n))
                    if i and j == 0:
                        act.wait_ge(l4_pv[s], l4_pv.at(c, i - 1))
                    nc.scalar.activation(at_p[s][:, j, :], P[s][n % 2][:, :], ACT.Square, scale=0.25 * 0.5 ** 0.5,
                                         bias=C("root_half")).then_inc(l4_sq[s], 1)

                def l4_keep_o(s):
                    act.wait_ge(l4_pv[s], l4_pv.at(c, 1))
                    act.wait_ge(l4_hsd[s], l4_hsd.at(c))
                    for i in range(2):
                        ins = nc.scalar.activation(at_o[s][:, i, :], P[s][2][:, 256 * i:256 * i + 256], ACT.Identity,
                                                   bias=tiny[s][:, 112 + i:113 + i])
                    ins.then_inc(l4_oin[s], 1)

                def l5_silu(s):
                    for f in range(4):
                        act.wait_ge(l5_z[s], l5_z.at(c, f))
                        if f > 1:
                            act.wait_ge(l5_h0[s], l5_h0.at(c, f - 2))
                        nc.scalar.activation(ex_g[s][:, f % 2, :], P[s][f % 3][:, 0:256], ACT.Silu,
                                             scale=W("l5_s1", f, f + 1)).then_inc(l5_sg[s], 1)

                def l5_gelu(s, n0, dst, scale, done):
                    for p in range(2):
                        act.wait_ge(l5_z[s], l5_z.at(c, n0 + p))
                        for f in range(2):
                            k = 2 * p + f
                            ins = nc.scalar.activation(dst[s][:, k, :], P[s][(n0 + p) % 3][:, 256 * f:256 * f + 256],
                                                       ACT.Gelu, scale=W(scale, k, k + 1))
                        ins.then_inc(done[s], 1)

                def l6_angles(s, step):
                    if step == 0:
                        act.wait_ge(l6_qk[s], l6_qk.at(c))
                        link(nc.scalar.activation(l6_th[s], P[s][0][:, :].rearrange("p (w n) -> p w n", w=2), ACT.Tanh))
                    else:
                        nc.scalar.activation(l6_cs[s], l6_th[s], ACT.Sin, scale=float(np.pi / 4),
                                             bias=C("half_pi")).then_inc(l6_csd[s], 1)

                def l6_keep_v(s):
                    for n in (0, 2):
                        act.wait_ge(l6_vp[s], l6_vp.at(c, n))
                        nc.scalar.copy(l6_v[s][:, n // 2, 0:512], P[s][n + 1][:, :]).then_inc(l6_va[s], 1)

                def l6_keep_o(s, p):
                    act.wait_ge(l6_o[s], l6_o.at(c, 2 * p + 1))
                    if p == 0:
                        act.wait_ge(l6_qkd[s], l6_qkd.at(c))
                    nc.scalar.copy(l6_oT[s][:, p, :], P[s][2 + p % 2][:, 0:256]).then_inc(l6_ot[s], 1)

                def l7_sigmoid(s):
                    act.wait_ge(l7_lgb[s], l7_lgb.at(c))
                    nc.scalar.activation(ex_m2[s], ex_log[s], ACT.Sigmoid).then_inc(l7_pr[s], 1)

                def l7_silu(s):
                    for n in range(18):
                        act.wait_ge(l7_z[s], l7_z.at(c, n))
                        if n > 1:
                            act.wait_ge(l7_h[s], l7_h.at(c, n - 2))
                        nc.scalar.activation(ex_g[s][:, n % 2, :], P[s][n % 3][:, 0:256], ACT.Silu).then_inc(l7_sg[s], 1)

                for s in S2:
                    keep_xT(s, 0)
                    l0_exps(s)
                if PHASES > 1:
                    for s in S2:
                        keep_xT(s, 1)
                        l1_relu(s)
                if PHASES > 2:
                    for s in S2:
                        keep_xT(s, 2)
                        l2_latent(s)
                    for s in S2:
                        keep_stacks(s)
                    for i in range(4):
                        for s in S2:
                            l2_exps(s, i)
                    for s in S2:
                        l2_keep_o(s)
                if PHASES > 3:
                    for L in range(2):
                        for s in S2:
                            keep_shifted(s, 3 + 2 * L)
                        for t in range(2):
                            for s in S2:
                                for w in range(2):
                                    l3_square(s, L, 2 * t + w)
                                    if w == 0:
                                        l3_keep_q(s, L, t)
                        for s in S2:
                            l3_keep_v(s, L)
                        for s in S2:
                            l3_keep_pair(s, L, 0)
                        for h in range(LH):
                            for s in S2:
                                l3_exp(s, L, h)
                            if h in L3_PAIR:
                                for s in S2:
                                    l3_keep_pair(s, L, L3_PAIR[h])
                        for g in range(2):
                            for s in S2:
                                l3_keep_oT(s, L, g)
                        for s in S2:
                            keep_shifted(s, 4 + 2 * L)
                        for s in S2:
                            l3_affine(s, L)
                        for s in S2:
                            l3_gelu(s, L)
                if PHASES > 4:
                    for s in S2:
                        l4_keep_xT(s)
                    for s in S2:
                        l4_keep_stacks(s)
                    for i in range(2):
                        for j in range(4):
                            for s in S2:
                                l4_square(s, i, j)
                    for s in S2:
                        l4_keep_o(s)
                if PHASES > 5:
                    for s in S2:
                        keep_xT(s, 8)
                        l5_silu(s)
                    for s in S2:
                        l5_gelu(s, 4, l5_hB, "l5_h1s", l5_h1)
                    for s in S2:
                        l5_gelu(s, 6, l5_hC, "l5_h2s", l5_h2)
                if PHASES > 6:
                    for s in S2:
                        keep_xT(s, 9)
                        l6_angles(s, 0)
                    for s in S2:
                        l6_angles(s, 1)
                    for s in S2:
                        l6_keep_v(s)
                    for p in range(8):
                        for s in S2:
                            l6_keep_o(s, p)
                if PHASES > 7:
                    for s in S2:
                        keep_xT(s, 10)
                        l7_sigmoid(s)
                        l7_silu(s)
                link.close()

        @block.vector
        def _(dve):
            v = nc.vector
            dve.wait_ge(s_const, 16)
            dve.wait_ge(s_small, 16)
            dve.wait_ge(s_stage, 16)
            v.tensor_copy(constr[:, :], scr[0][:, 0:N_CONSTR]).then_inc(s_constr, 1)
            for s in S2:
                v.memset(qTm[s][:, :, :, :], 0.0)
                ins = v.memset(shT[s][64:128, 0:1], 0.0)
            ins.then_inc(s_zd, 1)
            for L in range(2):
                for w in range(2):
                    for k in range(2):
                        at = ((2 * L + w) * 2 + k) * 64
                        v.tensor_tensor(xpos[:, L, w, k, :, :], C("xpos").rearrange("p (w k t d) -> p w k t d", w=2, k=2, t=2)[:, w, k, :, :],
                                        W("l3_scale", at, at + 64).unsqueeze(1).to_broadcast([128, 2, 64]), ALU.mult
                                        ).then_inc(s_xpos, 1)
            dve.wait_ge(s_xpos, 8)
            settled[dve] = sem("dve_settled")
            for s in S2:
                dve.sem_inc(x_ready[s], 1)
            with dve.Fori(0, TURNS) as c:
                link = Links("dve", dve, c)

                def spreads(s):
                    for t in range(2):
                        ins = v.bn_stats(stats[s][:, t, :], res[s][:, t, :])
                    link(ins)
                    settle(dve)
                    for t in range(2):
                        ins = v.bn_aggr(mv[s][:, t, :], stats[s][:, t, :])
                    link(ins)
                    v.tensor_scalar(ve[s][:, :], mv[s][:, :, 1], LN_EPS, None, ALU.add).then_inc(var_ready[s], 1)

                def normed(s, n):
                    dve.wait_ge(rstd_ready[s], rstd_ready.at(c, n))
                    for t in range(2):
                        ins = v.tensor_scalar(x[s][:, t, :], res[s][:, t, :], mv[s][:, t, 0:1], rstd[s][:, t:t + 1],
                                              ALU.subtract, ALU.mult)
                    ins.then_inc(x_ready[s], 1)

                def norm(n, total=None):
                    for s in S2:
                        if total:
                            total(s)
                        spreads(s)
                    for s in S2:
                        normed(s, n)

                def l0_elu(s):
                    dve.wait_ge(l0_v_in[s], l0_v_in.at(c))
                    v.tensor_scalar(l0_r[s][:, 0, :], P[s][1][:, 0:256], 0.0, None, ALU.max)
                    kv = P[s][2][:, :].rearrange("p (t w d) -> p t w d", t=2, w=2)
                    link(v.tensor_scalar(l0_r[s][:, 1, :].rearrange("p (t d) -> p t d", t=2), kv[:, :, 0, :], 0.0, None, ALU.max))
                    v.scalar_tensor_tensor(out=l0_r[s][:, 0:2, :], in0=l0_e[s][:, 0:2, :], scalar=1.0,
                                           in1=l0_r[s][:, 0:2, :], op0=ALU.min, op1=ALU.add).then_inc(l0_qk[s], 1)

                def l0_keep(s):
                    dve.wait_ge(l0_kv[s], l0_kv.at(c))
                    v.tensor_copy(l0_kvs[s][:, 0:129], P[s][3][:, 0:129]).then_inc(l0_kvs_in[s], 1)

                def l0_mix(s):
                    dve.wait_ge(l0_out[s], l0_out.at(c))
                    y = P[s][1][:, 0:258].rearrange("p (t d) -> p t d", t=2)
                    link(v.tensor_scalar(tiny[s][:, 0:2], y[:, :, 128], 1e-6, None, ALU.add))
                    link(v.reciprocal(tiny[s][:, 2:4], tiny[s][:, 0:2]))
                    for t in range(2):
                        ins = v.scalar_tensor_tensor(out=res[s][:, t, :], in0=y[:, t, 0:128], scalar=tiny[s][:, 2 + t:3 + t],
                                                     in1=x[s][:, t, :], op0=ALU.mult, op1=ALU.add)
                    link(ins)

                def l1_route(s):
                    dve.wait_ge(l1_lg[s], l1_lg.at(c))
                    lg = P[s][3][:, 0:16].rearrange("p (t e) -> p t e", t=2)
                    for t in range(2):
                        ins = v.tensor_tensor(ex_m2[s][:, t, :], lg[:, t, :], W("l1_gb"), ALU.add)
                    link(ins)
                    for t in range(2):
                        ins = v.tensor_tensor(ex_log[s][:, t, :], ex_m2[s][:, t, :], W("l1_eb"), ALU.add)
                    link(ins)
                    settle(dve)
                    for t in range(2):
                        ins = v.max(ex_mx[s][:, t, :], ex_log[s][:, t, :])
                    link(ins)
                    settle(dve)
                    for t in range(2):
                        ins = v.max_index(idx[s][:, t, :], ex_mx[s][:, t, :], ex_log[s][:, t, :])
                    link(ins)
                    link(v.tensor_copy(ex_ix[s][:, :, :], idx[s][:, :, :]))
                    for t in range(2):
                        ins = v.tensor_scalar(ex_mk[s][:, t, :], C("iota8"), ex_ix[s][:, t, 0:1], None, ALU.is_equal)
                    ins.then_inc(l1_mask[s], 1)
                    dve.wait_ge(l1_mask[s], l1_mask.at(c))

                def l1_relu(s, e):
                    dve.wait_ge(l1_z[s], l1_z.at(c, 2 * e + 1))
                    if e >= 2:
                        dve.wait_ge(l1_y[s], l1_y.at(c, e - 2))
                    for f in range(2):
                        ins = v.tensor_scalar(ex_h[s][:, e % 2, 2 + f, :], P[s][(2 * e + 1) % 3][:, 256 * f:256 * f + 256],
                                              W("l1_b1", 4 * e + 2 + f, 4 * e + 3 + f), 0.0, ALU.add, ALU.max)
                    ins.then_inc(l1_hd[s], 1)

                def l1_add(s, e):
                    dve.wait_ge(l1_y[s], l1_y.at(c, e))
                    if e:
                        dve.wait_ge(l1_acc[s], l1_acc.at(c, e - 1))
                    for t in range(2):
                        y = P[s][3][:, 128 * t:128 * t + 128]
                        if e < E0:
                            ins = v.scalar_tensor_tensor(out=res[s][:, t, :], in0=y, scalar=ex_mk[s][:, t, e:e + 1],
                                                         in1=(res if e else x)[s][:, t, :], op0=ALU.mult, op1=ALU.add)
                        else:
                            ins = v.tensor_tensor(res[s][:, t, :], y, res[s][:, t, :], ALU.add)
                    ins.then_inc(l1_acc[s], 1)

                def l1(s):
                    l1_route(s)
                    l1_relu(s, 0)
                    for e in range(E0):
                        if e + 1 < E0:
                            l1_relu(s, e + 1)
                        l1_add(s, e)
                    l1_add(s, E0)
                    dve.wait_ge(l1_acc[s], l1_acc.at(c, E0))

                def rope(s, pair, plain, b_r, b_rs, b_c, w, src_ready):
                    t = at_rope[s]
                    v.scalar_tensor_tensor(out=t[:, 3 * w, :], in0=pair[:, 0:256], scalar=W(b_r), in1=C("rope_c"),
                                           op0=ALU.add, op1=ALU.mult)
                    link(v.scalar_tensor_tensor(out=t[:, 3 * w + 1, :], in0=pair[:, 256:512], scalar=W(b_rs), in1=C("rope_s"),
                                                op0=ALU.add, op1=ALU.mult))
                    if src_ready is not None:
                        dve.wait_ge(src_ready[s], src_ready.at(c))
                    link(v.scalar_tensor_tensor(out=t[:, 3 * w + 2, :], in0=plain, scalar=W(b_c), in1=t[:, 3 * w, :],
                                                op0=ALU.add, op1=ALU.add))
                    link(v.tensor_tensor(at_kq[s][:, w, :], t[:, 3 * w + 2, :], t[:, 3 * w + 1, :], ALU.add))

                def split(s, n):
                    for w in range(2):
                        ins = v.tensor_copy(parts[s][:, 2 * w, :], at_kq[s][:, w, :])
                    link(ins)
                    for w in range(2):
                        ins = v.tensor_tensor(parts[s][:, 2 * w + 1, :], at_kq[s][:, w, :], f32(parts[s][:, 2 * w, :]), ALU.subtract)
                    return ins

                def l2_kq(s):
                    dve.wait_ge(l2_kp[s], l2_kp.at(c))
                    rope(s, P[s][2], P[s][0][:, 256:512], "l2_krb", "l2_krsb", "l2_kcb", 0, l2_qp)
                    rope(s, P[s][3], P[s][0][:, 0:256], "l2_qrb", "l2_qrsb", "l2_qcb", 1, None)
                    split(s, 0).then_inc(l2_split[s], 1)

                def l2_vals(s):
                    dve.wait_ge(l2_v[s], l2_v.at(c))
                    dve.wait_ge(l2_xb[s], l2_xb.at(c))
                    for t in range(2):
                        ins = v.tensor_tensor(at_v[s][:, t, :, 0:DH1],
                                              P[s][1][:, 128 * t:128 * t + 128].rearrange("p (h d) -> p h d", h=H1),
                                              W("l2_vb").rearrange("p (h d) -> p h d", h=H1), ALU.add)
                    ins.then_inc(l2_vs[s], 1)

                def l2_maxes(s, i):
                    for j in range(4):
                        dve.wait_ge(l2_s[s], l2_s.at(c, 4 * i + j))
                        if i and j == 0:
                            dve.wait_ge(l2_m[s], l2_m.at(c, i - 1))
                        ins = v.tensor_reduce(m_tok[s][:, :, j], P[s][(9 * i + j) % 2][:, :].rearrange("p (t k) -> p t k", t=2),
                                              X, ALU.max)
                        ins.then_inc(l2_su[s], 1)
                    dve.wait_ge(l2_su[s], l2_su.at(c, 4 * i + 3))
                    v.tensor_copy(tiny[s][:, 8:9], m_tok[s][:, 0, 0:1]).then_inc(l2_mtok[s], 1)

                def l2_max_rows(s, i):
                    dve.wait_ge(l2_m[s], l2_m.at(c, i))
                    if i:
                        dve.wait_ge(l2_st[s], l2_st.at(c, 4 * i - 1))
                    bank = P[s][(9 * i + 4) % 2]
                    link(v.tensor_copy(mT[s][0:4, :], bank[0:4, 0:256]))
                    v.tensor_tensor(mT[s][32:36, :], bank[0:4, 0:256], f32(mT[s][0:4, :]), ALU.subtract).then_inc(l2_mu[s], 1)

                def l2_recip(s):
                    dve.wait_ge(l2_dn[s], l2_dn.at(c))
                    v.reciprocal(inverse[s], P[s][0][:, 0:32]).then_inc(l2_rb[s], 1)

                def divide(s, n, src, done):
                    dve.wait_ge(src[s], src.at(c))
                    for b in range(n // 2):
                        o = at_o[s][:, 2 * b:2 * b + 2, :]
                        ins = v.tensor_tensor(o, o, P[s][b][:, :].rearrange("p (i n) -> p i n", i=2), ALU.mult)
                    ins.then_inc(done[s], 1)

                def l2_sum(s):
                    dve.wait_ge(l2_y[s], l2_y.at(c))
                    dve.wait_ge(l2_xb[s], l2_xb.at(c))
                    link(v.tensor_tensor(res[s][:, :, :], P[s][2][:, 0:256].rearrange("p (t d) -> p t d", t=2), at_xb[s], ALU.add))

                def l3_reduce(s, L, i):
                    dve.wait_ge(l3_sqd[s], l3_sqd.at(c, 4 * L + i))
                    v.tensor_reduce(tiny[s][:, 8 * i:8 * i + 8], l3_sq[s][:, i % 2, :].rearrange("p (h d) -> p h d", h=LH),
                                    X, ALU.add).then_inc(l3_ss[s], 1)

                def l3_clamp(s, L, t):
                    dve.wait_ge(l3_ss[s], l3_ss.at(c, 4 * L + 2 * t + 1))
                    q = tiny[s][:, 16 * t:16 * t + 16]
                    v.tensor_scalar(q, q, 1e-24 / 64, None, ALU.max).then_inc(l3_len[s], 1)

                def l3_unit(s, L, t):
                    dve.wait_ge(l3_rn[s], l3_rn.at(c, 2 * L + t))
                    if t:
                        dve.wait_ge(l3_ad[s], l3_ad.at(c, 4 * L + 1))
                    rn = tiny[s][:, 40 + 16 * t:48 + 16 * t].unsqueeze(2).to_broadcast([128, LH, LD])
                    v.tensor_tensor(l3_qn[s][:, 1, :].rearrange("p (h d) -> p h d", h=LH),
                                    P[s][2 * t + 1][:, :].rearrange("p (h d) -> p h d", h=LH), rn, ALU.mult).then_inc(l3_qnd[s], 1)

                def l3_sines(s, L, i):
                    t, w = divmod(i, 2)
                    done = l3_qnd if w else l3_qin
                    dve.wait_ge(done[s], done.at(c, 2 * L + t))
                    if i:
                        dve.wait_ge(l3_rot[s], l3_rot.at(c, 4 * L + i - 1))
                    qn = l3_qn[s][:, w, :].rearrange("p (h k d) -> p h k d", h=LH, k=2)
                    b = l3_b[s].rearrange("p (h k d) -> p h k d", h=LH, k=2)
                    for k in range(2):
                        sin = xpos[:, L, w, 1, t, 32 * k:32 * k + 32].unsqueeze(1).to_broadcast([128, LH, 32])
                        ins = v.tensor_tensor(b[:, :, k, :], qn[:, :, 1 - k, :], sin, ALU.mult)
                    return ins

                def l3_rotated(s, L, i):
                    t, w = divmod(i, 2)
                    dve.wait_ge(l3_ad[s], l3_ad.at(c, 4 * L + i))
                    v.tensor_tensor(l3_tok[s][:, w, t, :], l3_a[s], l3_b[s], ALU.add).then_inc(l3_rot[s], 1)

                def l3_mask(s, L, h):
                    dve.wait_ge(l3_s[s], l3_s.at(c, 8 * L + h))
                    a = 96 + 2 * (h % 2)
                    settle(dve)
                    for t, (lo, hi) in enumerate(((0, 128), (128, 384))):
                        ins = v.tensor_tensor_reduce(l3_sm[s][:, h % 2, lo:hi], P[s][h % 2][:, lo:hi], C("band", lo, hi),
                                                     tiny[s][:, 32 + 16 * t + h:33 + 16 * t + h], 3.0e38, ALU.add, ALU.min, tiny[s][:, a + t:a + t + 1])
                    ins.then_inc(l3_smd[s], 1)

                def l3_keep_pT(s, L, h):
                    dve.wait_ge(l3_pt[s], l3_pt.at(c, 8 * L + h))
                    v.tensor_copy(l3_pT[s][:, h % 2, :], P[s][h % 2][:, 0:384]).then_inc(l3_pte[s], 1)

                def l3_divide(s, L, g):
                    dve.wait_ge(l3_e[s], l3_e.at(c, 8 * L + 4 * g + 3))
                    total = tiny[s][:, 128:144].rearrange("p (t h) -> p t h", t=2)[:, :, 4 * g:4 * g + 4]
                    inverse = tiny[s][:, 144:160].rearrange("p (t h) -> p t h", t=2)[:, :, 4 * g:4 * g + 4]
                    link(v.reciprocal(inverse, total))
                    dve.wait_ge(l3_o[s], l3_o.at(c, 2 * L + g))
                    for t in range(2):
                        ins = v.tensor_tensor(l3_o_tok[s][:, t, 256 * g:256 * g + 256].rearrange("p (h d) -> p h d", h=4),
                                              P[s][2 + g][:, 256 * t:256 * t + 256].rearrange("p (h d) -> p h d", h=4),
                                              inverse[:, t, :].unsqueeze(2).to_broadcast([128, 4, LD]), ALU.mult)
                    ins.then_inc(l3_on[s], 1)

                def l3_mid(s, L):
                    dve.wait_ge(l3_y[s], l3_y.at(c, L))
                    if L == 0:
                        v.tensor_copy(res[s][:, :, :], x[s][:, :, :])
                    v.tensor_tensor(x[s][:, :, :], P[s][2][:, 0:256].rearrange("p (t d) -> p t d", t=2), x[s][:, :, :],
                                    ALU.add).then_inc(x_ready[s], 1)

                def l3_spreads(s, L):
                    dve.wait_ge(l3_hs[s], l3_hs.at(c, L))
                    for t in range(2):
                        ins = v.bn_stats(stats[s][:, t, :], P[s][1][:, 128 * t:128 * t + 128])
                    link(ins)
                    settle(dve)
                    for t in range(2):
                        ins = v.bn_aggr(mv[s][:, t, :], stats[s][:, t, :])
                    link(ins)
                    v.tensor_scalar(ve[s][:, :], mv[s][:, :, 1], LN_EPS, None, ALU.add).then_inc(var_ready[s], 1)

                def l3_norm(s, L):
                    dve.wait_ge(rstd_ready[s], rstd_ready.at(c, 3 + L))
                    for t in range(2):
                        ins = v.tensor_scalar(l3_hn[s][:, t, :], P[s][1][:, 128 * t:128 * t + 128], mv[s][:, t, 0:1],
                                              rstd[s][:, t:t + 1], ALU.subtract, ALU.mult)
                    ins.then_inc(l3_hnd[s], 1)

                def l3_glu(s, L):
                    for f, (b, M) in enumerate(zip((0, 1, 3), FT)):
                        dve.wait_ge(l3_gld[s], l3_gld.at(c, 3 * L + f))
                        k = 6 * L + f
                        v.scalar_tensor_tensor(out=l3_hh[s][0:M, f, :], in0=P[s][b][0:M, 0:256], scalar=W("l3_b1", k, k + 1, rows=M),
                                               in1=l3_gl[s][0:M, f, :], op0=ALU.add, op1=ALU.mult).then_inc(l3_h[s], 1)

                def l3_end(s, L):
                    dve.wait_ge(l3_y2[s], l3_y2.at(c, L))
                    dve.wait_ge(l3_xbd[s], l3_xbd.at(c, L))
                    y = P[s][2][:, 0:256].rearrange("p (t d) -> p t d", t=2)
                    if L == 0:
                        v.tensor_tensor(x[s][:, :, :], y, l3_xb[s], ALU.add).then_inc(x_ready[s], 1)
                    else:
                        link(v.tensor_tensor(res[s][:, :, :], y, l3_xb[s], ALU.add))

                def l4_sumsq(s):
                    dve.wait_ge(x_ready[s], x_ready.at(c, 6))
                    settle(dve)
                    for t in range(2):
                        ins = v.tensor_tensor_reduce(res[s][:, t, :], x[s][:, t, :], x[s][:, t, :], 1.0, 0.0, ALU.mult, ALU.add,
                                                     tiny[s][:, t:t + 1])
                    link(ins)
                    v.tensor_scalar(tiny[s][:, 2:4], tiny[s][:, 0:2], 1e-24, None, ALU.max).then_inc(l4_ss[s], 1)

                def l4_normed(s):
                    dve.wait_ge(l4_rn[s], l4_rn.at(c))
                    for t in range(2):
                        ins = v.tensor_scalar(l4_xn[s][:, t, :], x[s][:, t, :], tiny[s][:, 4 + t:5 + t], float(D) ** 0.5,
                                              ALU.mult, ALU.mult)
                    ins.then_inc(l4_xnd[s], 1)

                def l4_parts(s):
                    dve.wait_ge(l4_p[s], l4_p.at(c))
                    for w in range(2):
                        ins = v.tensor_copy(parts[s][:, 2 * w, :], P[s][1][:, 256 * w:256 * w + 256])
                    link(ins)
                    for w in range(2):
                        ins = v.tensor_tensor(parts[s][:, 2 * w + 1, :], P[s][1][:, 256 * w:256 * w + 256],
                                              f32(parts[s][:, 2 * w, :]), ALU.subtract)
                    ins.then_inc(l4_split[s], 1)
                    dve.wait_ge(l4_vset[s], l4_vset.at(c))
                    for t in range(2):
                        ins = v.tensor_copy(l4_v[s][:, t, :, 0:DH2], P[s][2][:, 128 * t:128 * t + 128].rearrange("p (h d) -> p h d", h=H2))
                    ins.then_inc(l4_vd[s], 1)

                def l4_halves(s):
                    dve.wait_ge(l4_hs[s], l4_hs.at(c))
                    v.tensor_copy(tiny[s][:, 112:114], P[s][3][:, 0:2]).then_inc(l4_hsd[s], 1)

                def l4_recip(s):
                    dve.wait_ge(l4_dn[s], l4_dn.at(c))
                    link(v.tensor_scalar(tiny[s][:, 120:136], P[s][0][:, 0:16], 1e-5, None, ALU.max))
                    v.reciprocal(inverse[s][:, 0:16], tiny[s][:, 120:136]).then_inc(l4_rb[s], 1)

                def l4_sum(s):
                    dve.wait_ge(l4_y[s], l4_y.at(c))
                    link(v.tensor_tensor(res[s][:, :, :], P[s][3][:, 0:256].rearrange("p (t d) -> p t d", t=2), x[s][:, :, :], ALU.add))

                def l5_gate(s):
                    for f in range(4):
                        dve.wait_ge(l5_sg[s], l5_sg.at(c, f))
                        v.scalar_tensor_tensor(out=l5_hA[s][:, f, :], in0=P[s][f % 3][:, 256:512], scalar=W("l5_s2", f, f + 1),
                                               in1=ex_g[s][:, f % 2, :], op0=ALU.mult, op1=ALU.mult).then_inc(l5_h0[s], 1)

                def l5_sum(s):
                    dve.wait_ge(l5_yd[s], l5_yd.at(c))
                    link(v.tensor_tensor(l5_y[s], P[s][3][:, 0:256].rearrange("p (t d) -> p t d", t=2),
                                         W("l5_s3").unsqueeze(1).to_broadcast([128, 2, 128]), ALU.mult))
                    link(v.tensor_tensor(res[s][:, :, :], l5_y[s], x[s][:, :, :], ALU.add))

                def l6_cumulate(s):
                    dve.wait_ge(l6_csd[s], l6_csd.at(c))
                    link(v.tensor_tensor_scan(l6_cum[s], C("ones"), l6_cs[s][:, 1, :], 0.0, ALU.mult, ALU.add))
                    v.tensor_tensor(l6_prod[s], l6_cum[s], l6_cs[s][:, 0, :], ALU.mult).then_inc(l6_pr[s], 1)

                def l6_keep_v(s):
                    for n in (1, 3):
                        dve.wait_ge(l6_vp[s], l6_vp.at(c, n))
                        v.tensor_copy(l6_v[s][:, n // 2, 512:1024], P[s][(n + 1) % 4][:, :]).then_inc(l6_vd[s], 1)

                def l6_parts(s):
                    v.tensor_copy(k6[s], l6_cs[s][:, 1, :])
                    dve.wait_ge(l6_dn[s], l6_dn.at(c))
                    link(v.tensor_scalar(l6_den[s], P[s][1][:, 0:256], 1e-6, None, ALU.add))
                    link(v.reciprocal(l6_rd[s], l6_den[s]))
                    link(v.tensor_tensor(l6_qn[s], l6_cs[s][:, 0, :], l6_rd[s], ALU.mult))
                    link(v.tensor_copy(q6[s], l6_qn[s]))
                    v.tensor_tensor(k6[s][64:128, :], l6_cs[s][64:128, 1, :], f32(k6[s][64:128, :]), ALU.subtract)
                    for a in (32, 96):
                        ins = v.tensor_tensor(q6[s][a:a + 32, :], l6_qn[s][a:a + 32, :], f32(q6[s][a:a + 32, :]), ALU.subtract)
                    ins.then_inc(l6_qkd[s], 1)

                def l6_causal(s, h):
                    dve.wait_ge(l6_a[s], l6_a.at(c, h))
                    if h > 3:
                        dve.wait_ge(l6_o[s], l6_o.at(c, h - 4))
                    v.tensor_tensor(l6_at[s][:, h % 4, :], P[s][h % 2][:, 0:384], C("tri"), ALU.mult).then_inc(l6_atd[s], 1)

                def l6_sum(s):
                    dve.wait_ge(l6_yd[s], l6_yd.at(c))
                    link(v.tensor_tensor(res[s][:, :, :], P[s][0][:, 0:256].rearrange("p (t d) -> p t d", t=2), x[s][:, :, :], ALU.add))

                def l7_route(s):
                    dve.wait_ge(l7_lg[s], l7_lg.at(c))
                    v.tensor_tensor(ex_log[s], P[s][3][:, 0:16].rearrange("p (t e) -> p t e", t=2),
                                    W("l7_rb").unsqueeze(1).to_broadcast([128, 2, 8]), ALU.add).then_inc(l7_lgb[s], 1)
                    dve.wait_ge(l7_pr[s], l7_pr.at(c))
                    settle(dve)
                    for t in range(2):
                        ins = v.max(ex_mx[s][:, t, :], ex_m2[s][:, t, :])
                    link(ins)
                    settle(dve)
                    for t in range(2):
                        ins = v.max_index(idx[s][:, t, :], ex_mx[s][:, t, :], ex_m2[s][:, t, :])
                    link(ins)
                    link(v.tensor_copy(ex_ix[s], idx[s][:, :, :]))
                    for t in range(2):
                        ins = v.tensor_scalar(ex_log[s][:, t, :], C("iota8"), ex_ix[s][:, t, 0:1], None, ALU.is_equal)
                    link(ins)
                    for t in range(2):
                        ins = v.scalar_tensor_tensor(out=ex_mx[s][:, t, :], in0=C("iota8"), scalar=ex_ix[s][:, t, 1:2],
                                                     in1=ex_log[s][:, t, :], op0=ALU.is_equal, op1=ALU.add)
                    link(ins)
                    link(v.tensor_tensor(ex_mk[s], ex_mx[s], ex_m2[s], ALU.mult))

                def l7_gate(s, n):
                    dve.wait_ge(l7_sg[s], l7_sg.at(c, n))
                    if n > 3:
                        dve.wait_ge(l7_y[s], l7_y.at(c, n // 2 - 2))
                    v.tensor_tensor(ex_h[s][:, n // 2 % 2, n % 2, :], P[s][n % 3][:, 256:512], ex_g[s][:, n % 2, :], ALU.mult
                                    ).then_inc(l7_h[s], 1)

                def l7_add(s, e):
                    dve.wait_ge(l7_y[s], l7_y.at(c, e))
                    if e:
                        dve.wait_ge(l7_acc[s], l7_acc.at(c, e - 1))
                    for t in range(2):
                        y = P[s][3][:, 128 * t:128 * t + 128]
                        if e:
                            ins = v.scalar_tensor_tensor(out=res[s][:, t, :], in0=y, scalar=ex_mk[s][:, t, e - 1:e],
                                                         in1=res[s][:, t, :], op0=ALU.mult, op1=ALU.add)
                        else:
                            ins = v.tensor_tensor(res[s][:, t, :], y, x[s][:, t, :], ALU.add)
                    ins.then_inc(l7_acc[s], 1)

                def l7(s):
                    l7_route(s)
                    for n in range(2):
                        l7_gate(s, n)
                    for e in range(E3):
                        if e + 1 < E3:
                            l7_gate(s, 2 * e + 2)
                            l7_gate(s, 2 * e + 3)
                        l7_add(s, e)
                    dve.wait_ge(l7_acc[s], l7_acc.at(c, E3 - 1))

                for s in S2:
                    l0_elu(s)
                for s in S2:
                    l0_keep(s)
                norm(0, l0_mix)
                if PHASES > 1:
                    for s in S2:
                        l1(s)
                        spreads(s)
                        normed(s, 1)
                if PHASES > 2:
                    for s in S2:
                        l2_kq(s)
                        l2_vals(s)
                    for i in range(4):
                        for s in S2:
                            l2_maxes(s, i)
                        for s in S2:
                            l2_max_rows(s, i)
                    for s in S2:
                        l2_recip(s)
                    for s in S2:
                        divide(s, 4, l2_bc, l2_on)
                    norm(2, l2_sum)
                if PHASES > 3:
                    for L in range(2):
                        for t in range(2):
                            for s in S2:
                                link(l3_sines(s, L, 2 * t))
                            for s in S2:
                                l3_reduce(s, L, 2 * t)
                                l3_reduce(s, L, 2 * t + 1)
                            for s in S2:
                                l3_clamp(s, L, t)
                            for s in S2:
                                l3_rotated(s, L, 2 * t)
                            for s in S2:
                                l3_unit(s, L, t)
                            for s in S2:
                                link(l3_sines(s, L, 2 * t + 1))
                            for s in S2:
                                l3_rotated(s, L, 2 * t + 1)
                        for h in range(LH + 1):
                            if h < LH:
                                for s in S2:
                                    l3_mask(s, L, h)
                            if h:
                                for s in S2:
                                    l3_keep_pT(s, L, h - 1)
                            if h == 6:
                                for s in S2:
                                    l3_divide(s, L, 0)
                        for s in S2:
                            l3_divide(s, L, 1)
                        for s in S2:
                            l3_mid(s, L)
                        for s in S2:
                            l3_spreads(s, L)
                        for s in S2:
                            l3_norm(s, L)
                        for s in S2:
                            l3_glu(s, L)
                        for s in S2:
                            l3_end(s, L)
                            if L:
                                spreads(s)
                    for s in S2:
                        normed(s, 5)
                if PHASES > 4:
                    for s in S2:
                        l4_sumsq(s)
                    for s in S2:
                        l4_normed(s)
                    for s in S2:
                        l4_parts(s)
                    for s in S2:
                        l4_halves(s)
                    for s in S2:
                        l4_recip(s)
                    for s in S2:
                        divide(s, 2, l4_bc, l4_on)
                    norm(6, l4_sum)
                if PHASES > 5:
                    for s in S2:
                        l5_gate(s)
                    norm(7, l5_sum)
                if PHASES > 6:
                    for s in S2:
                        l6_cumulate(s)
                    for s in S2:
                        l6_keep_v(s)
                    for s in S2:
                        l6_parts(s)
                    for h in range(H3):
                        for s in S2:
                            l6_causal(s, h)
                    norm(8, l6_sum)
                if PHASES > 7:
                    for s in S2:
                        l7(s)
                        spreads(s)
                        normed(s, 9)
                link.close()

        @block.gpsimd
        def _(pool):
            g = nc.gpsimd
            pool.wait_ge(s_const, 16)
            pool.wait_ge(s_small, 16)
            for s in S2:
                ins = g.memset(f32(mT[s]), 0.0)
            ins.then_inc(s_zero, 1)
            pool.wait_ge(s_constr, 1)
            settled[pool] = sem("pool_settled")
            with pool.Fori(0, TURNS) as c:
                link = Links("pool", pool, c)

                def rsqrt(s, n):
                    pool.wait_ge(var_ready[s], var_ready.at(c, n))
                    g.tensor_tensor(rstd[s][:, :], ve[s][:, :], C("mhalf", 0, 2), ALU.pow).then_inc(rstd_ready[s], 1)

                def l2_prepare(s):
                    pool.wait_ge(x_ready[s], x_ready.at(c, X_OF[2]))
                    g.tensor_tensor(at_xb[s], x[s][:, :, :], W("l2_ob").unsqueeze(1).to_broadcast([128, 2, 128]), ALU.add)
                    link(g.memset(at_v[s], 0.0))
                    settle(pool)
                    g.memset(at_v[s][:, :, :, DH1:DH1 + 1], 1.0).then_inc(l2_xb[s], 1)

                def l2_masked(s, i):
                    if i == 0:
                        pool.wait_ge(st_in[s], st_in.at(c, 3))
                    if i >= 2:
                        pool.wait_ge(l2_st[s], l2_st.at(c, 4 * (i - 2) + 3))
                    settle(pool)
                    g.tensor_scalar(qm[s][:, i % 2, :, :], f32(qst[s]), C("mask2", i, i + 1), None, ALU.mult).then_inc(l2_qm[s], 1)

                def l3_norms(s, L, t):
                    pool.wait_ge(l3_len[s], l3_len.at(c, 2 * L + t))
                    g.tensor_tensor(tiny[s][:, 32 + 16 * t:48 + 16 * t], tiny[s][:, 16 * t:16 * t + 16], C("mhalf"), ALU.pow
                                    ).then_inc(l3_rn[s], 1)

                def l3_cos(s, L, i):
                    t, w = divmod(i, 2)
                    done = l3_qnd if w else l3_qin
                    pool.wait_ge(done[s], done.at(c, 2 * L + t))
                    if i:
                        pool.wait_ge(l3_rot[s], l3_rot.at(c, 4 * L + i - 1))
                    cos = xpos[:, L, w, 0, t, :].unsqueeze(1).to_broadcast([128, LH, LD])
                    g.tensor_tensor(l3_a[s].rearrange("p (h d) -> p h d", h=LH), l3_qn[s][:, i % 2, :].rearrange("p (h d) -> p h d", h=LH),
                                    cos, ALU.mult).then_inc(l3_ad[s], 1)

                def l3_bias(s, L):
                    pool.wait_ge(x_ready[s], x_ready.at(c, 3 + 2 * L))
                    ins = g.tensor_tensor(l3_xb[s], x[s][:, :, :], W("l3_b2", 128 * L, 128 * L + 128).unsqueeze(1).to_broadcast([128, 2, 128]),
                                          ALU.add)
                    if L:
                        link(ins)
                        ins = g.tensor_tensor(l3_xb[s], l3_xb[s], res[s][:, :, :], ALU.add)
                    ins.then_inc(l3_xbd[s], 1)

                def l4_norms(s):
                    pool.wait_ge(l4_ss[s], l4_ss.at(c))
                    g.tensor_tensor(tiny[s][:, 4:6], tiny[s][:, 2:4], C("mhalf", 0, 2), ALU.pow).then_inc(l4_rn[s], 1)
                    link(g.memset(l4_v[s], 0.0))
                    settle(pool)
                    g.memset(l4_v[s][:, :, :, DH2:DH2 + 1], 1.0).then_inc(l4_vset[s], 1)

                def l4_masked(s, i):
                    if i == 0:
                        pool.wait_ge(l4_stin[s], l4_stin.at(c, 3))
                    settle(pool)
                    g.tensor_scalar(qm[s][:, i, :, :], f32(qst[s]), C("mask4", i, i + 1), None, ALU.mult).then_inc(l4_qm[s], 1)

                def l6_masked(s, h):
                    if h == 0:
                        pool.wait_ge(l6_qkd[s], l6_qkd.at(c))
                    if h > 7:
                        pool.wait_ge(l6_a[s], l6_a.at(c, h - 8))
                    settle(pool)
                    g.tensor_scalar(qm6[s][:, h % 8, :], f32(q6[s]), C("mask6", h, h + 1), None, ALU.mult).then_inc(l6_qm[s], 1)

                for s in S2:
                    pool.wait_ge(out_done[s], out_done.at(c, -1))
                    settle(pool)
                    g.memset(l0_v[s][:, :, 128:129], 1.0).then_inc(l0_ones[s], 1)
                for s in S2:
                    rsqrt(s, 0)
                if PHASES > 1:
                    for s in S2:
                        rsqrt(s, 1)
                if PHASES > 2:
                    for s in S2:
                        l2_prepare(s)
                    for i in range(4):
                        for s in S2:
                            l2_masked(s, i)
                    for s in S2:
                        rsqrt(s, 2)
                if PHASES > 3:
                    for L in range(2):
                        for t in range(2):
                            for s in S2:
                                l3_cos(s, L, 2 * t)
                            for s in S2:
                                l3_norms(s, L, t)
                            for s in S2:
                                l3_cos(s, L, 2 * t + 1)
                        for s in S2:
                            l3_bias(s, L)
                            rsqrt(s, 3 + L)
                    for s in S2:
                        rsqrt(s, 5)
                if PHASES > 4:
                    for s in S2:
                        l4_norms(s)
                    for i in range(2):
                        for s in S2:
                            l4_masked(s, i)
                    for s in S2:
                        rsqrt(s, 6)
                if PHASES > 5:
                    for s in S2:
                        rsqrt(s, 7)
                if PHASES > 6:
                    for h in range(H3):
                        for s in S2:
                            l6_masked(s, h)
                    for s in S2:
                        rsqrt(s, 8)
                if PHASES > 7:
                    for s in S2:
                        rsqrt(s, 9)
                link.close()


def pack(a):
    f = np.float32
    small = np.zeros((128, N_SMALL), f)

    def put(name, v, rows=128):
        at, n = SMALL[name]
        small[:rows, at:at + n] = np.asarray(v, f).reshape(rows, n)

    def bc(v):
        return np.broadcast_to(np.asarray(v, f).reshape(1, -1), (128, np.size(v)))

    put("l0_w", a["L0_attn_W"])
    put("l1_gate", a["L0_ffn_gate_w"].T)
    put("l1_gb", bc(a["L0_ffn_gate_b"]))
    put("l1_eb", bc(a["L0_ffn_expert_bias"]))
    put("l1_b1", a["L0_ffn_b1"].reshape(E0, 4, 128).transpose(2, 0, 1))
    put("l1_b2", a["L0_ffn_b2"], 8)
    l1 = np.concatenate([a["L0_ffn_w1"].transpose(1, 0, 2).reshape(128, -1),
                         a["L0_ffn_w2"].reshape(E0, 4, 128, D).transpose(2, 0, 1, 3).reshape(128, -1)], 1)
    swap = np.arange(128) ^ 1
    q_rows = lambda w: np.concatenate([w, np.zeros((64, w.shape[1]), f)], 0)
    kv_rows = lambda w: np.concatenate([np.zeros((64, w.shape[1]), f), w], 0)
    put("l2_down", np.concatenate([a["L1_attn_Wd_q_w"], a["L1_attn_Wd_kv_w"]], 1))
    put("l2_down_b", np.concatenate([a["L1_attn_Wd_q_b"], a["L1_attn_Wd_kv_b"]]))
    put("l2_qc", q_rows(a["L1_attn_Wu_q_w"]))
    put("l2_qr", q_rows(a["L1_attn_Wq_r_w"]))
    put("l2_qrs", q_rows(a["L1_attn_Wq_r_w"][:, swap]))
    put("l2_kc", kv_rows(a["L1_attn_Wu_k_w"]))
    put("l2_kr", a["L1_attn_Wk_r_w"])
    put("l2_krs", a["L1_attn_Wk_r_w"][:, swap])
    put("l2_v", kv_rows(a["L1_attn_Wu_v_w"]))
    put("l2_qcb", a["L1_attn_Wu_q_b"])
    put("l2_qrb", a["L1_attn_Wq_r_b"])
    put("l2_qrsb", a["L1_attn_Wq_r_b"][swap])
    put("l2_kcb", a["L1_attn_Wu_k_b"])
    put("l2_krb", a["L1_attn_Wk_r_b"])
    put("l2_krsb", a["L1_attn_Wk_r_b"][swap])
    put("l2_vb", bc(a["L1_attn_Wu_v_b"]))
    put("l2_ob", bc(a["L1_attn_Wo_b"]))
    o = np.zeros((4, 32, 4, D), f)
    o[:, 0:DH1] = a["L1_attn_Wo_w"].reshape(4, 4, DH1, D).transpose(0, 2, 1, 3)
    put("l2_o", o)
    l3 = np.zeros((128, 2, N_L3W), f)
    for L in range(2):
        at, n = L3W["qkv"]
        l3[:, L, at:at + n] = a["L1_ffn_wqkv"][L]
        at, n = L3W["o"]
        l3[:, L, at:at + n] = a["L1_ffn_wo"][L].reshape(4, 128, D).transpose(1, 0, 2).reshape(128, -1)
        at, n = L3W["w1"]
        l3[:, L, at:at + n] = a["L1_ffn_w1"][L]
        at, n = L3W["w2"]
        w2 = np.zeros((3, 128, D), f)
        w2.reshape(384, D)[0:HID] = a["L1_ffn_w2"][L]
        l3[:, L, at:at + n] = w2.transpose(1, 0, 2).reshape(128, -1)
    put("l3_g", a["L1_ffn_ln_g"].T)
    put("l3_b", a["L1_ffn_ln_b"].T)
    b1 = np.zeros((2, 2, 384), f)
    b1[:, :, 0:HID] = a["L1_ffn_b1"].reshape(2, 2, HID)
    put("l3_b1", b1.reshape(2, 2, 3, 128).transpose(3, 0, 1, 2))
    put("l3_b2", bc(a["L1_ffn_b2"]))
    rot = (np.arange(LD) + LD // 2) % LD
    qk = np.stack([a["L1_ffn_q_scale"], a["L1_ffn_k_scale"]], 1)
    put("l3_scale", bc(np.stack([qk, qk[:, :, rot]], 2)))
    put("l4_gamma", a["L2_attn_gamma"])
    put("l4_w", np.concatenate([a["L2_attn_w_q"], a["L2_attn_w_kv"]], 1))
    o = np.zeros((4, 32, 2, D), f)
    o[:, 0:DH2] = a["L2_attn_w_out"].reshape(4, 2, DH2, D).transpose(0, 2, 1, 3)
    put("l4_o", o)
    blocks = lambda w: w.T.reshape(w.shape[1] // 128, 128, w.shape[0]).transpose(1, 0, 2).reshape(128, -1)
    l5 = np.concatenate([blocks(a[f"L2_ffn_{n}_w"]) for n in ("w1", "w2", "h1", "h2", "w3")], 1)
    for n, k in (("l5_s1", "w1"), ("l5_s2", "w2"), ("l5_h1s", "h1"), ("l5_h2s", "h2")):
        put(n, a[f"L2_ffn_{k}_s"].reshape(4, 128).T)
    put("l5_s3", bc(a["L2_ffn_w3_s"]))
    wq, wk = a["L3_attn_W_Q"][:, :, 0].T, a["L3_attn_W_K"][:, :, 0].T
    put("l6_q", np.concatenate([wq] * 8, 1))
    put("l6_k", np.concatenate([wk] * 8, 1))
    put("l6_v", a["L3_attn_W_V"].transpose(1, 0, 2))
    put("l6_o", a["L3_attn_W_O"].transpose(2, 1, 0).reshape(8, 128, D).transpose(1, 0, 2))
    wg = np.concatenate([a["L3_ffn_Wg_s"][None], a["L3_ffn_Wg"]], 0)
    wu = np.concatenate([a["L3_ffn_Wu_s"][None], a["L3_ffn_Wu"]], 0)
    wd = np.concatenate([a["L3_ffn_Wd_s"][None], a["L3_ffn_Wd"]], 0)
    l7 = np.concatenate([wg.transpose(2, 0, 1), wu.transpose(2, 0, 1),
                         wd.transpose(0, 2, 1).reshape(E3, 2, 128, D).transpose(2, 0, 1, 3).reshape(128, E3, 2 * D)],
                        2).reshape(128, -1)
    put("l7_gate", a["L3_ffn_Wr"].T)
    put("l7_rb", bc(a["L3_ffn_rb"]))
    const, constr = shape_constants()
    out = dict(x=a["L0_attn_x"], small=small, l1=l1, l3=l3.reshape(128, -1), l5=l5, l7=l7, const=const, constr=constr)
    return {k: np.ascontiguousarray(v, f) for k, v in out.items()}


LINKS = {"act": 2, "dve": 144, "pool": 6}


def kernel(**inputs):
    import concourse.bacc as bacc
    from concourse.bass_utils import run_bass_kernel_spmd

    nc = bacc.Bacc("TRN2", target_bir_lowering=False, num_devices=1)
    arrays = pack({k: np.asarray(v) for k, v in inputs.items()})
    args = [nc.dram_tensor(f"in_{k}", v.shape, F32, kind="ExternalInput").ap() for k, v in arrays.items()]
    out = nc.dram_tensor("out", (NSEQ, SEQ, D), F32, kind="ExternalOutput").ap()
    build(nc, *args, out, LINKS)
    r = run_bass_kernel_spmd(nc, [{f"in_{k}": v for k, v in arrays.items()}], core_ids=[0])
    return r.results[0]["out"]
```

```python
from contextlib import ExitStack

import concourse.bass as bass
from concourse import mybir
import numpy as np

F32 = mybir.dt.float32
F32R = mybir.dt.float32r
U32 = mybir.dt.uint32
ALU = mybir.AluOpType
ACT = mybir.ActivationFunctionType
X = mybir.AxisListType.X

D = 128
SEQ = 256
NSEQ = 8
STREAMS = 2
TURNS = NSEQ // STREAMS
LN_EPS = 1e-5

E0, F0 = 8, 512
H1, DH1 = 16, 8
LH, LD, HID, WIN = 8, 64, 341, 64
FT = [128, 128, 85]
L3_PAIR = {1: 1, 2: 2, 4: 3}
H2, DH2 = 8, 16
H3, DH3 = 16, 64
E3, I3 = 9, 256


def columns(parts):
    at, out = 0, {}
    for name, n in parts:
        out[name] = (at, n)
        at += n
    return out, at


SMALL, N_SMALL = columns([
    ("l0_w", 384),
    ("l1_gate", E0), ("l1_gb", E0), ("l1_eb", E0), ("l1_b1", E0 * 4), ("l1_b2", D),
    ("l3_scale", 2 * 4 * 64),
    ("l2_down", 128), ("l2_down_b", 1), ("l2_qc", 128), ("l2_qr", 128), ("l2_qrs", 128),
    ("l2_kc", 128), ("l2_kr", 128), ("l2_krs", 128), ("l2_v", 128), ("l2_o", 4 * 128),
    ("l2_qcb", 1), ("l2_qrb", 1), ("l2_qrsb", 1), ("l2_kcb", 1), ("l2_krb", 1), ("l2_krsb", 1),
    ("l2_vb", 128), ("l2_ob", 128),
    ("l3_g", 2), ("l3_b", 2), ("l3_b1", 12), ("l3_b2", 2 * 128),
    ("l4_gamma", 1), ("l4_w", 384), ("l4_o", 2 * 128),
    ("l5_s1", 4), ("l5_s2", 4), ("l5_h1s", 4), ("l5_h2s", 4), ("l5_s3", 128),
    ("l6_q", 128), ("l6_k", 128), ("l6_v", 1024), ("l6_o", 1024),
    ("l7_gate", 8), ("l7_rb", 8),
])
N_FIRST = SMALL["l2_down"][0]
L3W, N_L3W = columns([("qkv", 1536), ("o", 512), ("w1", 2 * HID), ("w2", 3 * 128)])
L5W, N_L5W = columns([("w1", 512), ("w2", 512), ("h1", 2048), ("h2", 2048), ("w3", 512)])
N_L1W = E0 * (F0 + F0)
N_L7W = E3 * (2 * I3 + 2 * D)
N_REGION_A = max(N_L1W, N_L5W)
N_REGION_B = max(2 * N_L3W, N_L7W)
CONST, N_CONST = columns([
    ("ident", 128), ("iota8", 8), ("rope_c", 256), ("rope_s", 256), ("tri", 384), ("band", 384),
    ("xpos", 512), ("mask2", 4), ("mask4", 2), ("mask6", 16), ("half_pi", 1), ("mhalf", 16), ("ones", 256),
    ("rows8", 128), ("rows16", 128), ("pair_sum", 128), ("half", 1), ("root_half", 1),
])
CONSTR, N_CONSTR = columns([("sel_qh", 512), ("sel_ql", 512), ("sel_kh", 512), ("sel_kl", 512), ("sel_max", 512)])


def shape_constants():
    f = np.float32
    c = np.zeros((128, N_CONST), f)
    cr = np.zeros((128, N_CONSTR), f)
    p = np.arange(128)

    def put(name, a):
        at, n = CONST[name]
        c[:, at:at + n] = np.asarray(a, f).reshape(128, n)

    put("ident", np.eye(128))
    put("iota8", np.tile(np.arange(8), (128, 1)))
    theta = f(10000.0) ** (f(-2.0) * np.arange(64, dtype=f)) / f(64)
    r = np.arange(SEQ, dtype=f)[None, :] * theta[p // 2][:, None]
    put("rope_c", np.cos(r))
    put("rope_s", np.sin(r) * np.where(p % 2 == 0, -1, 1)[:, None])
    tri = (p[None, :] >= p[:, None]).astype(f)
    put("tri", np.concatenate([tri, np.ones((128, 128)), tri], 1))
    band = np.zeros((128, 384), f)
    for t, at, n in ((0, 0, 128), (1, 128, 256)):
        i = t * 128 + p[:, None]
        j = np.arange(n)[None, :]
        band[:, at:at + n] = np.where((i < j) | (i > j + WIN), f(1e25), f(0))
    put("band", band)
    half = np.arange(0, LD, 2, dtype=f)
    inv = f(1.0) / f(10000.0) ** (half / f(LD))
    t = np.arange(SEQ, dtype=f)
    fr = np.concatenate([t[:, None] * inv[None, :]] * 2, 1)
    base = (half + f(0.4 * LD)) / f(1.4 * LD)
    sc = base[None, :] ** ((t - SEQ // 2) / f(WIN // 2))[:, None]
    sc = np.concatenate([sc, sc], 1)
    sign = np.where(np.arange(LD) < LD // 2, -1, 1)[None, :]
    tabs = [[np.cos(fr) * sc, np.sin(fr) * sc * sign], [np.cos(fr) / sc * f(-0.125), np.sin(fr) / sc * sign * f(-0.125)]]
    x = np.zeros((128, 2, 2, 2, 64), f)
    for w in range(2):
        for k in range(2):
            x[:, w, k] = tabs[w][k].reshape(2, 128, 64).transpose(1, 0, 2)
    put("xpos", x)
    put("mask2", (p % 32 // DH1)[:, None] == np.arange(4)[None])
    put("mask4", (p % 32 // DH2)[:, None] == np.arange(2)[None])
    put("mask6", (p % 16)[:, None] == np.arange(16)[None])
    put("half_pi", np.where(p % 32 < 16, np.pi / 2, 0))
    put("mhalf", np.full((128, 16), -0.5))
    put("ones", np.ones((128, 256)))
    put("rows8", (p[:, None] == (p // 32 * 32 + DH1)[None, :]))
    put("rows16", (p[:, None] == (p // 32 * 32 + DH2)[None, :]))
    put("pair_sum", (p[:, None] < 32) & (p[:, None] % 16 == p[None, :] % 16))
    put("half", np.full((128, 1), 0.5))
    put("root_half", np.full((128, 1), 0.5 ** 0.5))
    for name, quads in (("sel_qh", (0, 2)), ("sel_ql", (1, 3)), ("sel_kh", (0, 1)), ("sel_kl", (2, 3))):
        at = CONSTR[name][0]
        for j in range(4):
            for q in quads:
                for k in range(32):
                    cr[32 * j + k, at + 128 * j + 32 * q + k] = 1
    at = CONSTR["sel_max"][0]
    for j in range(4):
        cr[j, at + 128 * j:at + 128 * (j + 1)] = -1
        cr[32 + j, at + 128 * j:at + 128 * (j + 1)] = -1
    return c, cr


SHARED = {
    "pe_input": ("l0_qkv", "l1_lg", "l2_ct", "l3_qkv", "l4_p", "l6_qk", "l7_lg"),
    "pe_second": ("l0_kv", "l1_mTp", "l2_kp", "l3_tp", "l4_hs", "l5_yd", "l6_dn"),
    "pe_hidden": ("l1_z", "l3_z", "l5_z", "l7_z"),
    "pe_values": ("l2_qp", "l3_otp", "l6_vp"),
    "pe_values2": ("l2_v", "l3_hs", "l4_bc"),
    "pe_stack": ("st_full", "l3_pt", "l4_stf"),
    "pe_scores": ("l2_s", "l3_s", "l6_a"),
    "pe_maxima": ("l2_m", "l3_hnp"),
    "pe_scoresT": ("l2_st", "l4_st"),
    "pe_weighted": ("l2_pv", "l3_o", "l4_pv", "l6_o"),
    "pe_spread": ("l2_bc", "l3_y2"),
    "pe_output": ("l0_out", "l1_y", "l2_y", "l3_y", "l4_y", "l6_yd", "l7_y"),
    "act_moved": ("l0_v_in", "l1_mT", "l2_cts", "l3_vin", "l4_oin", "l6_csd"),
    "act_stack": ("st_in", "l3_te", "l4_stin", "l5_sg", "l6_va"),
    "act_hidden": ("l1_ha", "l3_gld", "l5_h1", "l7_sg"),
    "act_probs": ("l2_p", "l3_e", "l4_sq", "l5_h2"),
    "act_out": ("l2_ob", "l3_ot", "l6_ot", "l7_pr"),
    "act_squares": ("l3_sqd",),
    "act_normedT": ("l3_hnTd",),
    "dve_first": ("l0_qk", "l1_mask", "l2_split", "l3_ss", "l4_ss", "l6_pr", "l7_lgb"),
    "dve_second": ("l0_kvs_in", "l1_hd", "l2_vs", "l3_qnd", "l4_xnd", "l5_h0", "l6_qkd", "l7_h"),
    "dve_sums": ("l1_acc", "l3_on", "l4_hsd", "l7_acc"),
    "dve_max": ("l2_su", "l3_smd", "l4_split", "l6_atd"),
    "dve_max_all": ("l2_mu", "l3_rot", "l4_vd"),
    "dve_turned": ("l3_pte",),
    "dve_inverse": ("l2_rb", "l3_hnd", "l4_rb"),
    "dve_hidden": ("l3_h",),
    "dve_lengths": ("l3_len",),
    "pool_first": ("l0_ones", "l2_xb", "l3_rn", "l4_rn"),
    "pool_cosines": ("l3_ad",),
    "pool_rotated": ("l3_rotq",),
    "act_masked": ("l2_qm", "l4_qm", "l6_qm"),
    "dve_normed": ("l2_on", "l4_on"),
    "pe_sums": ("l2_dn", "l4_dn"),
    "act_queries": ("l3_qin",),
    "act_lengths": ("l3_qsq",),
    "pool_bias": ("l3_xbd", "l4_vset"),
}


class Track:

    def __init__(self, new, name, before=0):
        self.before = before
        self.sems = [new(f"{name}_{s}") for s in range(STREAMS)]
        self.total = 0


class Signal:

    def __init__(self, track, per_turn=1):
        self.track, self.offset, self.per_turn = track, track.total, per_turn
        track.total += per_turn

    def __getitem__(self, s):
        return self.track.sems[s]

    def at(self, turn, k=0):
        return turn * self.track.total + (self.track.before + self.offset + k + 1)


X_OF = [-1, 0, 1, 2, 6, 7, 8, 9, 10]


def build(nc, x_in, small_in, l1_in, l3_in, l5_in, l7_in, const_in, constr_in, out, links):
    with ExitStack() as ctx:
        def sb(name, shape, dt=F32):
            return ctx.enter_context(nc.sbuf_tensor(name, shape, dt))

        def sem(name):
            return ctx.enter_context(nc.semaphore(name))

        tracks = {}

        def signal(name, per_turn=1, before=0):
            at = next((t for t, names in SHARED.items() if name in names), name)
            if at not in tracks:
                tracks[at] = Track(sem, at, before)
            return Signal(tracks[at], per_turn)

        def f32(ap):
            return ap.bitcast(F32)

        S2 = range(STREAMS)
        small = sb("small", [128, N_SMALL])
        region_a = sb("region_a", [128, N_REGION_A])
        region_b = sb("region_b", [128, N_REGION_B])
        const = sb("const", [128, N_CONST])
        constr = sb("constr", [128, N_CONSTR], F32R)
        xpos = sb("xpos", [128, 2, 2, 2, 2, 64])

        def W(name, a=0, b=None, rows=128):
            at, n = SMALL[name]
            return small[0:rows, at + a:at + (n if b is None else b)]

        def C(name, a=0, b=None):
            at, n = CONST[name]
            return const[:, at + a:at + (n if b is None else b)]

        def CR(name, j):
            at = CONSTR[name][0]
            return constr[:, at + 128 * j:at + 128 * (j + 1)]

        ident = C("ident")

        x = [sb(f"x{s}", [128, 2, D]) for s in S2]
        res = [sb(f"res{s}", [128, 2, D]) for s in S2]
        xT = [sb(f"xT{s}", [128, SEQ]) for s in S2]
        shT = [sb(f"shT{s}", [128, SEQ]) for s in S2]
        qTm = [sb(f"qTm{s}", [128, 2, 2, SEQ]) for s in S2]
        stats = [sb(f"stats{s}", [128, 2, 6]) for s in S2]
        mv = [sb(f"mv{s}", [128, 2, 2]) for s in S2]
        ve = [sb(f"ve{s}", [128, 2]) for s in S2]
        rstd = [sb(f"rstd{s}", [128, 2]) for s in S2]
        tiny = [sb(f"tiny{s}", [128, 224]) for s in S2]
        idx = [sb(f"idx{s}", [128, 2, 8], U32) for s in S2]
        scr = [sb(f"scr{s}", [128, 6144]) for s in S2]
        opr = [sb(f"opr{s}", [128, 4352], F32R) for s in S2]
        P = [[ctx.enter_context(nc.psum_tensor(f"P{s}{b}", [128, 512], F32)) for b in range(4)] for s in S2]

        def view(s, at, *dims):
            n = int(np.prod(dims))
            ap = scr[s][:, at:at + n]
            if len(dims) == 2:
                return ap.rearrange("p (a b) -> p a b", a=dims[0])
            if len(dims) == 3:
                return ap.rearrange("p (a b c) -> p a b c", a=dims[0], b=dims[1])
            return ap

        kst = [opr[s][:, 0:1024].rearrange("p (j n) -> p j n", j=4) for s in S2]
        qst = [opr[s][:, 1024:2048].rearrange("p (j n) -> p j n", j=4) for s in S2]
        qm = [opr[s][:, 2048:4096].rearrange("p (b j n) -> p b j n", b=2, j=4) for s in S2]
        qmask = [[qm[s][:, 0], qm[s][:, 1], qm[s][:, 0], qst[s]] for s in S2]
        qm6 = [opr[s][:, 2048:4096].rearrange("p (b n) -> p b n", b=8) for s in S2]
        parts = [opr[s][:, 3072:4096].rearrange("p (j n) -> p j n", j=4) for s in S2]
        mT = [opr[s][:, 4096:4352] for s in S2]

        l0_e = [view(s, 0, 3, 256) for s in S2]
        l0_r = [view(s, 768, 3, 256) for s in S2]
        l0_v = [view(s, 1536, 2, 132) for s in S2]
        l0_kvs = [view(s, 1800, 132) for s in S2]
        ex_h = [view(s, 0, 2, 4, 256) for s in S2]
        ex_g = [view(s, 2048, 2, 256) for s in S2]
        ex_log = [tiny[s][:, 0:16].rearrange("p (t e) -> p t e", t=2) for s in S2]
        ex_mx = [tiny[s][:, 16:32].rearrange("p (t e) -> p t e", t=2) for s in S2]
        ex_ix = [tiny[s][:, 32:48].rearrange("p (t e) -> p t e", t=2) for s in S2]
        ex_mk = [tiny[s][:, 48:64].rearrange("p (t e) -> p t e", t=2) for s in S2]
        ex_m2 = [tiny[s][:, 64:80].rearrange("p (t e) -> p t e", t=2) for s in S2]
        ex_mT = [view(s, 2560, 256) for s in S2]
        at_p = [view(s, 0, 4, 512) for s in S2]
        at_rope = [view(s, 0, 6, 256) for s in S2]
        at_v = [view(s, 2048, 2, 16, 32) for s in S2]
        at_o = [view(s, 3072, 4, 256) for s in S2]
        at_ct = [view(s, 5120, 256) for s in S2]
        at_kq = [view(s, 5376, 2, 256) for s in S2]
        at_xb = [view(s, 5888, 2, 128) for s in S2]
        inverse = [tiny[s][:, 160:192] for s in S2]
        m_tok = [tiny[s][:, 0:8].rearrange("p (t j) -> p t j", t=2) for s in S2]

        l3_tok = [view(s, 0, 2, 2, 512) for s in S2]
        l3_v = [view(s, 2048, 2, 512) for s in S2]
        l3_sq, l3_qn = [view(s, 3072, 2, 512) for s in S2], [view(s, 4096, 2, 512) for s in S2]
        l3_a = [[view(s, a, 512) for a in (5120, 3072)] for s in S2]
        l3_b, l3_bq = [view(s, 5632, 512) for s in S2], [view(s, 3584, 512) for s in S2]
        l3_kT = [view(s, 3072, 2, 256) for s in S2]
        l3_sm, l3_pT = [view(s, 3584, 2, 384) for s in S2], [view(s, 4352, 2, 384) for s in S2]
        l3_o_tok, l3_oT = [view(s, 0, 2, 512) for s in S2], [view(s, 1024, 4, 256) for s in S2]
        l3_hn, l3_hnT = [view(s, 3072, 2, 128) for s in S2], [view(s, 3328, 256) for s in S2]
        l3_gl, l3_hh = [view(s, 3584, 3, 256) for s in S2], [view(s, 4352, 3, 256) for s in S2]
        l3_xb = [view(s, 5120, 2, 128) for s in S2]
        l4_xn = [view(s, 0, 2, 128) for s in S2]
        l4_v = [view(s, 2048, 2, 8, 32) for s in S2]
        l5_hA, l5_hB, l5_hC = ([view(s, a, 4, 256) for s in S2] for a in (0, 1024, 3072))
        l5_y = [view(s, 4096, 2, 128) for s in S2]
        l6_v = [view(s, 0, 2, 1024) for s in S2]
        l6_at = [view(s, 2048, 4, 384) for s in S2]
        l6_oT = [view(s, 3584, 8, 256) for s in S2]
        l6_th, l6_cs = [view(s, 3584, 2, 256) for s in S2], [view(s, 4096, 2, 256) for s in S2]
        l6_cum, l6_prod, l6_den, l6_rd, l6_qn = ([view(s, a, 256) for s in S2] for a in (4608, 4864, 5120, 5376, 5632))
        k6 = [opr[s][:, 0:256] for s in S2]
        q6 = [opr[s][:, 1024:1280] for s in S2]

        s_first = sem("s_first")
        s_small, s_const, s_stage, s_zero, s_zd = (sem(n) for n in ("s_small", "s_const", "s_stage", "s_zero", "s_zd"))
        s_constr, s_xpos = sem("s_constr"), sem("s_xpos")
        s_wa, s_wb = sem("s_wa"), sem("s_wb")
        x_in_done, out_done = signal("x_in", 16), signal("out_done", 16)
        settled = {}
        chain = {e: sem(f"{e}_link") for e in ("act", "dve", "pool")}
        n_x = X_OF[-1] + 1
        n_ln = 10
        var_ready, rstd_ready = signal("var_ready", n_ln), signal("rstd_ready", n_ln)
        x_ready = signal("x_ready", n_x, before=1)
        xTp, xT_ready = signal("xTp", n_x), signal("xT_ready", n_x)

        l0_ones = signal("l0_ones")
        l0_qkv, l0_v_in, l0_qk, l0_kv, l0_kvs_in, l0_out = (signal(n) for n in
            ("l0_qkv", "l0_v_in", "l0_qk", "l0_kv", "l0_kvs_in", "l0_out"))
        l1_lg, l1_mask, l1_mTp, l1_mT = (signal(n) for n in ("l1_lg", "l1_mask", "l1_mTp", "l1_mT"))
        l1_z, l1_ha, l1_hd = signal("l1_z", 16), signal("l1_ha", 8), signal("l1_hd", 8)
        l1_y, l1_acc = signal("l1_y", 9), signal("l1_acc", 9)
        l2_ct, l2_cts, l2_kp, l2_qp, l2_split, l2_v, l2_vs, l2_xb = (signal(n) for n in
            ("l2_ct", "l2_cts", "l2_kp", "l2_qp", "l2_split", "l2_v", "l2_vs", "l2_xb"))
        st_full, st_in = signal("st_full", 4), signal("st_in", 4)
        l2_qm, l2_ob = signal("l2_qm", 4), signal("l2_ob", 4)
        l2_s, l2_su, l2_m, l2_mu = signal("l2_s", 16), signal("l2_su", 16), signal("l2_m", 4), signal("l2_mu", 4)
        l2_st, l2_p, l2_pv = signal("l2_st", 16), signal("l2_p", 16), signal("l2_pv", 4)
        l2_dn, l2_bc, l2_rb, l2_on, l2_y = (signal(n) for n in ("l2_dn", "l2_bc", "l2_rb", "l2_on", "l2_y"))

        l3_qkv, l3_sqd, l3_ss, l3_rn, l3_qnd, l3_ad, l3_rot, l3_qin, l3_len, l3_qsq, l3_rotq = (signal(n, 2 * k) for n, k in
            (("l3_qkv", 6), ("l3_sqd", 2), ("l3_ss", 2), ("l3_rn", 3), ("l3_qnd", 2), ("l3_ad", 1), ("l3_rot", 3),
             ("l3_qin", 2), ("l3_len", 3), ("l3_qsq", 2), ("l3_rotq", 1)))
        l3_vin, l3_tp, l3_te = signal("l3_vin", 4), signal("l3_tp", 8), signal("l3_te", 8)
        l3_s, l3_smd, l3_e, l3_pt, l3_pte = (signal(n, 16) for n in
            ("l3_s", "l3_smd", "l3_e", "l3_pt", "l3_pte"))
        l3_o, l3_on, l3_otp, l3_ot = (signal(n, 4) for n in ("l3_o", "l3_on", "l3_otp", "l3_ot"))
        l3_y, l3_hs, l3_hnd, l3_hnp, l3_hnTd, l3_y2, l3_xbd = (signal(n, 2) for n in
            ("l3_y", "l3_hs", "l3_hnd", "l3_hnp", "l3_hnTd", "l3_y2", "l3_xbd"))
        l3_z, l3_gld, l3_h = signal("l3_z", 6), signal("l3_gld", 6), signal("l3_h", 6)
        l4_ss, l4_rn, l4_xnd, l4_p, l4_split, l4_vd, l4_vset, l4_oin, l4_hs, l4_hsd, l4_dn, l4_bc, l4_rb, l4_on, l4_y = (
            signal(n) for n in ("l4_ss", "l4_rn", "l4_xnd", "l4_p", "l4_split", "l4_vd", "l4_vset", "l4_oin",
                                "l4_hs", "l4_hsd", "l4_dn", "l4_bc", "l4_rb", "l4_on", "l4_y"))
        l4_stf, l4_stin, l4_qm = signal("l4_stf", 4), signal("l4_stin", 4), signal("l4_qm", 2)
        l4_st, l4_sq, l4_pv = signal("l4_st", 8), signal("l4_sq", 8), signal("l4_pv", 2)
        l5_z, l5_sg, l5_h0 = signal("l5_z", 8), signal("l5_sg", 4), signal("l5_h0", 4)
        l5_h1, l5_h2, l5_yd = signal("l5_h1", 2), signal("l5_h2", 2), signal("l5_yd")
        l6_qk, l6_csd, l6_pr, l6_dn, l6_qkd, l6_yd = (signal(n) for n in
            ("l6_qk", "l6_csd", "l6_pr", "l6_dn", "l6_qkd", "l6_yd"))
        l6_vp, l6_va = signal("l6_vp", 4), signal("l6_va", 4)
        l6_qm, l6_a, l6_atd, l6_o, l6_ot = signal("l6_qm", 16), signal("l6_a", 16), signal("l6_atd", 16), signal("l6_o", 16), signal("l6_ot", 8)
        l7_lg, l7_lgb, l7_pr = (signal(n) for n in ("l7_lg", "l7_lgb", "l7_pr"))
        l7_z, l7_sg, l7_h = signal("l7_z", 18), signal("l7_sg", 18), signal("l7_h", 18)
        l7_y, l7_acc = signal("l7_y", 9), signal("l7_acc", 9)

        def settle(eng):
            eng.sem_inc(settled[eng], 1)

        def lengths(s, t, w):
            at = 16 * w + 8 * t
            return tiny[s][:, at:at + 8]

        def inverses(s, t, w):
            at = 32 + 16 * w + 8 * t
            return tiny[s][:, at:at + 8]

        def sine_part(engine, L, w, t, source, out_):
            q = source.rearrange("p (h k d) -> p h k d", h=LH, k=2)
            b = out_.rearrange("p (h k d) -> p h k d", h=LH, k=2)
            for k in range(2):
                sin = xpos[:, L, w, 1, t, 32 * k:32 * k + 32].unsqueeze(1).to_broadcast([128, LH, 32])
                ins = engine.tensor_tensor(b[:, :, k, :], q[:, :, 1 - k, :], sin, ALU.mult)
            return ins

        class Links:

            def __init__(self, name, eng, turn):
                self.name, self.eng, self.turn, self.n = name, eng, turn, 0

            def __call__(self, ins):
                ins.then_inc(chain[self.name], 1)
                self.n += 1
                self.eng.wait_ge(chain[self.name], self.turn * links[self.name] + self.n)

            def close(self):
                if links[self.name] != max(self.n, 1):
                    raise ValueError(f"LINK {self.name} {max(self.n, 1)}")

        block = ctx.enter_context(nc.Block())

        @block.sync
        def _(sp):
            sp.dma_start(small[:, 0:N_FIRST], small_in[:, 0:N_FIRST]).then_inc(s_first, 16)
            sp.dma_start(const[:, :], const_in).then_inc(s_const, 16)
            sp.dma_start(region_b[:, 0:N_CONSTR], constr_in).then_inc(s_stage, 16)

            def load_x(turn, s):
                sp.dma_start(x[s][:, :, :], x_in[2 * turn + s, :, :].rearrange("(t p) d -> p t d", p=128)).then_inc(x_in_done[s], 16)

            for s in S2:
                load_x(0, s)
            sp.dma_start(region_a[:, 0:N_L1W], l1_in).then_inc(s_wa, 16)
            sp.dma_start(small[:, N_FIRST:], small_in[:, N_FIRST:]).then_inc(s_small, 16)
            sp.wait_ge(s_constr, 1)
            with sp.Fori(0, TURNS) as c:
                for s in S2:
                    sp.wait_ge(x_ready[s], x_ready.at(c, -1))
                sp.dma_start(region_b[:, 0:2 * N_L3W], l3_in).then_inc(s_wb, 16)
                for s in S2:
                    sp.wait_ge(x_ready[s], x_ready.at(c, X_OF[2]))
                sp.dma_start(region_a[:, 0:N_L5W], l5_in).then_inc(s_wa, 16)
                for s in S2:
                    sp.wait_ge(x_ready[s], x_ready.at(c, X_OF[4]))
                sp.dma_start(region_b[:, 0:N_L7W], l7_in).then_inc(s_wb, 16)
                for s in S2:
                    sp.wait_ge(x_ready[s], x_ready.at(c, X_OF[6]))
                sp.dma_start(region_a[:, 0:N_L1W], l1_in).then_inc(s_wa, 16)
                for s in S2:
                    sp.wait_ge(x_ready[s], x_ready.at(c, n_x - 1))
                    sp.dma_start(out[2 * c + s, :, :].rearrange("(t p) d -> p t d", p=128), x[s][:, :, :]
                                 ).then_inc(out_done[s], 16)
                    sp.wait_ge(out_done[s], out_done.at(c, 15))
                    load_x(c + 1, s)
            for s in S2:
                sp.wait_ge(x_in_done[s], x_in_done.per_turn * (TURNS + 1))
            sp.wait_ge(s_wa, 32 * TURNS + 16)

        n_wa = 32
        n_wb = 32

        @block.tensor
        def _(pe):
            pe.wait_ge(s_const, 16)
            pe.wait_ge(s_first, 16)
            pe.wait_ge(s_zero, 1)
            pe.wait_ge(s_zd, 1)
            with pe.Fori(0, TURNS) as c:

                def mm(out_, lhsT, rhs, start=True, stop=True):
                    return pe.matmul(out_, lhsT, rhs, start=start, stop=stop)

                def transpose_x(s, k, src=x, ready=None):
                    if ready is not None:
                        pe.wait_ge(ready[s], ready.at(c))
                    if k == 0:
                        pe.wait_ge(x_in_done[s], x_in_done.at(c, 15))
                        pe.wait_ge(x_ready[s], x_ready.at(c, -1))
                    else:
                        pe.wait_ge(x_ready[s], x_ready.at(c, k - 1))
                    for t in range(2):
                        ins = pe.transpose(P[s][0][:, 128 * t:128 * t + 128], src[s][:, t, :], ident)
                    ins.then_inc(xTp[s], 1)

                def transposed(s, k):
                    pe.wait_ge(xT_ready[s], xT_ready.at(c, k))

                def l0_project(s):
                    ins = mm(P[s][1][:, 0:256], W("l0_w", 0, 128), xT[s][:, :])
                    for t in range(2):
                        ins = mm(P[s][2][:, 256 * t:256 * t + 256], xT[s][:, 128 * t:128 * t + 128], W("l0_w", 128, 384))
                    ins.then_inc(l0_qkv[s], 1)

                def l0_state(s):
                    pe.wait_ge(l0_qk[s], l0_qk.at(c))
                    pe.wait_ge(l0_v_in[s], l0_v_in.at(c))
                    pe.wait_ge(l0_ones[s], l0_ones.at(c))
                    for t in range(2):
                        ins = mm(P[s][3][:, 0:129], l0_r[s][:, 1, 128 * t:128 * t + 128], l0_v[s][:, t, 0:129], t == 0, t == 1)
                    ins.then_inc(l0_kv[s], 1)

                def l0_read(s):
                    pe.wait_ge(l0_kvs_in[s], l0_kvs_in.at(c))
                    for t in range(2):
                        ins = mm(P[s][1][:, 129 * t:129 * t + 129], l0_r[s][:, 0, 128 * t:128 * t + 128], l0_kvs[s][:, 0:129])
                    ins.then_inc(l0_out[s], 1)

                def l1_logits(s):
                    for t in range(2):
                        ins = mm(P[s][3][:, 8 * t:8 * t + 8], xT[s][:, 128 * t:128 * t + 128], W("l1_gate"))
                    ins.then_inc(l1_lg[s], 1)

                def l1(s):
                    w1 = region_a[:, 0:E0 * F0].rearrange("p (e f) -> p e f", e=E0)
                    w2 = region_a[:, E0 * F0:N_L1W].rearrange("p (e f d) -> p e f d", e=E0, f=4)
                    pe.wait_ge(s_wa, n_wa * c + 16)

                    def up(n):
                        e, p = divmod(n, 2)
                        if n >= 3:
                            m = n - 3
                            reader = l1_hd if m % 2 else l1_ha
                            pe.wait_ge(reader[s], reader.at(c, m // 2))
                        for f in range(2):
                            ins = mm(P[s][n % 3][:, 256 * f:256 * f + 256],
                                     w1[:, e, 128 * (2 * p + f):128 * (2 * p + f) + 128], xT[s][:, :])
                        ins.then_inc(l1_z[s], 1)

                    def down(e):
                        pe.wait_ge(l1_ha[s], l1_ha.at(c, e))
                        pe.wait_ge(l1_hd[s], l1_hd.at(c, e))
                        if e == 0:
                            pe.wait_ge(l1_mask[s], l1_mask.at(c))
                        else:
                            pe.wait_ge(l1_acc[s], l1_acc.at(c, e - 1))
                        for t in range(2):
                            for f in range(4):
                                ins = mm(P[s][3][:, 128 * t:128 * t + 128],
                                         ex_h[s][:, e % 2, f, 128 * t:128 * t + 128], w2[:, e, f, :], f == 0, f == 3)
                        ins.then_inc(l1_y[s], 1)

                    up(0)
                    up(1)
                    for e in range(E0):
                        if e + 1 < E0:
                            up(2 * e + 2)
                            up(2 * e + 3)
                        else:
                            pe.wait_ge(l1_mask[s], l1_mask.at(c))
                            pe.wait_ge(l1_hd[s], l1_hd.at(c, e - 1))
                            for t in range(2):
                                ins = pe.transpose(P[s][1][0:8, 128 * t:128 * t + 128], ex_mk[s][:, t, :], ident)
                            ins.then_inc(l1_mTp[s], 1)
                        down(e)
                    pe.wait_ge(l1_mT[s], l1_mT.at(c))
                    pe.wait_ge(l1_acc[s], l1_acc.at(c, E0 - 1))
                    for t in range(2):
                        ins = mm(P[s][3][:, 128 * t:128 * t + 128], ex_mT[s][0:8, 128 * t:128 * t + 128], W("l1_b2", rows=8))
                    ins.then_inc(l1_y[s], 1)

                def l2_down(s):
                    mm(P[s][1][:, 0:256], W("l2_down"), xT[s][:, :]).then_inc(l2_ct[s], 1)
                    mm(P[s][2][:, 0:256], W("l2_kr"), xT[s][:, :])
                    mm(P[s][2][:, 256:512], W("l2_krs"), xT[s][:, :]).then_inc(l2_kp[s], 1)

                def l2_up(s):
                    pe.wait_ge(l2_cts[s], l2_cts.at(c))
                    mm(P[s][3][:, 0:256], W("l2_qr"), at_ct[s])
                    mm(P[s][3][:, 256:512], W("l2_qrs"), at_ct[s])
                    mm(P[s][0][:, 0:256], W("l2_qc"), at_ct[s])
                    mm(P[s][0][:, 256:512], W("l2_kc"), at_ct[s]).then_inc(l2_qp[s], 1)
                    for t in range(2):
                        ins = mm(P[s][1][:, 128 * t:128 * t + 128], at_ct[s][:, 128 * t:128 * t + 128], W("l2_v"))
                    ins.then_inc(l2_v[s], 1)

                def stack(s, full):
                    for w, (hi, lo, names) in enumerate(((0, 1, ("sel_kh", "sel_kl")), (2, 3, ("sel_qh", "sel_ql")))):
                        for b in range(2):
                            bank = P[s][2 * w + b]
                            for j in (2 * b, 2 * b + 1):
                                o = bank[:, 256 * (j % 2):256 * (j % 2) + 256]
                                mm(o, CR(names[0], j), parts[s][:, hi, :], True, False)
                                ins = mm(o, CR(names[1], j), parts[s][:, lo, :], False, True)
                            ins.then_inc(full[s], 1)

                def l2_scores(s, i, j):
                    if j == 0:
                        pe.wait_ge(l2_qm[s], l2_qm.at(c, i))
                        if i:
                            pe.wait_ge(l2_mu[s], l2_mu.at(c, i - 1))
                    else:
                        pe.wait_ge(l2_su[s], l2_su.at(c, 4 * i + j - 1))
                    for t in range(2):
                        ins = mm(P[s][0][:, 256 * t:256 * t + 256], qmask[s][i][:, j, 128 * t:128 * t + 128], kst[s][:, j, :])
                    ins.then_inc(l2_s[s], 1)

                def l2_max(s, i):
                    pe.wait_ge(l2_su[s], l2_su.at(c, 4 * i + 3))
                    for t in range(2):
                        ins = pe.transpose(P[s][0][0:4, 128 * t:128 * t + 128], m_tok[s][:, t, :], ident)
                    ins.then_inc(l2_m[s], 1)

                def l2_shifted(s, i, j):
                    if j == 0:
                        pe.wait_ge(l2_mu[s], l2_mu.at(c, i))
                    if 4 * i + j > 1:
                        pe.wait_ge(l2_p[s], l2_p.at(c, 4 * i + j - 2))
                    for t in range(2):
                        o = P[s][1 + j % 2][:, 256 * t:256 * t + 256]
                        mm(o, kst[s][:, j, 128 * t:128 * t + 128], qmask[s][i][:, j, :], True, False)
                        ins = mm(o, CR("sel_max", j), mT[s], False, True)
                    ins.then_inc(l2_st[s], 1)

                def l2_values(s, i):
                    pe.wait_ge(l2_p[s], l2_p.at(c, 4 * i + 3))
                    if i:
                        pe.wait_ge(l2_ob[s], l2_ob.at(c, i - 1))
                    o = P[s][3][:, 256 * (i % 2):256 * (i % 2) + 256]
                    for t in range(2):
                        for j in range(4):
                            ins = mm(o[32 * j:32 * j + 32, :], at_v[s][:, t, 4 * j + i, :],
                                     at_p[s][:, j, 256 * t:256 * t + 256], t == 0, t == 1)
                    ins.then_inc(l2_pv[s], 1)

                def sums(s, n, rows, src, done):
                    pe.wait_ge(src[s], src.at(c, src.per_turn - 1))
                    for t in range(2):
                        for i in range(n):
                            at = 4 * (n * t + i)
                            ins = mm(P[s][0][:, at:at + 4], at_o[s][:, i, 128 * t:128 * t + 128], C(rows)[:, 0:128:32])
                    ins.then_inc(done[s], 1)

                def spread(s, n, src, done):
                    pe.wait_ge(src[s], src.at(c, src.per_turn - 1))
                    for t in range(2):
                        for i in range(n):
                            at = 4 * (n * t + i)
                            o = P[s][i // 2][:, 256 * (i % 2) + 128 * t:256 * (i % 2) + 128 * t + 128]
                            for j in range(4):
                                ins = mm(o[32 * j:32 * j + 32, :], inverse[s][:, at + j:at + j + 1].to_broadcast([128, 32]), ident)
                    ins.then_inc(done[s], 1)

                def l2_out(s):
                    pe.wait_ge(l2_on[s], l2_on.at(c))
                    for t in range(2):
                        for i in range(4):
                            ins = mm(P[s][2][:, 128 * t:128 * t + 128], at_o[s][:, i, 128 * t:128 * t + 128],
                                     W("l2_o", 128 * i, 128 * i + 128), i == 0, i == 3)
                    ins.then_inc(l2_y[s], 1)

                def l3_project(s, L, n):
                    if n == 0:
                        pe.wait_ge(s_wb, n_wb * c + 16)
                    t, k = n // 2, 1 - n % 2
                    at = L * N_L3W + 512 * k
                    mm(P[s][2 * t + k][:, :], shT[s][:, 128 * t:128 * t + 128], region_b[:, at:at + 512]).then_inc(l3_qkv[s], 1)

                def l3_project_v(s, L):
                    w = region_b[:, L * N_L3W + 1024:L * N_L3W + 1536]
                    for t in range(2):
                        if t == 0:
                            pe.wait_ge(l3_qsq[s], l3_qsq.at(c, 2 * L))
                        else:
                            pe.wait_ge(l3_qnd[s], l3_qnd.at(c, 2 * L))
                        mm(P[s][t][:, :], shT[s][:, 128 * t:128 * t + 128], w).then_inc(l3_qkv[s], 1)

                def l3_pair(s, L, p):
                    if p == 0:
                        pe.wait_ge(l3_rot[s], l3_rot.at(c, 3 * L + 2))
                        pe.wait_ge(l3_rotq[s], l3_rotq.at(c, L))
                    else:
                        pe.wait_ge(l3_te[s], l3_te.at(c, 4 * L + p - 1))
                    for k in range(2):
                        for t in range(2):
                            ins = pe.transpose(P[s][3][:, 256 * k + 128 * t:256 * k + 128 * t + 128],
                                               l3_tok[s][:, k, t, 128 * p:128 * p + 128], ident)
                    ins.then_inc(l3_tp[s], 1)

                def l3_scores(s, L, h):
                    pe.wait_ge(l3_te[s], l3_te.at(c, 4 * L + h // 2))
                    if h == 0:
                        pe.wait_ge(l3_vin[s], l3_vin.at(c, 2 * L + 1))
                    if h > 1:
                        pe.wait_ge(l3_pte[s], l3_pte.at(c, 8 * L + h - 2))
                    q, k, o = qTm[s][:, h // 2 % 2, h % 2, :], l3_kT[s][:, h // 2 % 2, :], P[s][h % 2]
                    mm(o[:, 0:128], q[:, 0:128], k[:, 0:128])
                    mm(o[:, 128:384], q[:, 128:256], k).then_inc(l3_s[s], 1)

                def l3_turn(s, L, h):
                    pe.wait_ge(l3_e[s], l3_e.at(c, 8 * L + h))
                    for b in range(3):
                        ins = pe.transpose(P[s][h % 2][:, 128 * b:128 * b + 128], l3_sm[s][:, h % 2, 128 * b:128 * b + 128], ident)
                    ins.then_inc(l3_pt[s], 1)

                def l3_values(s, L, h):
                    pe.wait_ge(l3_pte[s], l3_pte.at(c, 8 * L + h))
                    if h == 4:
                        pe.wait_ge(l3_te[s], l3_te.at(c, 4 * L + 3))
                    at, pT, vh = 64 * (h % 4), l3_pT[s][:, h % 2, :], l3_v[s][:, :, 64 * h:64 * h + 64]
                    o = P[s][2 + h // 4]
                    mm(o[:, at:at + 64], pT[:, 0:128], vh[:, 0, :])
                    mm(o[:, 256 + at:320 + at], pT[:, 128:256], vh[:, 0, :], True, False)
                    ins = mm(o[:, 256 + at:320 + at], pT[:, 256:384], vh[:, 1, :], False, True)
                    if h % 4 == 3:
                        ins.then_inc(l3_o[s], 1)

                def l3_o_turn(s, L, g):
                    pe.wait_ge(l3_on[s], l3_on.at(c, 2 * L + g))
                    for j in range(2):
                        for t in range(2):
                            at = 128 * (2 * g + j)
                            ins = pe.transpose(P[s][2 + g][:, 256 * j + 128 * t:256 * j + 128 * t + 128],
                                               l3_o_tok[s][:, t, at:at + 128], ident)
                    ins.then_inc(l3_otp[s], 1)

                def l3_out(s, L):
                    at, _ = L3W["o"]
                    w = region_b[:, L * N_L3W + at:L * N_L3W + at + 512].rearrange("p (j d) -> p j d", j=4)
                    pe.wait_ge(l3_ot[s], l3_ot.at(c, 2 * L + 1))
                    for t in range(2):
                        for p in range(4):
                            ins = mm(P[s][2][:, 128 * t:128 * t + 128], l3_oT[s][:, p, 128 * t:128 * t + 128], w[:, p, :], p == 0, p == 3)
                    ins.then_inc(l3_y[s], 1)

                def l3_back(s, L):
                    for t in range(2):
                        ins = pe.transpose(P[s][1][:, 128 * t:128 * t + 128], shT[s][:, 128 * t:128 * t + 128], ident)
                    ins.then_inc(l3_hs[s], 1)

                def l3_normed(s, L):
                    pe.wait_ge(l3_hnd[s], l3_hnd.at(c, L))
                    for t in range(2):
                        ins = pe.transpose(P[s][2][:, 128 * t:128 * t + 128], l3_hn[s][:, t, :], ident)
                    ins.then_inc(l3_hnp[s], 1)

                def l3_ffn(s, L):
                    at, _ = L3W["w1"]
                    w = region_b[:, L * N_L3W + at:L * N_L3W + at + 2 * HID]
                    pe.wait_ge(l3_hnTd[s], l3_hnTd.at(c, L))
                    for f, (b, M) in enumerate(zip((0, 1, 3), FT)):
                        for k in range(2):
                            ins = mm(P[s][b][0:M, 256 * k:256 * k + 256], w[:, HID * k + 128 * f:HID * k + 128 * f + M], l3_hnT[s])
                        ins.then_inc(l3_z[s], 1)

                def l3_ffn_out(s, L):
                    at, _ = L3W["w2"]
                    w = region_b[:, L * N_L3W + at:L * N_L3W + at + 384].rearrange("p (j d) -> p j d", j=3)
                    pe.wait_ge(l3_h[s], l3_h.at(c, 3 * L + 2))
                    for t in range(2):
                        for f, M in enumerate(FT):
                            ins = mm(P[s][2][:, 128 * t:128 * t + 128], l3_hh[s][0:M, f, 128 * t:128 * t + 128], w[0:M, f, :], f == 0, f == 2)
                    ins.then_inc(l3_y2[s], 1)

                def l4_project(s):
                    mm(P[s][1][:, 0:256], W("l4_w", 128, 256), xT[s][:, :])
                    mm(P[s][1][:, 256:512], W("l4_w", 0, 128), xT[s][:, :])
                    for t in range(2):
                        ins = mm(P[s][2][:, 128 * t:128 * t + 128], xT[s][:, 128 * t:128 * t + 128], W("l4_w", 256, 384))
                    ins.then_inc(l4_p[s], 1)

                def l4_scores(s, i, j):
                    n = 4 * i + j
                    pe.wait_ge(l4_qm[s], l4_qm.at(c, i))
                    if n > 1:
                        pe.wait_ge(l4_sq[s], l4_sq.at(c, n - 2))
                    for t in range(2):
                        ins = mm(P[s][n % 2][:, 256 * t:256 * t + 256], kst[s][:, j, 128 * t:128 * t + 128], qm[s][:, i, j, :])
                    ins.then_inc(l4_st[s], 1)

                def l4_values(s, i):
                    pe.wait_ge(l4_sq[s], l4_sq.at(c, 4 * i + 3))
                    for t in range(2):
                        for j in range(4):
                            ins = mm(P[s][2][32 * j:32 * j + 32, 256 * i:256 * i + 256], l4_v[s][:, t, 2 * j + i, :],
                                     at_p[s][:, j, 256 * t:256 * t + 256], t == 0, t == 1)
                    ins.then_inc(l4_pv[s], 1)

                def l4_halves(s):
                    for i in range(2):
                        for j in range(4):
                            for t in range(2):
                                ins = mm(P[s][3][32 * j:32 * j + 32, i:i + 1], l4_v[s][:, t, 2 * j + i, :], C("half"), t == 0, t == 1)
                    ins.then_inc(l4_hs[s], 1)

                def l4_out(s):
                    pe.wait_ge(l4_on[s], l4_on.at(c))
                    for t in range(2):
                        for i in range(2):
                            ins = mm(P[s][3][:, 128 * t:128 * t + 128], at_o[s][:, i, 128 * t:128 * t + 128],
                                     W("l4_o", 128 * i, 128 * i + 128), i == 0, i == 1)
                    ins.then_inc(l4_y[s], 1)

                def L5(name):
                    at, n = L5W[name]
                    return region_a[:, at:at + n]

                def l5_gates(s):
                    pe.wait_ge(s_wa, n_wa * c + 32)
                    for f in range(4):
                        if f == 3:
                            pe.wait_ge(l5_h0[s], l5_h0.at(c, 0))
                        for k, w in enumerate(("w1", "w2")):
                            ins = mm(P[s][f % 3][:, 256 * k:256 * k + 256], L5(w)[:, 128 * f:128 * f + 128], xT[s][:, :])
                        ins.then_inc(l5_z[s], 1)

                def l5_hidden(s, w, src, n0, ready, last, steps=range(2)):
                    m = L5(w).rearrange("p (k o) -> p k o", k=4)
                    pe.wait_ge(ready[s], ready.at(c, ready.per_turn - 1))
                    for p in steps:
                        n = n0 + p
                        if n > 5:
                            pe.wait_ge(last[s], last.at(c, n - 7))
                        for f in range(2):
                            for k in range(4):
                                ins = mm(P[s][n % 3][:, 256 * f:256 * f + 256],
                                         m[:, k, 128 * (2 * p + f):128 * (2 * p + f) + 128], src[s][:, k, :], k == 0, k == 3)
                        ins.then_inc(l5_z[s], 1)

                def l5_out(s):
                    m = L5("w3").rearrange("p (k o) -> p k o", k=4)
                    pe.wait_ge(l5_h2[s], l5_h2.at(c, 1))
                    for t in range(2):
                        for k in range(4):
                            ins = mm(P[s][3][:, 128 * t:128 * t + 128], l5_hC[s][:, k, 128 * t:128 * t + 128], m[:, k, :], k == 0, k == 3)
                    ins.then_inc(l5_yd[s], 1)

                def l6_project(s):
                    mm(P[s][0][:, 0:256], W("l6_q"), xT[s][:, :])
                    mm(P[s][0][:, 256:512], W("l6_k"), xT[s][:, :]).then_inc(l6_qk[s], 1)

                def l6_project_v(s, steps):
                    for n in steps:
                        t, k = divmod(n, 2)
                        if n == 3:
                            pe.wait_ge(l6_csd[s], l6_csd.at(c))
                        mm(P[s][(n + 1) % 4][:, :], xT[s][:, 128 * t:128 * t + 128], W("l6_v", 512 * k, 512 * k + 512)
                           ).then_inc(l6_vp[s], 1)

                def l6_denominator(s):
                    pe.wait_ge(l6_pr[s], l6_pr.at(c))
                    pe.wait_ge(l6_va[s], l6_va.at(c, 0))
                    mm(P[s][1][:, 0:256], C("pair_sum"), l6_prod[s]).then_inc(l6_dn[s], 1)

                def l6_scores(s, h):
                    if h == 0:
                        pe.wait_ge(l6_va[s], l6_va.at(c, 3))
                    pe.wait_ge(l6_qm[s], l6_qm.at(c, h))
                    if h > 1:
                        pe.wait_ge(l6_atd[s], l6_atd.at(c, h - 2))
                    o, q = P[s][h % 2], qm6[s][:, h % 8, :]
                    mm(o[:, 0:256], k6[s][:, 0:128], q)
                    mm(o[:, 256:384], k6[s][:, 128:256], q[:, 128:256]).then_inc(l6_a[s], 1)

                def l6_values(s, h):
                    p = h // 2
                    pe.wait_ge(l6_atd[s], l6_atd.at(c, h))
                    if p > 1 and h % 2 == 0:
                        pe.wait_ge(l6_ot[s], l6_ot.at(c, p - 2))
                    o, a = P[s][2 + p % 2][64 * (h % 2):64 * (h % 2) + 64, :], l6_at[s][:, h % 4, :]
                    mm(o[:, 0:256], l6_v[s][:, 0, 64 * h:64 * h + 64], a[:, 0:256], True, False)
                    mm(o[:, 128:256], l6_v[s][:, 1, 64 * h:64 * h + 64], a[:, 256:384], False, True).then_inc(l6_o[s], 1)

                def l6_out(s):
                    pe.wait_ge(l6_ot[s], l6_ot.at(c, 7))
                    for t in range(2):
                        for p in range(8):
                            ins = mm(P[s][0][:, 128 * t:128 * t + 128], l6_oT[s][:, p, 128 * t:128 * t + 128],
                                     W("l6_o", 128 * p, 128 * p + 128), p == 0, p == 7)
                    ins.then_inc(l6_yd[s], 1)

                def l7_logits(s):
                    for t in range(2):
                        ins = mm(P[s][3][:, 8 * t:8 * t + 8], xT[s][:, 128 * t:128 * t + 128], W("l7_gate"))
                    ins.then_inc(l7_lg[s], 1)

                def l7(s):
                    n_e = 2 * I3 + 2 * D
                    pe.wait_ge(s_wb, n_wb * c + 32)

                    def up(n):
                        e, f = divmod(n, 2)
                        if n >= 3:
                            pe.wait_ge(l7_h[s], l7_h.at(c, n - 3))
                        for k in range(2):
                            ins = mm(P[s][n % 3][:, 256 * k:256 * k + 256],
                                     region_b[:, e * n_e + I3 * k + 128 * f:e * n_e + I3 * k + 128 * f + 128], xT[s][:, :])
                        ins.then_inc(l7_z[s], 1)

                    def down(e):
                        pe.wait_ge(l7_h[s], l7_h.at(c, 2 * e + 1))
                        if e == 0:
                            pe.wait_ge(l7_lgb[s], l7_lgb.at(c))
                        else:
                            pe.wait_ge(l7_acc[s], l7_acc.at(c, e - 1))
                        for t in range(2):
                            for f in range(2):
                                ins = mm(P[s][3][:, 128 * t:128 * t + 128], ex_h[s][:, e % 2, f, 128 * t:128 * t + 128],
                                         region_b[:, e * n_e + 2 * I3 + D * f:e * n_e + 2 * I3 + D * f + D], f == 0, f == 1)
                        ins.then_inc(l7_y[s], 1)

                    up(0)
                    up(1)
                    for e in range(E3):
                        if e + 1 < E3:
                            up(2 * e + 2)
                            up(2 * e + 3)
                        down(e)

                for s in S2:
                    transpose_x(s, 0)
                for s in S2:
                    transposed(s, 0)
                    l0_project(s)
                for s in S2:
                    l0_state(s)
                for s in S2:
                    l0_read(s)
                for s in S2:
                    transpose_x(s, 1)
                    transposed(s, 1)
                    l1_logits(s)
                    l1(s)
                pe.wait_ge(s_small, 16)
                pe.wait_ge(s_constr, 1)
                for s in S2:
                    transpose_x(s, 2)
                for s in S2:
                    transposed(s, 2)
                    l2_down(s)
                for s in S2:
                    l2_up(s)
                for s in S2:
                    pe.wait_ge(l2_split[s], l2_split.at(c))
                    pe.wait_ge(l2_vs[s], l2_vs.at(c))
                    stack(s, st_full)
                for s in S2:
                    pe.wait_ge(st_in[s], st_in.at(c, 3))
                for j in range(4):
                    for s in S2:
                        l2_scores(s, 0, j)
                for s in S2:
                    l2_max(s, 0)
                for i in range(4):
                    for j in range(4):
                        for s in S2:
                            l2_shifted(s, i, j)
                        if i < 3:
                            for s in S2:
                                l2_scores(s, i + 1, j)
                    if i < 3:
                        for s in S2:
                            l2_max(s, i + 1)
                    for s in S2:
                        l2_values(s, i)
                for s in S2:
                    sums(s, 4, "rows8", l2_ob, l2_dn)
                for s in S2:
                    spread(s, 4, l2_rb, l2_bc)
                for s in S2:
                    l2_out(s)
                for L in range(2):
                    for s in S2:
                        transpose_x(s, 3 + 2 * L)
                    for s in S2:
                        transposed(s, 3 + 2 * L)
                    for n in range(4):
                        for s in S2:
                            l3_project(s, L, n)
                    for s in S2:
                        l3_project_v(s, L)
                    for s in S2:
                        l3_pair(s, L, 0)
                    for h in range(LH + 2):
                        if h < LH:
                            for s in S2:
                                l3_scores(s, L, h)
                        if 0 < h <= LH:
                            for s in S2:
                                l3_turn(s, L, h - 1)
                        if h > 1:
                            for s in S2:
                                l3_values(s, L, h - 2)
                        if h in L3_PAIR:
                            for s in S2:
                                l3_pair(s, L, L3_PAIR[h])
                        if h == 7:
                            for s in S2:
                                l3_o_turn(s, L, 0)
                    for s in S2:
                        l3_o_turn(s, L, 1)
                    for s in S2:
                        l3_out(s, L)
                    for s in S2:
                        transpose_x(s, 4 + 2 * L)
                    for s in S2:
                        transposed(s, 4 + 2 * L)
                        l3_back(s, L)
                    for s in S2:
                        l3_normed(s, L)
                    for s in S2:
                        l3_ffn(s, L)
                    for s in S2:
                        l3_ffn_out(s, L)
                for s in S2:
                    transpose_x(s, 7, l4_xn, l4_xnd)
                for s in S2:
                    transposed(s, 7)
                    l4_project(s)
                for s in S2:
                    pe.wait_ge(l4_split[s], l4_split.at(c))
                    pe.wait_ge(l4_vd[s], l4_vd.at(c))
                    stack(s, l4_stf)
                for s in S2:
                    pe.wait_ge(l4_stin[s], l4_stin.at(c, 3))
                    l4_halves(s)
                for i in range(2):
                    for j in range(4):
                        for s in S2:
                            l4_scores(s, i, j)
                    for s in S2:
                        l4_values(s, i)
                for s in S2:
                    sums(s, 2, "rows16", l4_oin, l4_dn)
                for s in S2:
                    spread(s, 2, l4_rb, l4_bc)
                for s in S2:
                    l4_out(s)
                for s in S2:
                    transpose_x(s, 8)
                for s in S2:
                    transposed(s, 8)
                    l5_gates(s)
                for s in S2:
                    l5_hidden(s, "h1", l5_hA, 4, l5_h0, None)
                l5_hidden(0, "h2", l5_hB, 6, l5_h1, l5_h1)
                l5_hidden(1, "h2", l5_hB, 6, l5_h1, l5_h1, (0,))
                l5_out(0)
                l5_hidden(1, "h2", l5_hB, 6, l5_h1, l5_h1, (1,))
                l5_out(1)
                for s in S2:
                    transpose_x(s, 9)
                    transposed(s, 9)
                    l6_project(s)
                    l6_project_v(s, range(3))
                for s in S2:
                    l6_project_v(s, (3,))
                for s in S2:
                    l6_denominator(s)
                for h in range(H3 + 2):
                    for s in S2:
                        if h > 1:
                            l6_values(s, h - 2)
                        if h < H3:
                            l6_scores(s, h)
                for s in S2:
                    l6_out(s)
                for s in S2:
                    transpose_x(s, 10)
                    transposed(s, 10)
                    l7_logits(s)
                    l7(s)

        @block.scalar
        def _(act):
            act.wait_ge(s_const, 16)
            act.wait_ge(s_first, 16)
            with act.Fori(0, TURNS) as c:
                link = Links("act", act, c)

                def keep_xT(s, k):
                    act.wait_ge(xTp[s], xTp.at(c, k))
                    nc.scalar.copy(xT[s][:, :], P[s][0][:, 0:256]).then_inc(xT_ready[s], 1)

                def l0_exps(s):
                    act.wait_ge(l0_qkv[s], l0_qkv.at(c))
                    nc.scalar.activation(l0_e[s][:, 0, :], P[s][1][:, 0:256], ACT.Exp)
                    kv = P[s][2][:, :].rearrange("p (t w d) -> p t w d", t=2, w=2)
                    nc.scalar.activation(l0_e[s][:, 1, :].rearrange("p (t d) -> p t d", t=2), kv[:, :, 0, :], ACT.Exp)
                    nc.scalar.copy(l0_v[s][:, :, 0:128], kv[:, :, 1, :]).then_inc(l0_v_in[s], 1)

                def l1_relu(s):
                    for e in range(E0):
                        act.wait_ge(l1_z[s], l1_z.at(c, 2 * e))
                        if e >= 2:
                            act.wait_ge(l1_y[s], l1_y.at(c, e - 2))
                        for f in range(2):
                            ins = nc.scalar.activation(ex_h[s][:, e % 2, f, :], P[s][2 * e % 3][:, 256 * f:256 * f + 256],
                                                       ACT.Relu, bias=W("l1_b1", 4 * e + f, 4 * e + f + 1))
                        ins.then_inc(l1_ha[s], 1)
                    act.wait_ge(l1_mTp[s], l1_mTp.at(c))
                    nc.scalar.copy(ex_mT[s][0:8, :], P[s][1][0:8, 0:256]).then_inc(l1_mT[s], 1)

                def l2_latent(s):
                    act.wait_ge(l2_ct[s], l2_ct.at(c))
                    nc.scalar.activation(at_ct[s], P[s][1][:, 0:256], ACT.Identity, bias=W("l2_down_b")
                                         ).then_inc(l2_cts[s], 1)

                def keep_stacks(s):
                    for n in range(4):
                        act.wait_ge(st_full[s], st_full.at(c, n))
                        dst = (kst if n < 2 else qst)[s]
                        nc.scalar.copy(dst[:, 2 * (n % 2):2 * (n % 2) + 2, :],
                                       P[s][n][:, :].rearrange("p (j n) -> p j n", j=2)).then_inc(st_in[s], 1)

                def masked(s, i, name, stacked, done, last=None):
                    if i == 0:
                        act.wait_ge(stacked[s], stacked.at(c, 3))
                    if i == 2:
                        act.wait_ge(last[s], last.at(c, 3))
                    if i == 3:
                        act.wait_ge(done[s], done.at(c, 2))
                    nc.scalar.mul(qmask[s][i], f32(qst[s]), C(name, i, i + 1)).then_inc(done[s], 1)

                def l6_masked(s, h):
                    if h == 0:
                        act.wait_ge(l6_qkd[s], l6_qkd.at(c))
                    if h > 7:
                        act.wait_ge(l6_a[s], l6_a.at(c, h - 8))
                    nc.scalar.mul(qm6[s][:, h % 8, :], f32(q6[s]), C("mask6", h, h + 1)).then_inc(l6_qm[s], 1)

                def l2_exps(s, i, j):
                    act.wait_ge(l2_st[s], l2_st.at(c, 4 * i + j))
                    if i and j == 0:
                        act.wait_ge(l2_pv[s], l2_pv.at(c, i - 1))
                    nc.scalar.activation(at_p[s][:, j, :], P[s][1 + j % 2][:, :], ACT.Exp, scale=1.0 / 12.0).then_inc(l2_p[s], 1)

                def l2_keep_o(s, i):
                    act.wait_ge(l2_pv[s], l2_pv.at(c, i))
                    nc.scalar.copy(at_o[s][:, i, :], P[s][3][:, 256 * (i % 2):256 * (i % 2) + 256]).then_inc(l2_ob[s], 1)

                def keep_shifted(s, k):
                    act.wait_ge(xTp[s], xTp.at(c, k))
                    nc.scalar.copy(shT[s][0:64, :], P[s][0][0:64, 0:256])
                    nc.scalar.copy(shT[s][64:128, 1:256], P[s][0][64:128, 0:255]).then_inc(xT_ready[s], 1)

                def l3_square(s, L, t):
                    act.wait_ge(l3_qkv[s], l3_qkv.at(c, 6 * L + 2 * t))
                    nc.scalar.activation(l3_sq[s][:, 1 - t, :], P[s][2 * t + 1][:, :], ACT.Square, scale=0.125).then_inc(l3_sqd[s], 1)

                def l3_square_q(s, L, t):
                    act.wait_ge(l3_qin[s], l3_qin.at(c, 2 * L + t))
                    for h in range(LH):
                        q = P[s][2 * t][:, LD * h:LD * h + LD]
                        ins = nc.scalar.activation(q, q, ACT.Square, scale=0.125, accum_out=lengths(s, t, 0)[:, h:h + 1])
                    ins.then_inc(l3_qsq[s], 1)

                def l3_keep_q(s, L, t):
                    act.wait_ge(l3_qkv[s], l3_qkv.at(c, 6 * L + 2 * t + 1))
                    if t:
                        act.wait_ge(l3_rot[s], l3_rot.at(c, 3 * L))
                    nc.scalar.copy(l3_qn[s][:, 0, :], P[s][2 * t][:, :]).then_inc(l3_qin[s], 1)

                def l3_keep_v(s, L):
                    for t in range(2):
                        act.wait_ge(l3_qkv[s], l3_qkv.at(c, 6 * L + 4 + t))
                        nc.scalar.copy(l3_v[s][:, t, :], P[s][t][:, :]).then_inc(l3_vin[s], 1)

                def l3_keep_pair(s, L, p):
                    act.wait_ge(l3_tp[s], l3_tp.at(c, 4 * L + p))
                    if p > 1:
                        act.wait_ge(l3_s[s], l3_s.at(c, 8 * L + 2 * p - 3))
                    nc.scalar.copy(qTm[s][0:64, p % 2, 0, :], P[s][3][0:64, 0:256])
                    nc.scalar.copy(qTm[s][64:128, p % 2, 1, :], P[s][3][64:128, 0:256])
                    nc.scalar.copy(l3_kT[s][:, p % 2, :], P[s][3][:, 256:512]).then_inc(l3_te[s], 1)

                def l3_exp(s, L, h):
                    act.wait_ge(l3_smd[s], l3_smd.at(c, 8 * L + h))
                    a = 96 + 2 * (h % 2)
                    for t, (lo, hi) in enumerate(((0, 128), (128, 384))):
                        b = l3_sm[s][:, h % 2, lo:hi]
                        ins = nc.scalar.activation(b, b, ACT.Exp, scale=-1.0, bias=tiny[s][:, a + t:a + t + 1],
                                                   accum_out=tiny[s][:, 128 + 8 * t + h:129 + 8 * t + h])
                    ins.then_inc(l3_e[s], 1)

                def l3_keep_oT(s, L, g):
                    act.wait_ge(l3_otp[s], l3_otp.at(c, 2 * L + g))
                    nc.scalar.copy(l3_oT[s][:, 2 * g:2 * g + 2, :], P[s][2 + g][:, :].rearrange("p (j n) -> p j n", j=2)
                                   ).then_inc(l3_ot[s], 1)

                def l3_affine(s, L):
                    act.wait_ge(l3_hnp[s], l3_hnp.at(c, L))
                    nc.scalar.activation(l3_hnT[s], P[s][2][:, 0:256], ACT.Identity, scale=W("l3_g", L, L + 1),
                                         bias=W("l3_b", L, L + 1)).then_inc(l3_hnTd[s], 1)

                def l3_gelu(s, L):
                    for f, (b, M) in enumerate(zip((0, 1, 3), FT)):
                        act.wait_ge(l3_z[s], l3_z.at(c, 3 * L + f))
                        k = 6 * L + 3 + f
                        nc.scalar.activation(l3_gl[s][0:M, f, :], P[s][b][0:M, 256:512], ACT.Gelu,
                                             bias=W("l3_b1", k, k + 1, rows=M)).then_inc(l3_gld[s], 1)

                def l4_keep_xT(s):
                    act.wait_ge(xTp[s], xTp.at(c, 7))
                    nc.scalar.mul(xT[s][:, :], P[s][0][:, 0:256], W("l4_gamma")).then_inc(xT_ready[s], 1)

                def l4_keep_stacks(s):
                    for n in range(4):
                        act.wait_ge(l4_stf[s], l4_stf.at(c, n))
                        dst = (kst if n < 2 else qst)[s]
                        nc.scalar.copy(dst[:, 2 * (n % 2):2 * (n % 2) + 2, :],
                                       P[s][n][:, :].rearrange("p (j n) -> p j n", j=2)).then_inc(l4_stin[s], 1)

                def l4_square(s, i, j):
                    n = 4 * i + j
                    act.wait_ge(l4_st[s], l4_st.at(c, n))
                    if i and j == 0:
                        act.wait_ge(l4_pv[s], l4_pv.at(c, i - 1))
                    nc.scalar.activation(at_p[s][:, j, :], P[s][n % 2][:, :], ACT.Square, scale=0.25 * 0.5 ** 0.5,
                                         bias=C("root_half")).then_inc(l4_sq[s], 1)

                def l4_keep_o(s):
                    act.wait_ge(l4_pv[s], l4_pv.at(c, 1))
                    act.wait_ge(l4_hsd[s], l4_hsd.at(c))
                    for i in range(2):
                        ins = nc.scalar.activation(at_o[s][:, i, :], P[s][2][:, 256 * i:256 * i + 256], ACT.Identity,
                                                   bias=tiny[s][:, 112 + i:113 + i])
                    ins.then_inc(l4_oin[s], 1)

                def l5_silu(s):
                    for f in range(4):
                        act.wait_ge(l5_z[s], l5_z.at(c, f))
                        if f > 1:
                            act.wait_ge(l5_h0[s], l5_h0.at(c, f - 2))
                        nc.scalar.activation(ex_g[s][:, f % 2, :], P[s][f % 3][:, 0:256], ACT.Silu,
                                             scale=W("l5_s1", f, f + 1)).then_inc(l5_sg[s], 1)

                def l5_gelu(s, n0, dst, scale, done):
                    for p in range(2):
                        act.wait_ge(l5_z[s], l5_z.at(c, n0 + p))
                        for f in range(2):
                            k = 2 * p + f
                            ins = nc.scalar.activation(dst[s][:, k, :], P[s][(n0 + p) % 3][:, 256 * f:256 * f + 256],
                                                       ACT.Gelu, scale=W(scale, k, k + 1))
                        ins.then_inc(done[s], 1)

                def l6_angles(s, step):
                    if step == 0:
                        act.wait_ge(l6_qk[s], l6_qk.at(c))
                        link(nc.scalar.activation(l6_th[s], P[s][0][:, :].rearrange("p (w n) -> p w n", w=2), ACT.Tanh))
                    else:
                        nc.scalar.activation(l6_cs[s], l6_th[s], ACT.Sin, scale=float(np.pi / 4),
                                             bias=C("half_pi")).then_inc(l6_csd[s], 1)

                def l6_keep_v(s, n):
                    t, k = divmod(n, 2)
                    act.wait_ge(l6_vp[s], l6_vp.at(c, n))
                    nc.scalar.copy(l6_v[s][:, t, 512 * k:512 * k + 512], P[s][(n + 1) % 4][:, :]).then_inc(l6_va[s], 1)

                def l6_keep_o(s, p):
                    act.wait_ge(l6_o[s], l6_o.at(c, 2 * p + 1))
                    if p == 0:
                        act.wait_ge(l6_qkd[s], l6_qkd.at(c))
                    nc.scalar.copy(l6_oT[s][:, p, :], P[s][2 + p % 2][:, 0:256]).then_inc(l6_ot[s], 1)

                def l7_sigmoid(s):
                    act.wait_ge(l7_lgb[s], l7_lgb.at(c))
                    nc.scalar.activation(ex_m2[s], ex_log[s], ACT.Sigmoid).then_inc(l7_pr[s], 1)

                def l7_silu(s, steps):
                    for n in steps:
                        act.wait_ge(l7_z[s], l7_z.at(c, n))
                        if n > 1:
                            act.wait_ge(l7_h[s], l7_h.at(c, n - 2))
                        nc.scalar.activation(ex_g[s][:, n % 2, :], P[s][n % 3][:, 0:256], ACT.Silu).then_inc(l7_sg[s], 1)

                for s in S2:
                    keep_xT(s, 0)
                for s in S2:
                    l0_exps(s)
                for s in S2:
                    keep_xT(s, 1)
                    l1_relu(s)
                act.wait_ge(s_small, 16)
                for s in S2:
                    keep_xT(s, 2)
                for s in S2:
                    l2_latent(s)
                for s in S2:
                    keep_stacks(s)
                    masked(s, 0, "mask2", st_in, l2_qm)
                for s in S2:
                    masked(s, 1, "mask2", st_in, l2_qm)
                for i in range(4):
                    for j in range(4):
                        for s in S2:
                            l2_exps(s, i, j)
                    for s in S2:
                        if i == 0:
                            masked(s, 2, "mask2", st_in, l2_qm, l2_st)
                    for s in S2:
                        l2_keep_o(s, i)
                        if i == 0:
                            masked(s, 3, "mask2", st_in, l2_qm)
                for L in range(2):
                    for s in S2:
                        keep_shifted(s, 3 + 2 * L)
                    for t in range(2):
                        for s in S2:
                            if t == 0:
                                l3_square(s, L, 0)
                        for s in S2:
                            l3_keep_q(s, L, t)
                        for s in S2:
                            if t == 0:
                                l3_square(s, L, 1)
                        for s in S2:
                            l3_square_q(s, L, t)
                    for s in S2:
                        l3_keep_v(s, L)
                    for s in S2:
                        l3_keep_pair(s, L, 0)
                    for h in range(LH):
                        for s in S2:
                            l3_exp(s, L, h)
                        if h in L3_PAIR:
                            for s in S2:
                                l3_keep_pair(s, L, L3_PAIR[h])
                    for g in range(2):
                        for s in S2:
                            l3_keep_oT(s, L, g)
                    for s in S2:
                        keep_shifted(s, 4 + 2 * L)
                    for s in S2:
                        l3_affine(s, L)
                    for s in S2:
                        l3_gelu(s, L)
                for s in S2:
                    l4_keep_xT(s)
                for s in S2:
                    l4_keep_stacks(s)
                    for i in range(2):
                        masked(s, i, "mask4", l4_stin, l4_qm)
                for i in range(2):
                    for j in range(4):
                        for s in S2:
                            l4_square(s, i, j)
                for s in S2:
                    l4_keep_o(s)
                for s in S2:
                    keep_xT(s, 8)
                for s in S2:
                    l5_silu(s)
                for s in S2:
                    l5_gelu(s, 4, l5_hB, "l5_h1s", l5_h1)
                for s in S2:
                    l5_gelu(s, 6, l5_hC, "l5_h2s", l5_h2)
                for s in S2:
                    keep_xT(s, 9)
                    l6_angles(s, 0)
                for s in S2:
                    l6_angles(s, 1)
                for n in range(4):
                    for s in S2:
                        l6_keep_v(s, n)
                for h in range(8):
                    for s in S2:
                        l6_masked(s, h)
                for p in range(8):
                    for s in S2:
                        if p < 4:
                            l6_masked(s, 8 + 2 * p)
                            l6_masked(s, 9 + 2 * p)
                    for s in S2:
                        l6_keep_o(s, p)
                for s in S2:
                    keep_xT(s, 10)
                    l7_silu(s, range(4))
                    l7_sigmoid(s)
                    l7_silu(s, range(4, 2 * E3))
                link.close()

        @block.vector
        def _(dve):
            v = nc.vector
            dve.wait_ge(s_const, 16)
            dve.wait_ge(s_first, 16)
            for s in S2:
                v.memset(qTm[s][:, :, :, :], 0.0)
                ins = v.memset(shT[s][64:128, 0:1], 0.0)
            ins.then_inc(s_zd, 1)
            for L in range(2):
                for w in range(2):
                    for k in range(2):
                        at = ((2 * L + w) * 2 + k) * 64
                        v.tensor_tensor(xpos[:, L, w, k, :, :], C("xpos").rearrange("p (w k t d) -> p w k t d", w=2, k=2, t=2)[:, w, k, :, :],
                                        W("l3_scale", at, at + 64).unsqueeze(1).to_broadcast([128, 2, 64]), ALU.mult
                                        ).then_inc(s_xpos, 1)
            dve.wait_ge(s_xpos, 8)
            settled[dve] = sem("dve_settled")
            for s in S2:
                dve.sem_inc(x_ready[s], 1)
            with dve.Fori(0, TURNS) as c:
                link = Links("dve", dve, c)

                def spreads(s):
                    for t in range(2):
                        ins = v.bn_stats(stats[s][:, t, :], res[s][:, t, :])
                    link(ins)
                    settle(dve)
                    for t in range(2):
                        ins = v.bn_aggr(mv[s][:, t, :], stats[s][:, t, :])
                    link(ins)
                    v.tensor_scalar(ve[s][:, :], mv[s][:, :, 1], LN_EPS, None, ALU.add).then_inc(var_ready[s], 1)

                def normed(s, n):
                    dve.wait_ge(rstd_ready[s], rstd_ready.at(c, n))
                    for t in range(2):
                        ins = v.tensor_scalar(x[s][:, t, :], res[s][:, t, :], mv[s][:, t, 0:1], rstd[s][:, t:t + 1],
                                              ALU.subtract, ALU.mult)
                    ins.then_inc(x_ready[s], 1)

                def norm(n, total=None):
                    for s in S2:
                        if total:
                            total(s)
                        spreads(s)
                    for s in S2:
                        normed(s, n)

                def l0_elu(s):
                    dve.wait_ge(l0_v_in[s], l0_v_in.at(c))
                    v.tensor_scalar(l0_r[s][:, 0, :], P[s][1][:, 0:256], 0.0, None, ALU.max)
                    kv = P[s][2][:, :].rearrange("p (t w d) -> p t w d", t=2, w=2)
                    link(v.tensor_scalar(l0_r[s][:, 1, :].rearrange("p (t d) -> p t d", t=2), kv[:, :, 0, :], 0.0, None, ALU.max))
                    v.scalar_tensor_tensor(out=l0_r[s][:, 0:2, :], in0=l0_e[s][:, 0:2, :], scalar=1.0,
                                           in1=l0_r[s][:, 0:2, :], op0=ALU.min, op1=ALU.add).then_inc(l0_qk[s], 1)

                def l0_keep(s):
                    dve.wait_ge(l0_kv[s], l0_kv.at(c))
                    v.tensor_copy(l0_kvs[s][:, 0:129], P[s][3][:, 0:129]).then_inc(l0_kvs_in[s], 1)

                def l0_mix(s):
                    dve.wait_ge(l0_out[s], l0_out.at(c))
                    y = P[s][1][:, 0:258].rearrange("p (t d) -> p t d", t=2)
                    link(v.tensor_scalar(tiny[s][:, 0:2], y[:, :, 128], 1e-6, None, ALU.add))
                    link(v.reciprocal(tiny[s][:, 2:4], tiny[s][:, 0:2]))
                    for t in range(2):
                        ins = v.scalar_tensor_tensor(out=res[s][:, t, :], in0=y[:, t, 0:128], scalar=tiny[s][:, 2 + t:3 + t],
                                                     in1=x[s][:, t, :], op0=ALU.mult, op1=ALU.add)
                    link(ins)

                def l1_route(s):
                    dve.wait_ge(l1_lg[s], l1_lg.at(c))
                    lg = P[s][3][:, 0:16].rearrange("p (t e) -> p t e", t=2)
                    for t in range(2):
                        ins = v.tensor_tensor(ex_m2[s][:, t, :], lg[:, t, :], W("l1_gb"), ALU.add)
                    link(ins)
                    for t in range(2):
                        ins = v.tensor_tensor(ex_log[s][:, t, :], ex_m2[s][:, t, :], W("l1_eb"), ALU.add)
                    link(ins)
                    settle(dve)
                    for t in range(2):
                        ins = v.max(ex_mx[s][:, t, :], ex_log[s][:, t, :])
                    link(ins)
                    settle(dve)
                    for t in range(2):
                        ins = v.max_index(idx[s][:, t, :], ex_mx[s][:, t, :], ex_log[s][:, t, :])
                    link(ins)
                    link(v.tensor_copy(ex_ix[s][:, :, :], idx[s][:, :, :]))
                    for t in range(2):
                        ins = v.tensor_scalar(ex_mk[s][:, t, :], C("iota8"), ex_ix[s][:, t, 0:1], None, ALU.is_equal)
                    ins.then_inc(l1_mask[s], 1)
                    dve.wait_ge(l1_mask[s], l1_mask.at(c))

                def l1_relu(s, e):
                    dve.wait_ge(l1_z[s], l1_z.at(c, 2 * e + 1))
                    if e >= 2:
                        dve.wait_ge(l1_y[s], l1_y.at(c, e - 2))
                    for f in range(2):
                        ins = v.tensor_scalar(ex_h[s][:, e % 2, 2 + f, :], P[s][(2 * e + 1) % 3][:, 256 * f:256 * f + 256],
                                              W("l1_b1", 4 * e + 2 + f, 4 * e + 3 + f), 0.0, ALU.add, ALU.max)
                    ins.then_inc(l1_hd[s], 1)

                def l1_add(s, e):
                    dve.wait_ge(l1_y[s], l1_y.at(c, e))
                    if e:
                        dve.wait_ge(l1_acc[s], l1_acc.at(c, e - 1))
                    for t in range(2):
                        y = P[s][3][:, 128 * t:128 * t + 128]
                        if e < E0:
                            ins = v.scalar_tensor_tensor(out=res[s][:, t, :], in0=y, scalar=ex_mk[s][:, t, e:e + 1],
                                                         in1=(res if e else x)[s][:, t, :], op0=ALU.mult, op1=ALU.add)
                        else:
                            ins = v.tensor_tensor(res[s][:, t, :], y, res[s][:, t, :], ALU.add)
                    ins.then_inc(l1_acc[s], 1)

                def l1(s):
                    l1_route(s)
                    l1_relu(s, 0)
                    for e in range(E0):
                        if e + 1 < E0:
                            l1_relu(s, e + 1)
                        l1_add(s, e)
                    l1_add(s, E0)
                    dve.wait_ge(l1_acc[s], l1_acc.at(c, E0))

                def rope(s, pair, plain, b_r, b_rs, b_c, w, src_ready):
                    t = at_rope[s]
                    v.scalar_tensor_tensor(out=t[:, 3 * w, :], in0=pair[:, 0:256], scalar=W(b_r), in1=C("rope_c"),
                                           op0=ALU.add, op1=ALU.mult)
                    link(v.scalar_tensor_tensor(out=t[:, 3 * w + 1, :], in0=pair[:, 256:512], scalar=W(b_rs), in1=C("rope_s"),
                                                op0=ALU.add, op1=ALU.mult))
                    if src_ready is not None:
                        dve.wait_ge(src_ready[s], src_ready.at(c))
                    link(v.scalar_tensor_tensor(out=t[:, 3 * w + 2, :], in0=plain, scalar=W(b_c), in1=t[:, 3 * w, :],
                                                op0=ALU.add, op1=ALU.add))
                    link(v.tensor_tensor(at_kq[s][:, w, :], t[:, 3 * w + 2, :], t[:, 3 * w + 1, :], ALU.add))

                def split(s):
                    for w in range(2):
                        ins = v.tensor_copy(parts[s][:, 2 * w, :], at_kq[s][:, w, :])
                    link(ins)
                    for w in range(2):
                        ins = v.tensor_tensor(parts[s][:, 2 * w + 1, :], at_kq[s][:, w, :], f32(parts[s][:, 2 * w, :]), ALU.subtract)
                    return ins

                def l2_kq(s):
                    dve.wait_ge(l2_kp[s], l2_kp.at(c))
                    rope(s, P[s][2], P[s][0][:, 256:512], "l2_krb", "l2_krsb", "l2_kcb", 0, l2_qp)
                    rope(s, P[s][3], P[s][0][:, 0:256], "l2_qrb", "l2_qrsb", "l2_qcb", 1, None)
                    split(s).then_inc(l2_split[s], 1)

                def l2_vals(s):
                    dve.wait_ge(l2_v[s], l2_v.at(c))
                    dve.wait_ge(l2_xb[s], l2_xb.at(c))
                    for t in range(2):
                        ins = v.tensor_tensor(at_v[s][:, t, :, 0:DH1],
                                              P[s][1][:, 128 * t:128 * t + 128].rearrange("p (h d) -> p h d", h=H1),
                                              W("l2_vb").rearrange("p (h d) -> p h d", h=H1), ALU.add)
                    ins.then_inc(l2_vs[s], 1)

                def l2_maxes(s, i, j):
                    dve.wait_ge(l2_s[s], l2_s.at(c, 4 * i + j))
                    if i and j == 0:
                        dve.wait_ge(l2_m[s], l2_m.at(c, i - 1))
                    v.tensor_reduce(m_tok[s][:, :, j], P[s][0][:, :].rearrange("p (t k) -> p t k", t=2), X, ALU.max
                                    ).then_inc(l2_su[s], 1)

                def l2_max_rows(s, i):
                    dve.wait_ge(l2_m[s], l2_m.at(c, i))
                    if i:
                        dve.wait_ge(l2_st[s], l2_st.at(c, 4 * i - 1))
                    bank = P[s][0]
                    link(v.tensor_copy(mT[s][0:4, :], bank[0:4, 0:256]))
                    v.tensor_tensor(mT[s][32:36, :], bank[0:4, 0:256], f32(mT[s][0:4, :]), ALU.subtract).then_inc(l2_mu[s], 1)

                def l2_recip(s):
                    dve.wait_ge(l2_dn[s], l2_dn.at(c))
                    v.reciprocal(inverse[s], P[s][0][:, 0:32]).then_inc(l2_rb[s], 1)

                def divide(s, n, src, done):
                    dve.wait_ge(src[s], src.at(c))
                    for b in range(n // 2):
                        o = at_o[s][:, 2 * b:2 * b + 2, :]
                        ins = v.tensor_tensor(o, o, P[s][b][:, :].rearrange("p (i n) -> p i n", i=2), ALU.mult)
                    ins.then_inc(done[s], 1)

                def l2_sum(s):
                    dve.wait_ge(l2_y[s], l2_y.at(c))
                    dve.wait_ge(l2_xb[s], l2_xb.at(c))
                    link(v.tensor_tensor(res[s][:, :, :], P[s][2][:, 0:256].rearrange("p (t d) -> p t d", t=2), at_xb[s], ALU.add))

                def l3_reduce(s, L, t):
                    dve.wait_ge(l3_sqd[s], l3_sqd.at(c, 2 * L + t))
                    v.tensor_reduce(lengths(s, t, 1), l3_sq[s][:, 1 - t, :].rearrange("p (h d) -> p h d", h=LH), X, ALU.add
                                    ).then_inc(l3_ss[s], 1)

                def l3_clamp(s, L, t):
                    dve.wait_ge(l3_ss[s], l3_ss.at(c, 2 * L + t))
                    q = lengths(s, t, 1)
                    v.tensor_scalar(q, q, 1e-24 / 64, None, ALU.max).then_inc(l3_len[s], 1)

                def l3_clamp_q(s, L):
                    dve.wait_ge(l3_qsq[s], l3_qsq.at(c, 2 * L + 1))
                    q = tiny[s][:, 0:16]
                    v.tensor_scalar(q, q, 1e-24 / 64, None, ALU.max).then_inc(l3_len[s], 1)

                def l3_unit(s, L, t):
                    dve.wait_ge(l3_rn[s], l3_rn.at(c, 3 * L + t))
                    if t:
                        dve.wait_ge(l3_rot[s], l3_rot.at(c, 3 * L + 1))
                    rn = inverses(s, t, 1).unsqueeze(2).to_broadcast([128, LH, LD])
                    v.tensor_tensor(l3_qn[s][:, 1, :].rearrange("p (h d) -> p h d", h=LH),
                                    P[s][2 * t + 1][:, :].rearrange("p (h d) -> p h d", h=LH), rn, ALU.mult).then_inc(l3_qnd[s], 1)

                def l3_sines(s, L, i):
                    t, w = divmod(i, 2)
                    done = l3_qnd if w else l3_qin
                    dve.wait_ge(done[s], done.at(c, 2 * L + t))
                    if i:
                        dve.wait_ge(l3_rot[s], l3_rot.at(c, 3 * L + (1 if i == 3 else 0)))
                    return sine_part(v, L, w, t, l3_qn[s][:, w, :], l3_b[s])

                def l3_cosines(s, L, t):
                    cos = xpos[:, L, 1, 0, t, :].unsqueeze(1).to_broadcast([128, LH, LD])
                    link(v.tensor_tensor(l3_a[s][1].rearrange("p (h d) -> p h d", h=LH),
                                         l3_qn[s][:, 1, :].rearrange("p (h d) -> p h d", h=LH), cos, ALU.mult))

                def l3_rotated(s, L, i):
                    t, w = divmod(i, 2)
                    if w == 0:
                        dve.wait_ge(l3_ad[s], l3_ad.at(c, L))
                    v.tensor_tensor(l3_tok[s][:, w, t, :], l3_a[s][w], l3_b[s], ALU.add).then_inc(l3_rot[s], 1)

                def l3_mask(s, L, h):
                    dve.wait_ge(l3_s[s], l3_s.at(c, 8 * L + h))
                    if h == 0:
                        dve.wait_ge(l3_rn[s], l3_rn.at(c, 3 * L + 2))
                    a = 96 + 2 * (h % 2)
                    settle(dve)
                    for t, (lo, hi) in enumerate(((0, 128), (128, 384))):
                        ins = v.tensor_tensor_reduce(l3_sm[s][:, h % 2, lo:hi], P[s][h % 2][:, lo:hi], C("band", lo, hi),
                                                     inverses(s, t, 0)[:, h:h + 1], 3.0e38, ALU.add, ALU.min, tiny[s][:, a + t:a + t + 1])
                    ins.then_inc(l3_smd[s], 1)

                def l3_keep_pT(s, L, h):
                    dve.wait_ge(l3_pt[s], l3_pt.at(c, 8 * L + h))
                    v.tensor_copy(l3_pT[s][:, h % 2, :], P[s][h % 2][:, 0:384]).then_inc(l3_pte[s], 1)

                def l3_divide(s, L, g):
                    dve.wait_ge(l3_e[s], l3_e.at(c, 8 * L + 4 * g + 3))
                    total = tiny[s][:, 128:144].rearrange("p (t h) -> p t h", t=2)[:, :, 4 * g:4 * g + 4]
                    inverse = tiny[s][:, 144:160].rearrange("p (t h) -> p t h", t=2)[:, :, 4 * g:4 * g + 4]
                    link(v.reciprocal(inverse, total))
                    dve.wait_ge(l3_o[s], l3_o.at(c, 2 * L + g))
                    for t in range(2):
                        ins = v.tensor_tensor(l3_o_tok[s][:, t, 256 * g:256 * g + 256].rearrange("p (h d) -> p h d", h=4),
                                              P[s][2 + g][:, 256 * t:256 * t + 256].rearrange("p (h d) -> p h d", h=4),
                                              inverse[:, t, :].unsqueeze(2).to_broadcast([128, 4, LD]), ALU.mult)
                    ins.then_inc(l3_on[s], 1)

                def l3_mid(s, L):
                    dve.wait_ge(l3_y[s], l3_y.at(c, L))
                    if L == 0:
                        v.tensor_copy(res[s][:, :, :], x[s][:, :, :])
                    v.tensor_tensor(x[s][:, :, :], P[s][2][:, 0:256].rearrange("p (t d) -> p t d", t=2), x[s][:, :, :],
                                    ALU.add).then_inc(x_ready[s], 1)

                def l3_spreads(s, L):
                    dve.wait_ge(l3_hs[s], l3_hs.at(c, L))
                    for t in range(2):
                        ins = v.bn_stats(stats[s][:, t, :], P[s][1][:, 128 * t:128 * t + 128])
                    link(ins)
                    settle(dve)
                    for t in range(2):
                        ins = v.bn_aggr(mv[s][:, t, :], stats[s][:, t, :])
                    link(ins)
                    v.tensor_scalar(ve[s][:, :], mv[s][:, :, 1], LN_EPS, None, ALU.add).then_inc(var_ready[s], 1)

                def l3_norm(s, L):
                    dve.wait_ge(rstd_ready[s], rstd_ready.at(c, 3 + L))
                    for t in range(2):
                        ins = v.tensor_scalar(l3_hn[s][:, t, :], P[s][1][:, 128 * t:128 * t + 128], mv[s][:, t, 0:1],
                                              rstd[s][:, t:t + 1], ALU.subtract, ALU.mult)
                    ins.then_inc(l3_hnd[s], 1)

                def l3_glu(s, L):
                    for f, (b, M) in enumerate(zip((0, 1, 3), FT)):
                        dve.wait_ge(l3_gld[s], l3_gld.at(c, 3 * L + f))
                        k = 6 * L + f
                        v.scalar_tensor_tensor(out=l3_hh[s][0:M, f, :], in0=P[s][b][0:M, 0:256], scalar=W("l3_b1", k, k + 1, rows=M),
                                               in1=l3_gl[s][0:M, f, :], op0=ALU.add, op1=ALU.mult).then_inc(l3_h[s], 1)

                def l3_end(s, L):
                    dve.wait_ge(l3_y2[s], l3_y2.at(c, L))
                    dve.wait_ge(l3_xbd[s], l3_xbd.at(c, L))
                    y = P[s][2][:, 0:256].rearrange("p (t d) -> p t d", t=2)
                    if L == 0:
                        v.tensor_tensor(x[s][:, :, :], y, l3_xb[s], ALU.add).then_inc(x_ready[s], 1)
                    else:
                        link(v.tensor_tensor(res[s][:, :, :], y, l3_xb[s], ALU.add))

                def l4_sumsq(s):
                    dve.wait_ge(x_ready[s], x_ready.at(c, 6))
                    settle(dve)
                    for t in range(2):
                        ins = v.tensor_tensor_reduce(res[s][:, t, :], x[s][:, t, :], x[s][:, t, :], 1.0, 0.0, ALU.mult, ALU.add,
                                                     tiny[s][:, t:t + 1])
                    link(ins)
                    v.tensor_scalar(tiny[s][:, 2:4], tiny[s][:, 0:2], 1e-24, None, ALU.max).then_inc(l4_ss[s], 1)

                def l4_normed(s):
                    dve.wait_ge(l4_rn[s], l4_rn.at(c))
                    for t in range(2):
                        ins = v.tensor_scalar(l4_xn[s][:, t, :], x[s][:, t, :], tiny[s][:, 4 + t:5 + t], float(D) ** 0.5,
                                              ALU.mult, ALU.mult)
                    ins.then_inc(l4_xnd[s], 1)

                def l4_parts(s):
                    dve.wait_ge(l4_p[s], l4_p.at(c))
                    for w in range(2):
                        ins = v.tensor_copy(parts[s][:, 2 * w, :], P[s][1][:, 256 * w:256 * w + 256])
                    link(ins)
                    for w in range(2):
                        ins = v.tensor_tensor(parts[s][:, 2 * w + 1, :], P[s][1][:, 256 * w:256 * w + 256],
                                              f32(parts[s][:, 2 * w, :]), ALU.subtract)
                    ins.then_inc(l4_split[s], 1)
                    dve.wait_ge(l4_vset[s], l4_vset.at(c))
                    for t in range(2):
                        ins = v.tensor_copy(l4_v[s][:, t, :, 0:DH2], P[s][2][:, 128 * t:128 * t + 128].rearrange("p (h d) -> p h d", h=H2))
                    ins.then_inc(l4_vd[s], 1)

                def l4_halves(s):
                    dve.wait_ge(l4_hs[s], l4_hs.at(c))
                    v.tensor_copy(tiny[s][:, 112:114], P[s][3][:, 0:2]).then_inc(l4_hsd[s], 1)

                def l4_recip(s):
                    dve.wait_ge(l4_dn[s], l4_dn.at(c))
                    link(v.tensor_scalar(tiny[s][:, 120:136], P[s][0][:, 0:16], 1e-5, None, ALU.max))
                    v.reciprocal(inverse[s][:, 0:16], tiny[s][:, 120:136]).then_inc(l4_rb[s], 1)

                def l4_sum(s):
                    dve.wait_ge(l4_y[s], l4_y.at(c))
                    link(v.tensor_tensor(res[s][:, :, :], P[s][3][:, 0:256].rearrange("p (t d) -> p t d", t=2), x[s][:, :, :], ALU.add))

                def l5_gate(s):
                    for f in range(4):
                        dve.wait_ge(l5_sg[s], l5_sg.at(c, f))
                        v.scalar_tensor_tensor(out=l5_hA[s][:, f, :], in0=P[s][f % 3][:, 256:512], scalar=W("l5_s2", f, f + 1),
                                               in1=ex_g[s][:, f % 2, :], op0=ALU.mult, op1=ALU.mult).then_inc(l5_h0[s], 1)

                def l5_sum(s):
                    dve.wait_ge(l5_yd[s], l5_yd.at(c))
                    link(v.tensor_tensor(l5_y[s], P[s][3][:, 0:256].rearrange("p (t d) -> p t d", t=2),
                                         W("l5_s3").unsqueeze(1).to_broadcast([128, 2, 128]), ALU.mult))
                    link(v.tensor_tensor(res[s][:, :, :], l5_y[s], x[s][:, :, :], ALU.add))

                def l6_cumulate(s):
                    dve.wait_ge(l6_csd[s], l6_csd.at(c))
                    link(v.tensor_tensor_scan(l6_cum[s], C("ones"), l6_cs[s][:, 1, :], 0.0, ALU.mult, ALU.add))
                    v.tensor_tensor(l6_prod[s], l6_cum[s], l6_cs[s][:, 0, :], ALU.mult).then_inc(l6_pr[s], 1)

                def l6_key_parts(s):
                    link(v.tensor_copy(k6[s], l6_cs[s][:, 1, :]))
                    v.tensor_tensor(k6[s][64:128, :], l6_cs[s][64:128, 1, :], f32(k6[s][64:128, :]), ALU.subtract)

                def l6_parts(s):
                    dve.wait_ge(l6_dn[s], l6_dn.at(c))
                    link(v.tensor_scalar(l6_den[s], P[s][1][:, 0:256], 1e-6, None, ALU.add))
                    link(v.reciprocal(l6_rd[s], l6_den[s]))
                    link(v.tensor_tensor(l6_qn[s], l6_cs[s][:, 0, :], l6_rd[s], ALU.mult))
                    link(v.tensor_copy(q6[s], l6_qn[s]))
                    for a in (32, 96):
                        ins = v.tensor_tensor(q6[s][a:a + 32, :], l6_qn[s][a:a + 32, :], f32(q6[s][a:a + 32, :]), ALU.subtract)
                    ins.then_inc(l6_qkd[s], 1)

                def l6_causal(s, h):
                    dve.wait_ge(l6_a[s], l6_a.at(c, h))
                    if h > 3:
                        dve.wait_ge(l6_o[s], l6_o.at(c, h - 4))
                    v.tensor_tensor(l6_at[s][:, h % 4, :], P[s][h % 2][:, 0:384], C("tri"), ALU.mult).then_inc(l6_atd[s], 1)

                def l6_sum(s):
                    dve.wait_ge(l6_yd[s], l6_yd.at(c))
                    link(v.tensor_tensor(res[s][:, :, :], P[s][0][:, 0:256].rearrange("p (t d) -> p t d", t=2), x[s][:, :, :], ALU.add))

                def l7_bias(s):
                    dve.wait_ge(l7_lg[s], l7_lg.at(c))
                    v.tensor_tensor(ex_log[s], P[s][3][:, 0:16].rearrange("p (t e) -> p t e", t=2),
                                    W("l7_rb").unsqueeze(1).to_broadcast([128, 2, 8]), ALU.add).then_inc(l7_lgb[s], 1)

                def l7_route(s):
                    dve.wait_ge(l7_pr[s], l7_pr.at(c))
                    settle(dve)
                    for t in range(2):
                        ins = v.max(ex_mx[s][:, t, :], ex_m2[s][:, t, :])
                    link(ins)
                    settle(dve)
                    for t in range(2):
                        ins = v.max_index(idx[s][:, t, :], ex_mx[s][:, t, :], ex_m2[s][:, t, :])
                    link(ins)
                    link(v.tensor_copy(ex_ix[s], idx[s][:, :, :]))
                    for t in range(2):
                        ins = v.tensor_scalar(ex_log[s][:, t, :], C("iota8"), ex_ix[s][:, t, 0:1], None, ALU.is_equal)
                    link(ins)
                    for t in range(2):
                        ins = v.scalar_tensor_tensor(out=ex_mx[s][:, t, :], in0=C("iota8"), scalar=ex_ix[s][:, t, 1:2],
                                                     in1=ex_log[s][:, t, :], op0=ALU.is_equal, op1=ALU.add)
                    link(ins)
                    link(v.tensor_tensor(ex_mk[s], ex_mx[s], ex_m2[s], ALU.mult))

                def l7_gate(s, n):
                    dve.wait_ge(l7_sg[s], l7_sg.at(c, n))
                    if n > 3:
                        dve.wait_ge(l7_y[s], l7_y.at(c, n // 2 - 2))
                    v.tensor_tensor(ex_h[s][:, n // 2 % 2, n % 2, :], P[s][n % 3][:, 256:512], ex_g[s][:, n % 2, :], ALU.mult
                                    ).then_inc(l7_h[s], 1)

                def l7_add(s, e):
                    dve.wait_ge(l7_y[s], l7_y.at(c, e))
                    if e:
                        dve.wait_ge(l7_acc[s], l7_acc.at(c, e - 1))
                    for t in range(2):
                        y = P[s][3][:, 128 * t:128 * t + 128]
                        if e:
                            ins = v.scalar_tensor_tensor(out=res[s][:, t, :], in0=y, scalar=ex_mk[s][:, t, e - 1:e],
                                                         in1=res[s][:, t, :], op0=ALU.mult, op1=ALU.add)
                        else:
                            ins = v.tensor_tensor(res[s][:, t, :], y, x[s][:, t, :], ALU.add)
                    ins.then_inc(l7_acc[s], 1)

                def l7(s):
                    l7_bias(s)
                    for n in range(2):
                        l7_gate(s, n)
                    for e in range(E3):
                        if e + 1 < E3:
                            l7_gate(s, 2 * e + 2)
                            l7_gate(s, 2 * e + 3)
                        l7_add(s, e)
                        if e == 0:
                            l7_route(s)
                    dve.wait_ge(l7_acc[s], l7_acc.at(c, E3 - 1))

                for s in S2:
                    l0_elu(s)
                for s in S2:
                    l0_keep(s)
                norm(0, l0_mix)
                for s in S2:
                    l1(s)
                    spreads(s)
                    normed(s, 1)
                dve.wait_ge(s_small, 16)
                for s in S2:
                    l2_kq(s)
                    l2_vals(s)
                for i in range(4):
                    for j in range(4):
                        for s in S2:
                            l2_maxes(s, i, j)
                    for s in S2:
                        l2_max_rows(s, i)
                for s in S2:
                    l2_recip(s)
                for s in S2:
                    divide(s, 4, l2_bc, l2_on)
                norm(2, l2_sum)
                for L in range(2):
                    for s in S2:
                        l3_reduce(s, L, 0)
                    for s in S2:
                        l3_clamp(s, L, 0)
                    for t in range(2):
                        if t == 0:
                            for s in S2:
                                link(l3_sines(s, L, 0))
                            for s in S2:
                                l3_reduce(s, L, 1)
                            for s in S2:
                                l3_clamp(s, L, 1)
                            for s in S2:
                                l3_rotated(s, L, 0)
                        if t:
                            for s in S2:
                                l3_clamp_q(s, L)
                        for s in S2:
                            l3_unit(s, L, t)
                        for s in S2:
                            l3_sines(s, L, 2 * t + 1)
                            l3_cosines(s, L, t)
                        for s in S2:
                            l3_rotated(s, L, 2 * t + 1)
                    for h in range(LH + 1):
                        if h < LH:
                            for s in S2:
                                l3_mask(s, L, h)
                        if h:
                            for s in S2:
                                l3_keep_pT(s, L, h - 1)
                        if h == 6:
                            for s in S2:
                                l3_divide(s, L, 0)
                    for s in S2:
                        l3_divide(s, L, 1)
                    for s in S2:
                        l3_mid(s, L)
                    for s in S2:
                        l3_spreads(s, L)
                    for s in S2:
                        l3_norm(s, L)
                    for s in S2:
                        l3_glu(s, L)
                    for s in S2:
                        l3_end(s, L)
                        if L:
                            spreads(s)
                for s in S2:
                    normed(s, 5)
                for s in S2:
                    l4_sumsq(s)
                for s in S2:
                    l4_normed(s)
                for s in S2:
                    l4_parts(s)
                for s in S2:
                    l4_halves(s)
                for s in S2:
                    l4_recip(s)
                for s in S2:
                    divide(s, 2, l4_bc, l4_on)
                norm(6, l4_sum)
                for s in S2:
                    l5_gate(s)
                for s in S2:
                    l5_sum(s)
                    spreads(s)
                    normed(s, 7)
                for s in S2:
                    l6_cumulate(s)
                for s in S2:
                    l6_key_parts(s)
                for s in S2:
                    l6_parts(s)
                for h in range(H3):
                    for s in S2:
                        l6_causal(s, h)
                norm(8, l6_sum)
                for s in S2:
                    l7(s)
                    spreads(s)
                    normed(s, 9)
                link.close()

        @block.gpsimd
        def _(pool):
            g = nc.gpsimd
            pool.wait_ge(s_const, 16)
            for s in S2:
                ins = g.memset(f32(mT[s]), 0.0)
            ins.then_inc(s_zero, 1)
            pool.wait_ge(s_stage, 16)
            g.tensor_copy(constr[:, :], region_b[:, 0:N_CONSTR]).then_inc(s_constr, 1)
            settled[pool] = sem("pool_settled")
            with pool.Fori(0, TURNS) as c:
                link = Links("pool", pool, c)

                def rsqrt(s, n):
                    pool.wait_ge(var_ready[s], var_ready.at(c, n))
                    g.tensor_tensor(rstd[s][:, :], ve[s][:, :], C("mhalf", 0, 2), ALU.pow).then_inc(rstd_ready[s], 1)

                def l2_prepare(s):
                    pool.wait_ge(x_ready[s], x_ready.at(c, X_OF[2]))
                    g.tensor_tensor(at_xb[s], x[s][:, :, :], W("l2_ob").unsqueeze(1).to_broadcast([128, 2, 128]), ALU.add)
                    link(g.memset(at_v[s], 0.0))
                    settle(pool)
                    g.memset(at_v[s][:, :, :, DH1:DH1 + 1], 1.0).then_inc(l2_xb[s], 1)

                def l3_norms(s, L, n):
                    pool.wait_ge(l3_len[s], l3_len.at(c, 3 * L + n))
                    a, b = (0, 16) if n == 2 else (16 + 8 * n, 24 + 8 * n)
                    g.tensor_tensor(tiny[s][:, 32 + a:32 + b], tiny[s][:, a:b], C("mhalf", 0, b - a), ALU.pow).then_inc(l3_rn[s], 1)

                def l3_cos(s, L, t):
                    pool.wait_ge(l3_qin[s], l3_qin.at(c, 2 * L + t))
                    if t:
                        pool.wait_ge(l3_rot[s], l3_rot.at(c, 3 * L))
                    cos = xpos[:, L, 0, 0, t, :].unsqueeze(1).to_broadcast([128, LH, LD])
                    ins = g.tensor_tensor(l3_a[s][0].rearrange("p (h d) -> p h d", h=LH),
                                          l3_qn[s][:, 0, :].rearrange("p (h d) -> p h d", h=LH), cos, ALU.mult)
                    if t == 0:
                        ins.then_inc(l3_ad[s], 1)
                    else:
                        link(sine_part(g, L, 0, 1, l3_qn[s][:, 0, :], l3_bq[s]))
                        g.tensor_tensor(l3_tok[s][:, 0, 1, :], l3_a[s][0], l3_bq[s], ALU.add).then_inc(l3_rotq[s], 1)

                def l3_bias(s, L):
                    pool.wait_ge(x_ready[s], x_ready.at(c, 3 + 2 * L))
                    ins = g.tensor_tensor(l3_xb[s], x[s][:, :, :], W("l3_b2", 128 * L, 128 * L + 128).unsqueeze(1).to_broadcast([128, 2, 128]),
                                          ALU.add)
                    if L:
                        link(ins)
                        ins = g.tensor_tensor(l3_xb[s], l3_xb[s], res[s][:, :, :], ALU.add)
                    ins.then_inc(l3_xbd[s], 1)

                def l4_norms(s):
                    pool.wait_ge(l4_ss[s], l4_ss.at(c))
                    g.tensor_tensor(tiny[s][:, 4:6], tiny[s][:, 2:4], C("mhalf", 0, 2), ALU.pow).then_inc(l4_rn[s], 1)
                    link(g.memset(l4_v[s], 0.0))
                    settle(pool)
                    g.memset(l4_v[s][:, :, :, DH2:DH2 + 1], 1.0).then_inc(l4_vset[s], 1)

                for s in S2:
                    pool.wait_ge(x_ready[s], x_ready.at(c, -1))
                    settle(pool)
                    g.memset(l0_v[s][:, :, 128:129], 1.0).then_inc(l0_ones[s], 1)
                for s in S2:
                    rsqrt(s, 0)
                for s in S2:
                    rsqrt(s, 1)
                pool.wait_ge(s_small, 16)
                for s in S2:
                    l2_prepare(s)
                for s in S2:
                    rsqrt(s, 2)
                for L in range(2):
                    for t in range(2):
                        for s in S2:
                            l3_norms(s, L, t)
                        for s in S2:
                            l3_cos(s, L, t)
                    for s in S2:
                        l3_norms(s, L, 2)
                    for s in S2:
                        l3_bias(s, L)
                        rsqrt(s, 3 + L)
                for s in S2:
                    rsqrt(s, 5)
                for s in S2:
                    l4_norms(s)
                for s in S2:
                    rsqrt(s, 6)
                for s in S2:
                    rsqrt(s, 7)
                for s in S2:
                    rsqrt(s, 8)
                for s in S2:
                    rsqrt(s, 9)
                link.close()


def pack(a):
    f = np.float32
    small = np.zeros((128, N_SMALL), f)

    def put(name, v, rows=128):
        at, n = SMALL[name]
        small[:rows, at:at + n] = np.asarray(v, f).reshape(rows, n)

    def bc(v):
        return np.broadcast_to(np.asarray(v, f).reshape(1, -1), (128, np.size(v)))

    put("l0_w", a["L0_attn_W"])
    put("l1_gate", a["L0_ffn_gate_w"].T)
    put("l1_gb", bc(a["L0_ffn_gate_b"]))
    put("l1_eb", bc(a["L0_ffn_expert_bias"]))
    put("l1_b1", a["L0_ffn_b1"].reshape(E0, 4, 128).transpose(2, 0, 1))
    put("l1_b2", a["L0_ffn_b2"], 8)
    l1 = np.concatenate([a["L0_ffn_w1"].transpose(1, 0, 2).reshape(128, -1),
                         a["L0_ffn_w2"].reshape(E0, 4, 128, D).transpose(2, 0, 1, 3).reshape(128, -1)], 1)
    swap = np.arange(128) ^ 1
    q_rows = lambda w: np.concatenate([w, np.zeros((64, w.shape[1]), f)], 0)
    kv_rows = lambda w: np.concatenate([np.zeros((64, w.shape[1]), f), w], 0)
    put("l2_down", np.concatenate([a["L1_attn_Wd_q_w"], a["L1_attn_Wd_kv_w"]], 1))
    put("l2_down_b", np.concatenate([a["L1_attn_Wd_q_b"], a["L1_attn_Wd_kv_b"]]))
    put("l2_qc", q_rows(a["L1_attn_Wu_q_w"]))
    put("l2_qr", q_rows(a["L1_attn_Wq_r_w"]))
    put("l2_qrs", q_rows(a["L1_attn_Wq_r_w"][:, swap]))
    put("l2_kc", kv_rows(a["L1_attn_Wu_k_w"]))
    put("l2_kr", a["L1_attn_Wk_r_w"])
    put("l2_krs", a["L1_attn_Wk_r_w"][:, swap])
    put("l2_v", kv_rows(a["L1_attn_Wu_v_w"]))
    put("l2_qcb", a["L1_attn_Wu_q_b"])
    put("l2_qrb", a["L1_attn_Wq_r_b"])
    put("l2_qrsb", a["L1_attn_Wq_r_b"][swap])
    put("l2_kcb", a["L1_attn_Wu_k_b"])
    put("l2_krb", a["L1_attn_Wk_r_b"])
    put("l2_krsb", a["L1_attn_Wk_r_b"][swap])
    put("l2_vb", bc(a["L1_attn_Wu_v_b"]))
    put("l2_ob", bc(a["L1_attn_Wo_b"]))
    o = np.zeros((4, 32, 4, D), f)
    o[:, 0:DH1] = a["L1_attn_Wo_w"].reshape(4, 4, DH1, D).transpose(0, 2, 1, 3)
    put("l2_o", o)
    l3 = np.zeros((128, 2, N_L3W), f)
    for L in range(2):
        at, n = L3W["qkv"]
        l3[:, L, at:at + n] = a["L1_ffn_wqkv"][L]
        at, n = L3W["o"]
        l3[:, L, at:at + n] = a["L1_ffn_wo"][L].reshape(4, 128, D).transpose(1, 0, 2).reshape(128, -1)
        at, n = L3W["w1"]
        l3[:, L, at:at + n] = a["L1_ffn_w1"][L]
        at, n = L3W["w2"]
        w2 = np.zeros((3, 128, D), f)
        w2.reshape(384, D)[0:HID] = a["L1_ffn_w2"][L]
        l3[:, L, at:at + n] = w2.transpose(1, 0, 2).reshape(128, -1)
    put("l3_g", a["L1_ffn_ln_g"].T)
    put("l3_b", a["L1_ffn_ln_b"].T)
    b1 = np.zeros((2, 2, 384), f)
    b1[:, :, 0:HID] = a["L1_ffn_b1"].reshape(2, 2, HID)
    put("l3_b1", b1.reshape(2, 2, 3, 128).transpose(3, 0, 1, 2))
    put("l3_b2", bc(a["L1_ffn_b2"]))
    rot = (np.arange(LD) + LD // 2) % LD
    qk = np.stack([a["L1_ffn_q_scale"], a["L1_ffn_k_scale"]], 1)
    put("l3_scale", bc(np.stack([qk, qk[:, :, rot]], 2)))
    put("l4_gamma", a["L2_attn_gamma"])
    put("l4_w", np.concatenate([a["L2_attn_w_q"], a["L2_attn_w_kv"]], 1))
    o = np.zeros((4, 32, 2, D), f)
    o[:, 0:DH2] = a["L2_attn_w_out"].reshape(4, 2, DH2, D).transpose(0, 2, 1, 3)
    put("l4_o", o)
    blocks = lambda w: w.T.reshape(w.shape[1] // 128, 128, w.shape[0]).transpose(1, 0, 2).reshape(128, -1)
    l5 = np.concatenate([blocks(a[f"L2_ffn_{n}_w"]) for n in ("w1", "w2", "h1", "h2", "w3")], 1)
    for n, k in (("l5_s1", "w1"), ("l5_s2", "w2"), ("l5_h1s", "h1"), ("l5_h2s", "h2")):
        put(n, a[f"L2_ffn_{k}_s"].reshape(4, 128).T)
    put("l5_s3", bc(a["L2_ffn_w3_s"]))
    wq, wk = a["L3_attn_W_Q"][:, :, 0].T, a["L3_attn_W_K"][:, :, 0].T
    put("l6_q", np.concatenate([wq] * 8, 1))
    put("l6_k", np.concatenate([wk] * 8, 1))
    put("l6_v", a["L3_attn_W_V"].transpose(1, 0, 2))
    put("l6_o", a["L3_attn_W_O"].transpose(2, 1, 0).reshape(8, 128, D).transpose(1, 0, 2))
    wg = np.concatenate([a["L3_ffn_Wg_s"][None], a["L3_ffn_Wg"]], 0)
    wu = np.concatenate([a["L3_ffn_Wu_s"][None], a["L3_ffn_Wu"]], 0)
    wd = np.concatenate([a["L3_ffn_Wd_s"][None], a["L3_ffn_Wd"]], 0)
    l7 = np.concatenate([wg.transpose(2, 0, 1), wu.transpose(2, 0, 1),
                         wd.transpose(0, 2, 1).reshape(E3, 2, 128, D).transpose(2, 0, 1, 3).reshape(128, E3, 2 * D)],
                        2).reshape(128, -1)
    put("l7_gate", a["L3_ffn_Wr"].T)
    put("l7_rb", bc(a["L3_ffn_rb"]))
    const, constr = shape_constants()
    x = np.concatenate([a["L0_attn_x"], np.zeros((STREAMS, SEQ, D), f)], 0)
    out = dict(x=x, small=small, l1=l1, l3=l3.reshape(128, -1), l5=l5, l7=l7, const=const, constr=constr)
    return {k: np.ascontiguousarray(v, f) for k, v in out.items()}


LINKS = {"act": 2, "dve": 142, "pool": 10}


def kernel(**inputs):
    import concourse.bacc as bacc
    from concourse.bass_utils import run_bass_kernel_spmd

    nc = bacc.Bacc("TRN2", target_bir_lowering=False, num_devices=1)
    arrays = pack({k: np.asarray(v) for k, v in inputs.items()})
    args = [nc.dram_tensor(f"in_{k}", v.shape, F32, kind="ExternalInput").ap() for k, v in arrays.items()]
    out = nc.dram_tensor("out", (NSEQ, SEQ, D), F32, kind="ExternalOutput").ap()
    build(nc, *args, out, LINKS)
    r = run_bass_kernel_spmd(nc, [{f"in_{k}": v for k, v in arrays.items()}], core_ids=[0])
    return r.results[0]["out"]
```
